# Optimizing a Trainium2 kernel written in Bass

```python
import numpy as np
import jax
import jax.numpy as jnp

def _softmax(x, axis=-1):
    return jax.nn.softmax(x, axis=axis)

def _gelu(x):
    return jax.nn.gelu(x, approximate=True)

def _silu(x):
    return jax.nn.silu(x)

def _sigmoid(x):
    return jax.nn.sigmoid(x)

def _layernorm(x, axis=-1, eps=1e-05):
    m = jnp.mean(x, axis=axis, keepdims=True)
    v = jnp.var(x, axis=axis, keepdims=True)
    return (x - m) / jnp.sqrt(v + eps)

def _scatter_add(tgt, idx, src, axis=0):
    return tgt.at[idx].add(src)

def _segment_sum(src, seg, n):
    return jax.ops.segment_sum(src, seg, n)
kernel_name = 'mk_adj_resnorm_d4_adj_r2_b74b78'

def setup_inputs(seed: int=0):
    np.random.seed(seed)
    _w = jnp.asarray

    def _rec_inputs():
        import jax
        import jax.numpy as jnp
        _gk = jax.random.key(seed)
        x = -0.0005207 + 1.001 * jax.random.normal(jax.random.fold_in(_gk, 1), (2048, 256), jnp.float32)
        _a = jax.random.bernoulli(jax.random.fold_in(_gk, 2), 0.000976562, (2048, 2048))
        _a = jnp.logical_or(_a, jnp.swapaxes(_a, -1, -2))
        _a = jnp.logical_or(_a, jnp.eye(2048, dtype=bool))
        adj = _a.astype(jnp.int32)
        return (x, adj)
    x, adj = _rec_inputs()

    def _L0_gnn_setup():
        import jax, jax.numpy as jnp
        import numpy as np
        HEAD_SIZE = 8
        QK_DIM = 256
        V_DIM = 256
        N = 2048
        ATT_DIM = QK_DIM // HEAD_SIZE
        SCALE = ATT_DIM ** (-0.5)
        NEG_FILL = jnp.float32(-9000000000000000.0)
        key = jax.random.key(seed)
        k1, k2, k3, k4 = jax.random.split(key, 4)
        x1 = jax.random.normal(k1, (N, QK_DIM), dtype=jnp.float32)
        x2 = jax.random.normal(k2, (N, QK_DIM), dtype=jnp.float32)
        v = jax.random.normal(k3, (N, V_DIM), dtype=jnp.float32)
        adj = jax.random.randint(k4, (N, N), 0, 2, dtype=jnp.int32)
        return {'x1': x1, 'x2': x2, 'v': v, 'adj': adj}
    _L0_gnn_all = _L0_gnn_setup()
    _L0_gnn_in = {k: v for k, v in _L0_gnn_all.items() if k in ('x2', 'v')}
    del _L0_gnn_all

    def _L1_gnn_setup():
        import jax, jax.numpy as jnp
        import numpy as np
        N, IN_DIM, OUT_DIM = (2048, 256, 256)
        H, D = (8, OUT_DIM // 8)
        ALPHA = 0.2
        NEG = -9000000000000000.0
        EPS = 1e-05
        key = jax.random.key(seed)
        k1, k2, k3, k4 = jax.random.split(key, 4)
        x = jax.random.normal(k1, (N, IN_DIM), dtype=jnp.float32)
        adj = jax.random.randint(k2, (N, N), 0, 2, dtype=jnp.int32)
        W = jax.random.normal(k3, (OUT_DIM, IN_DIM), dtype=jnp.float32) / np.sqrt(IN_DIM)
        a = jax.random.normal(k4, (2 * D,), dtype=jnp.float32) / np.sqrt(2 * D)
        gamma = jnp.ones((OUT_DIM,), dtype=jnp.float32)
        beta = jnp.zeros((OUT_DIM,), dtype=jnp.float32)
        return {'x': x, 'adj': adj, 'W': W, 'a': a, 'gamma': gamma, 'beta': beta}
    _L1_gnn_all = _L1_gnn_setup()
    _L1_gnn_in = {k: v for k, v in _L1_gnn_all.items() if k in ('W', 'a', 'gamma', 'beta')}
    del _L1_gnn_all

    def _L2_gnn_setup():
        import jax, jax.numpy as jnp
        import numpy as np
        key = jax.random.key(seed)
        kX, kA, k1, k2, k3, k4 = jax.random.split(key, 6)
        N, Cin, Cout = (4096, 256, 256)
        X = jax.random.normal(kX, (N, Cin), dtype=jnp.float32)
        A = jax.random.randint(kA, (N, N), 0, 2, dtype=jnp.int32)
        bound = 1.0 / np.sqrt(Cin)
        W_nb = jax.random.uniform(k1, (Cout, Cin), jnp.float32, -bound, bound)
        b_nb = jax.random.uniform(k2, (Cout,), jnp.float32, -bound, bound)
        W_line = jax.random.uniform(k3, (Cout, Cin), jnp.float32, -bound, bound)
        b_line = jax.random.uniform(k4, (Cout,), jnp.float32, -bound, bound)
        return {'X': X, 'A': A, 'W_nb': W_nb, 'b_nb': b_nb, 'W_line': W_line, 'b_line': b_line, 'neibor_num': 64}
    _L2_gnn_all = _L2_gnn_setup()
    _L2_gnn_in = {k: v for k, v in _L2_gnn_all.items() if k in ('W_nb', 'b_nb', 'W_line', 'b_line')}
    del _L2_gnn_all

    def _L3_gnn_setup():
        import jax, jax.numpy as jnp
        import numpy as np
        N, D_IN, D_OUT = (4096, 256, 256)
        key = jax.random.key(seed)
        ks = jax.random.split(key, 8)
        scale_in = 1.0 / np.sqrt(D_IN)
        scale_cat = 1.0 / np.sqrt(2 * D_OUT)
        return {'x': jax.random.normal(ks[0], (N, D_IN), dtype=jnp.float32), 'adj': jax.random.randint(ks[1], (N, N), 0, 2, dtype=jnp.int32), 'W_self': jax.random.uniform(ks[2], (D_IN, D_OUT), jnp.float32, -scale_in, scale_in), 'b_self': jax.random.uniform(ks[3], (D_OUT,), jnp.float32, -scale_in, scale_in), 'W_nb': jax.random.uniform(ks[4], (D_IN, D_OUT), jnp.float32, -scale_in, scale_in), 'b_nb': jax.random.uniform(ks[5], (D_OUT,), jnp.float32, -scale_in, scale_in), 'W_comb': jax.random.uniform(ks[6], (2 * D_OUT, D_OUT), jnp.float32, -scale_cat, scale_cat), 'b_comb': jax.random.uniform(ks[7], (D_OUT,), jnp.float32, -scale_cat, scale_cat)}
    _L3_gnn_all = _L3_gnn_setup()
    _L3_gnn_in = {k: v for k, v in _L3_gnn_all.items() if k in ('W_self', 'b_self', 'W_nb', 'b_nb', 'W_comb', 'b_comb')}
    del _L3_gnn_all
    return {'x': x, 'adj': adj, 'L0_gnn_x2': _L0_gnn_in['x2'], 'L0_gnn_v': _L0_gnn_in['v'], 'L1_gnn_W': _L1_gnn_in['W'], 'L1_gnn_a': _L1_gnn_in['a'], 'L1_gnn_gamma': _L1_gnn_in['gamma'], 'L1_gnn_beta': _L1_gnn_in['beta'], 'L2_gnn_W_nb': _L2_gnn_in['W_nb'], 'L2_gnn_b_nb': _L2_gnn_in['b_nb'], 'L2_gnn_W_line': _L2_gnn_in['W_line'], 'L2_gnn_b_line': _L2_gnn_in['b_line'], 'L3_gnn_W_self': _L3_gnn_in['W_self'], 'L3_gnn_b_self': _L3_gnn_in['b_self'], 'L3_gnn_W_nb': _L3_gnn_in['W_nb'], 'L3_gnn_b_nb': _L3_gnn_in['b_nb'], 'L3_gnn_W_comb': _L3_gnn_in['W_comb'], 'L3_gnn_b_comb': _L3_gnn_in['b_comb']}

def reference(x, adj, L0_gnn_x2, L0_gnn_v, L1_gnn_W, L1_gnn_a, L1_gnn_gamma, L1_gnn_beta, L2_gnn_W_nb, L2_gnn_b_nb, L2_gnn_W_line, L2_gnn_b_line, L3_gnn_W_self, L3_gnn_b_self, L3_gnn_W_nb, L3_gnn_b_nb, L3_gnn_W_comb, L3_gnn_b_comb):
    import jax
    import jax.numpy as jnp

    def _L0_gnn_ref(x1, x2, v, adj):
        import jax, jax.numpy as jnp
        import numpy as np
        HEAD_SIZE = 8
        QK_DIM = 256
        V_DIM = 256
        N = 2048
        ATT_DIM = QK_DIM // HEAD_SIZE
        SCALE = ATT_DIM ** (-0.5)
        NEG_FILL = jnp.float32(-9000000000000000.0)
        n = x1.shape[0]
        q = x1.reshape(n, HEAD_SIZE, -1).transpose(1, 0, 2) * SCALE
        k = x2.reshape(n, HEAD_SIZE, -1).transpose(1, 0, 2)
        vv = v.reshape(n, HEAD_SIZE, -1).transpose(1, 0, 2)
        scores = jnp.einsum('hnd,hmd->hnm', q, k)
        scores = jnp.where(adj > 0, scores, NEG_FILL)
        attn = jax.nn.softmax(scores, axis=-1)
        out = jnp.einsum('hnm,hmd->hnd', attn, vv)
        return out.transpose(1, 0, 2).reshape(n, -1)

    def _L1_gnn_ref(x, adj, W, a, gamma, beta):
        import jax, jax.numpy as jnp
        import numpy as np
        N, IN_DIM, OUT_DIM = (2048, 256, 256)
        H, D = (8, OUT_DIM // 8)
        ALPHA = 0.2
        NEG = -9000000000000000.0
        EPS = 1e-05
        n = x.shape[0]
        Wh = (x @ W.T).reshape(n, H, D)
        a_src, a_dst = (a[:D], a[D:])
        s_src = jnp.einsum('jhd,d->jh', Wh, a_src)
        s_dst = jnp.einsum('ihd,d->ih', Wh, a_dst)
        e = jax.nn.leaky_relu(s_dst[:, None, :] + s_src[None, :, :], negative_slope=ALPHA)
        e = jnp.where((adj > 0)[:, :, None], e, NEG)
        attn = jax.nn.softmax(e, axis=1)
        h_prime = jnp.einsum('ijh,jhd->ihd', attn, Wh).reshape(n, H * D)
        mean = jnp.mean(h_prime, axis=0)
        var = jnp.var(h_prime, axis=0)
        h_prime = gamma * (h_prime - mean) * jax.lax.rsqrt(var + EPS) + beta
        return jax.nn.relu(h_prime)

    def _L2_gnn_ref(X, A, W_nb, b_nb, W_line, b_line, neibor_num):
        import jax, jax.numpy as jnp
        import numpy as np
        Ab = A > 0
        keep = Ab & (jnp.cumsum(Ab.astype(jnp.int32), axis=1) <= neibor_num)
        cnt = keep.sum(axis=1, keepdims=True).astype(X.dtype)
        nb_sum = keep.astype(X.dtype) @ X
        nb_mean = nb_sum / jnp.maximum(cnt, 1.0)
        xj = jax.nn.leaky_relu(nb_mean @ W_nb.T + b_nb)
        xi = jax.nn.leaky_relu(X @ W_line.T + b_line)
        return xi + jnp.where(cnt > 0, xj, jnp.zeros((), X.dtype))

    def _L3_gnn_ref(x, adj, W_self, b_self, W_nb, b_nb, W_comb, b_comb):
        import jax, jax.numpy as jnp
        import numpy as np
        N, D_IN, D_OUT = (4096, 256, 256)
        mask = (adj > 0).astype(x.dtype)
        deg = jnp.sum(mask, axis=1, keepdims=True)
        agg = mask @ x / jnp.maximum(deg, 1.0)
        self_f = x @ W_self + b_self
        nb_f = agg @ W_nb + b_nb
        combined = jnp.concatenate([self_f, nb_f], axis=-1)
        out = combined @ W_comb + b_comb
        return jax.nn.relu(out)
    x = _layernorm(x + _L0_gnn_ref(x, L0_gnn_x2, L0_gnn_v, adj), axis=-1)
    x = _layernorm(x + _L1_gnn_ref(x, adj, L1_gnn_W, L1_gnn_a, L1_gnn_gamma, L1_gnn_beta), axis=-1)
    x = _layernorm(x + _L2_gnn_ref(x, adj, L2_gnn_W_nb, L2_gnn_b_nb, L2_gnn_W_line, L2_gnn_b_line, 64), axis=-1)
    x = _layernorm(x + _L3_gnn_ref(x, adj, L3_gnn_W_self, L3_gnn_b_self, L3_gnn_W_nb, L3_gnn_b_nb, L3_gnn_W_comb, L3_gnn_b_comb), axis=-1)
    return x

_drawn_inputs = setup_inputs


def setup_inputs(seed=0):
    import zlib

    import numpy as np

    out = dict(_drawn_inputs(seed))
    spreads = {'L1_gnn_gamma': (1.0, 0.2), 'L1_gnn_beta': (0.0, 0.1)}
    factors = {'L2_gnn_b_nb': 2.706, 'L3_gnn_b_self': 6.218, 'L3_gnn_b_nb': 5.272, 'L3_gnn_b_comb': 3.172}
    for name, (base, spread) in spreads.items():
        noise = np.random.default_rng([zlib.crc32(name.encode()), seed]).standard_normal(out[name].shape)
        drawn = base * np.exp(spread * noise) if base else spread * noise
        out[name] = jnp.asarray(drawn.astype(out[name].dtype))
    for name, factor in factors.items():
        out[name] = (out[name] * factor).astype(out[name].dtype)
    return out
```

```python
from contextlib import ExitStack

import concourse.bass as bass
from concourse import mybir
from concourse.alu_op_type import AluOpType as ALU

fp32 = mybir.dt.float32
fp32r = mybir.dt.float32r
bf16 = mybir.dt.bfloat16
int32 = mybir.dt.int32
ACT = mybir.ActivationFunctionType
AX = mybir.AxisListType
RMAX = bass.bass_isa.ReduceOp.max

P = 128
N = 2048
D = 256
H = 8
DH = D // H
T = N // P
KT = D // P
CW = 512
NC = N // CW
HG = 4
G = H // HG
GW = HG * DH
SCALE = DH ** -0.5
NEG = -9.0e15
ALPHA = 0.2
SLOPE = 0.01
EPS = 1e-5
KEEP = 64


class Chain:

    def __init__(self, eng, sem, base=0):
        self.eng, self.sem, self.n, self.base = eng, sem, 0, base

    def __call__(self, ins):
        self.n += 1
        ins.then_inc(self.sem, 1)
        self.eng.wait_ge(self.sem, self.base + self.n)


class Space:

    def __init__(self, nc):
        self.nc, self.base, self.scopes, self.n = nc, ExitStack(), [], 0

    def __enter__(self):
        self.scopes.append(ExitStack())
        return self

    def __exit__(self, *a):
        self.scopes.pop().close()
        if not self.scopes:
            self.base.close()

    def sb(self, name, shape, dt):
        self.n += 1
        return self.scopes[-1].enter_context(self.nc.sbuf_tensor(f"{name}_{self.n}", shape, dt))

    def pb(self, name, shape, dt):
        self.n += 1
        return self.scopes[-1].enter_context(self.nc.psum_tensor(f"{name}_{self.n}", shape, dt))

    def sem(self, name):
        self.n += 1
        return self.base.enter_context(self.nc.semaphore(f"{name}_{self.n}"))


def every(ap):
    return ap.rearrange("(o n) -> o n", o=1).broadcast_to([P, ap.shape[0]])


def tiles(ap):
    return ap.rearrange("(t p) n -> p t n", p=P)


def constants(nc, S, ident, ones, mhalf, negI):
    done, made = S.sem("const_chain"), S.sem("ident_made")
    with nc.Block() as block:

        @block.gpsimd
        def _(pool):
            step = Chain(pool, done)
            step(nc.gpsimd.memset(ident[:], 0.0))
            step(nc.gpsimd.memset(ones[:], 1.0))
            step(nc.gpsimd.memset(mhalf[:], -0.5))
            nc.gpsimd.affine_select(out=ident[:], in_=ident[:], pattern=[[-1, P]], compare_op=ALU.not_equal,
                                    fill=1.0, base=0, channel_multiplier=1).then_inc(made, 1)

        @block.vector
        def _(dve):
            dve.wait_ge(made, 1)
            nc.vector.tensor_scalar(negI[:], ident[:], NEG, None, ALU.mult)


def load_edges(nc, S, adjT, edge):
    R = 4
    with S:
        raw = S.sb("adj_raw", [P, R, N], int32)
        landed = [S.sem(f"adj_landed{i}") for i in range(R)]
        used = S.sem("adj_used")
        with nc.Block() as block:

            @block.sync
            def _(sp):
                for t in range(T):
                    if t >= R:
                        sp.wait_ge(used, t - R + 1)
                    sp.dma_start(raw[:, t % R, :], adjT[t * P:(t + 1) * P, :]).then_inc(landed[t % R], 16)

            @block.vector
            def _(dve):
                for t in range(T):
                    dve.wait_ge(landed[t % R], 16 * (t // R + 1))
                    nc.vector.tensor_scalar(edge[:, t, :], raw[:, t % R, :], 0, None, ALU.is_le).then_inc(used, 1)


def shifts(nc, S, x, x2, shift):
    with S:
        xs = S.sb("xs", [P, 2, T, D], fp32)
        sq = S.sb("sq", [P, 2, T * H], fp32)
        mx = S.sb("mx", [P, 2 * H], fp32)
        am = S.sb("am", [P, 2 * H], fp32)
        landed, squared, summed, reduced, largest, chain = (
            S.sem(n) for n in ("xs_landed", "squared", "sq_summed", "mx_reduced", "mx_all", "shift_chain"))
        with nc.Block() as block:

            @block.sync
            def _(sp):
                for i, src in enumerate((x, x2)):
                    sp.dma_start(xs[:, i], tiles(src)).then_inc(landed, 16)

            @block.scalar
            def _(act):
                act.wait_ge(landed, 32)
                for i in range(2):
                    nc.scalar.activation(xs[:, i], xs[:, i], ACT.Square).then_inc(squared, 1)

            @block.vector
            def _(dve):
                for i in range(2):
                    dve.wait_ge(squared, i + 1)
                    nc.vector.tensor_reduce(out=sq[:, i, :], in_=xs[:, i].rearrange("p t (h d) -> p (t h) d", d=DH),
                                            axis=AX.X, op=ALU.add).then_inc(summed, 1)
                    dve.wait_ge(summed, i + 1)
                    nc.vector.tensor_reduce(out=mx[:, i * H:(i + 1) * H],
                                            in_=sq[:, i, :].rearrange("p (t h) -> p h t", h=H),
                                            axis=AX.X, op=ALU.max).then_inc(reduced, 1)
                dve.wait_ge(largest, 1)
                step = Chain(dve, chain)
                step(nc.vector.tensor_tensor(mx[:, 0:H], am[:, 0:H], am[:, H:2 * H], ALU.add))
                nc.vector.tensor_scalar(shift[:], mx[:, 0:H], -SCALE / 2, None, ALU.mult)

            @block.gpsimd
            def _(pool):
                pool.wait_ge(reduced, 2)
                nc.gpsimd.partition_all_reduce(am[:], mx[:], P, RMAX).then_inc(largest, 1)


def load_stacks(nc, S, g, xT, x2T, v, kst, qst, vg):
    R = 4
    with S:
        raw = S.sb("raw", [P, R, N], fp32)
        landed = [S.sem(f"raw_landed{i}") for i in range(R)]
        high, klow, qlow, vland = S.sem("high"), S.sem("k_low"), S.sem("q_low"), S.sem("v_landed")
        order = [(src, dst, h) for h in range(HG) for src, dst in ((x2T, kst), (xT, qst))]
        with nc.Block() as block:

            @block.sync
            def _(sp):
                for n, (src, dst, h) in enumerate(order):
                    if n >= R:
                        sp.wait_ge(klow if n % 2 == 0 else qlow, (n - R) // 2 + 1)
                    rows = src[(g * HG + h) * DH:(g * HG + h + 1) * DH, :]
                    for r in range(P // DH):
                        sp.dma_start(raw[r * DH:(r + 1) * DH, n % R, :], rows).then_inc(landed[n % R], 16)
                sp.dma_start(vg[:], tiles(v)[:, :, g * GW:(g + 1) * GW]).then_inc(vland, 16)
                sp.wait_ge(vland, 16)

            @block.scalar
            def _(act):
                for n, (src, dst, h) in enumerate(order):
                    act.wait_ge(landed[n % R], 16 * (P // DH) * (n // R + 1))
                    nc.scalar.copy(dst[:, h, :], raw[:, n % R, :]).then_inc(high, 1)

            @block.vector
            def _(dve):
                for h in range(HG):
                    dve.wait_ge(high, 2 * h + 1)
                    for r in (1, 3):
                        at = slice(r * DH, (r + 1) * DH)
                        last = nc.vector.tensor_tensor(kst[at, h, :], raw[at, 2 * h % R, :],
                                                       kst[at, h, :].bitcast(fp32), ALU.subtract)
                    last.then_inc(klow, 1)

            @block.gpsimd
            def _(pool):
                for h in range(HG):
                    pool.wait_ge(high, 2 * h + 2)
                    nc.gpsimd.tensor_tensor(qst[64:128, h, :], raw[64:128, (2 * h + 1) % R, :],
                                            qst[64:128, h, :].bitcast(fp32), ALU.subtract).then_inc(qlow, 1)


def attention(nc, S, g, kst, qst, vg, negI, shift, edge, ones, attnT):
    PR = 8
    JP = T // 2
    U = JP * HG
    with S:
        ex = S.sb("ex", [P, PR, 2 * CW], fp32)
        esum = S.sb("esum", [P, HG, 2 * CW], fp32)
        recip = S.sb("recip", [P, CW], fp32)
        scores_ps = S.pb("scores_ps", [P, 2, 2 * CW], fp32)
        mixed_ps = S.pb("mixed_ps", [P, CW], fp32)
        total_ps = S.pb("total_ps", [P, CW], fp32)
        scores_ready, exp_ready, mixed, summed, totals, recip_ready, stored = (
            S.sem(n) for n in ("scores_ready", "exp_ready", "mixed", "summed", "totals", "recip_ready", "stored"))
        EXP0, MIX0, SUM0, TOT0, STO0 = 2, 2, PR, 1, 1
        with nc.Block() as block:

            @block.tensor
            def _(pe):
                pe.sem_inc(mixed, MIX0)
                pe.sem_inc(totals, TOT0)

                def score(ic, jp, h):
                    u = jp * HG + h
                    pe.wait_ge(exp_ready, ic * U + (u - 2 + 1 + EXP0))
                    for t in range(2):
                        jt = 2 * jp + t
                        to = scores_ps[:, u % 2, t * CW:(t + 1) * CW]
                        nc.tensor.matmul(to, kst[:, h, jt * P:(jt + 1) * P], qst[:, h, bass.ds(ic * CW, CW)],
                                         start=True, stop=False)
                        last = nc.tensor.matmul(to, negI[:], edge[:, jt, bass.ds(ic * CW, CW)],
                                                start=False, stop=True)
                    last.then_inc(scores_ready, 1)

                def mix(ic, jp, t):
                    if t == 0:
                        pe.wait_ge(exp_ready, ic * U + (jp * HG + HG + EXP0))
                    if t == 0 and jp == 0:
                        pe.wait_ge(stored, ic + STO0)
                    jt = 2 * jp + t
                    for h in range(HG):
                        u = jp * HG + h
                        last = nc.tensor.matmul(mixed_ps[h * DH:(h + 1) * DH, :], vg[:, jt, h * DH:(h + 1) * DH],
                                                ex[:, u % PR, t * CW:(t + 1) * CW],
                                                start=(jt == 0), stop=(jt == T - 1))
                    if t == 1:
                        last.then_inc(mixed, 1)

                with pe.Fori(0, NC) as ic:
                    for jp in range(JP):
                        score(ic, jp, 0)
                        score(ic, jp, 1)
                        if jp:
                            mix(ic, jp - 1, 0)
                        score(ic, jp, 2)
                        score(ic, jp, 3)
                        if jp:
                            mix(ic, jp - 1, 1)
                    mix(ic, JP - 1, 0)
                    mix(ic, JP - 1, 1)
                    pe.wait_ge(summed, ic * U + (U + SUM0))
                    for t in range(2):
                        for h in range(HG):
                            last = nc.tensor.matmul(total_ps[h * DH:(h + 1) * DH, :], ones[:, 0:DH],
                                                    esum[:, h, t * CW:(t + 1) * CW], start=(t == 0), stop=(t == 1))
                    last.then_inc(totals, 1)

            @block.scalar
            def _(act):
                act.sem_inc(exp_ready, EXP0)
                with act.Fori(0, NC) as ic:
                    for u in range(U):
                        act.wait_ge(scores_ready, ic * U + (u + 1))
                        act.wait_ge(mixed, ic * JP + (u // HG - PR // HG + 1 + MIX0))
                        act.wait_ge(summed, ic * U + (u - PR + 1 + SUM0))
                        nc.scalar.activation(ex[:, u % PR, :], scores_ps[:, u % 2, :], ACT.Exp,
                                             bias=shift[:, g * HG + u % HG:g * HG + u % HG + 1],
                                             scale=SCALE).then_inc(exp_ready, 1)

            @block.vector
            def _(dve):
                dve.sem_inc(summed, SUM0)
                dve.sem_inc(stored, STO0)
                with dve.Fori(0, NC) as ic:
                    for u in range(U):
                        h = u % HG
                        dve.wait_ge(exp_ready, ic * U + (u + 1 + EXP0))
                        if u < HG:
                            dve.wait_ge(totals, ic + TOT0)
                            nc.vector.tensor_copy(esum[:, h, :], ex[:, u % PR, :]).then_inc(summed, 1)
                        else:
                            dve.wait_ge(summed, ic * U + (u - HG + 1 + SUM0))
                            nc.vector.tensor_tensor(esum[:, h, :], esum[:, h, :], ex[:, u % PR, :],
                                                    ALU.add).then_inc(summed, 1)
                    dve.wait_ge(totals, ic + (1 + TOT0))
                    dve.wait_ge(mixed, ic * JP + (JP + MIX0))
                    nc.vector.reciprocal(recip[:], total_ps[:]).then_inc(recip_ready, 1)
                    dve.wait_ge(recip_ready, ic + 1)
                    nc.vector.tensor_tensor(attnT[:, g, bass.ds(ic * CW, CW)], mixed_ps[:], recip[:],
                                            ALU.mult).then_inc(stored, 1)


def layer_norm(nc, S, block, y, mhalf, cur, y_ready, per_tile=1):
    st = S.sb("bn_stats", [P, T, 6], fp32)
    mv = S.sb("mean_var", [P, T, 2], fp32)
    rs = S.sb("rstd", [P, T], fp32)
    stats, aggr, rstd, chain = (S.sem(n) for n in ("ln_stats", "ln_aggr", "ln_rstd", "ln_chain"))

    @block.vector
    def _(dve):
        for t in range(T):
            dve.wait_ge(y_ready, (t + 1) * per_tile)
            nc.vector.bn_stats(st[:, t, :], y[:, t, :]).then_inc(stats, 1)
        for t in range(T):
            dve.wait_ge(stats, t + 1)
            nc.vector.bn_aggr(mv[:, t, :], st[:, t, :]).then_inc(aggr, 1)
        dve.wait_ge(rstd, 1)
        for t in range(T):
            nc.vector.tensor_scalar(cur[:, t, :], y[:, t, :], mv[:, t, 0:1], rs[:, t:t + 1],
                                    ALU.subtract, ALU.mult)

    @block.gpsimd
    def _(pool):
        pool.wait_ge(aggr, T)
        step = Chain(pool, chain)
        step(nc.gpsimd.tensor_scalar(rs[:], mv[:, :, 1], EPS, None, ALU.add))
        nc.gpsimd.tensor_tensor(rs[:], rs[:], mhalf[:], ALU.pow).then_inc(rstd, 1)


def close_layer0(nc, S, x, ident, mhalf, cur):
    attnT = cur[:, :].rearrange("p (g n) -> p g n", g=G)
    with S:
        xs = S.sb("x_nodes", [P, T, D], fp32)
        y = S.sb("y0", [P, T, D], fp32)
        turned = S.pb("turned", [P, 4, CW], fp32)
        landed, transposed, added, freed = (S.sem(n) for n in ("x_landed", "transposed", "y_added", "turned_free"))
        with nc.Block() as block:

            @block.sync
            def _(sp):
                sp.dma_start(xs[:], tiles(x)).then_inc(landed, 16)

            @block.tensor
            def _(pe):
                for t in range(T):
                    if t >= 4:
                        pe.wait_ge(added, t - 3)
                    for g in range(G):
                        last = nc.tensor.transpose(turned[:, t % 4, g * GW:(g + 1) * GW],
                                                   attnT[:, g, t * P:(t + 1) * P], ident[:])
                    last.then_inc(transposed, 1)

            @block.vector
            def _(dve):
                dve.wait_ge(landed, 16)
                for t in range(T):
                    dve.wait_ge(transposed, t + 1)
                    nc.vector.tensor_tensor(y[:, t, :], turned[:, t % 4, 0:D], xs[:, t, :], ALU.add).then_inc(added, 1)

            layer_norm(nc, S, block, y, mhalf, cur[:, :].rearrange("p (t d) -> p t d", d=D), added)


def transpose_nodes(nc, S, ident, cur, xT_sb):
    with S:
        turned = S.pb("turned", [P, 4, CW], fp32)
        transposed, copied = S.sem("transposed"), S.sem("copied")
        with nc.Block() as block:

            @block.tensor
            def _(pe):
                for t in range(T // 2):
                    if t >= 4:
                        pe.wait_ge(copied, t - 3)
                    for k in range(KT):
                        for s in range(2):
                            at = (k * 2 + s) * P
                            last = nc.tensor.transpose(turned[:, t % 4, at:at + P],
                                                       cur[:, 2 * t + s, k * P:(k + 1) * P], ident[:])
                    last.then_inc(transposed, 1)

            def copy(engine, op, parity):
                for t in range(parity, T // 2, 2):
                    engine.wait_ge(transposed, t + 1)
                    if t:
                        engine.wait_ge(copied, t)
                    op(xT_sb[:, :, 2 * t * P:2 * (t + 1) * P],
                       turned[:, t % 4, :].rearrange("p (k n) -> p k n", k=KT)).then_inc(copied, 1)

            @block.scalar
            def _(act):
                copy(act, nc.scalar.copy, 0)

            @block.vector
            def _(dve):
                copy(dve, nc.vector.tensor_copy, 1)


def gat_features(nc, S, W1T, a1, ident, cur, xT_sb, wh1, dst_rows, scores):
    with S:
        w = S.sb("w1", [P, KT, D + 2 * H], fp32)
        ab = S.sb("a_all", [P, 2, DH], fp32)
        wa = S.sb("wa_prod", [P, KT, H, DH], fp32)
        arow = S.sb("arow", [H, N], fp32)
        transpose_nodes(nc, S, ident, cur, xT_sb)
        ps = S.pb("wh_ps", [P, 4, CW], fp32)
        landed, ready, projected, taken, rows, row_kept, written = (
            S.sem(n) for n in ("w_landed", "wa_ready", "projected", "taken", "rows", "row_kept", "rows_written"))
        with nc.Block() as block:

            @block.sync
            def _(sp):
                sp.dma_start(w[:, :, 0:D], W1T.rearrange("(k p) o -> p k o", p=P)).then_inc(landed, 16)
                sp.dma_start(ab[:].rearrange("p s d -> p (s d)"), every(a1)).then_inc(landed, 16)
                sp.wait_ge(row_kept, NC)
                sp.dma_start(dst_rows, arow[:]).then_inc(written, 16)
                sp.wait_ge(written, 16)

            @block.vector
            def _(dve):
                dve.wait_ge(landed, 32)
                n = 0
                for s in range(2):
                    for k in range(KT):
                        if n:
                            dve.wait_ge(ready, 2 * n)
                        nc.vector.tensor_tensor(
                            wa[:, k], w[:, k, 0:D].rearrange("p (h d) -> p h d", d=DH),
                            ab[:, s, :].rearrange("p (o d) -> p o d", o=1).broadcast_to([P, H, DH]),
                            ALU.mult).then_inc(ready, 1)
                        dve.wait_ge(ready, 2 * n + 1)
                        nc.vector.tensor_reduce(out=w[:, k, D + s * H:D + (s + 1) * H], in_=wa[:, k], axis=AX.X,
                                                op=ALU.add).then_inc(ready, 1)
                        n += 1
                nc.vector.memset(wh1[:, :, :, DH:DH + 1], 1.0)
                for t in range(T):
                    dve.wait_ge(projected, t + 1)
                    nc.vector.tensor_copy(scores[:, t, :], ps[:, t % 2, D:D + 2 * H]).then_inc(taken, 1)

            @block.scalar
            def _(act):
                for t in range(T):
                    act.wait_ge(taken, t + 1)
                    nc.scalar.copy(wh1[:, t, :, 0:DH], ps[:, t % 2, 0:D].rearrange("p (h d) -> p h d", d=DH)
                                   ).then_inc(rows, 1)
                for c in range(NC):
                    act.wait_ge(projected, T + c + 1)
                    nc.scalar.copy(arow[:, c * CW:(c + 1) * CW], ps[0:H, 2 + c % 2, :]).then_inc(row_kept, 1)

            @block.tensor
            def _(pe):
                pe.wait_ge(ready, 4 * KT)
                for t in range(T):
                    if t >= 2:
                        pe.wait_ge(rows, t - 1)
                    for k in range(KT):
                        last = nc.tensor.matmul(ps[:, t % 2, 0:D + 2 * H], xT_sb[:, k, t * P:(t + 1) * P], w[:, k, :],
                                                start=(k == 0), stop=(k == KT - 1))
                    last.then_inc(projected, 1)
                for c in range(NC):
                    if c >= 2:
                        pe.wait_ge(row_kept, c - 1)
                    for k in range(KT):
                        last = nc.tensor.matmul(ps[0:H, 2 + c % 2, :], w[:, k, D + H:D + 2 * H],
                                                xT_sb[:, k, c * CW:(c + 1) * CW], start=(k == 0), stop=(k == KT - 1))
                    last.then_inc(projected, 1)


def gat_factors(nc, S, scores, fac, efac, negb, edge):
    b, a = scores[:, :, 0:H], scores[:, :, H:2 * H]
    with S:
        mx = S.sb("mx", [P, H], fp32)
        bm = S.sb("bm", [P, H], fp32)
        top = S.sb("top", [P, T, H], fp32)
        m = S.sb("m", [P, T, H], fp32)
        chain, most, ready = (S.sem(n) for n in ("fac_chain", "b_most", "fac_args"))
        ALL = bm[:].rearrange("p (o h) -> p o h", o=1).broadcast_to([P, T, H])
        with nc.Block() as block:

            @block.vector
            def _(dve):
                step = Chain(dve, chain)
                step(nc.vector.tensor_reduce(out=mx[:], in_=b.rearrange("p t h -> p h t"), axis=AX.X, op=ALU.max))
                dve.wait_ge(most, 1)
                step(nc.vector.tensor_tensor(fac[:, 0], b, ALL, ALU.subtract))
                step(nc.vector.tensor_tensor(top[:], a, ALL, ALU.add))
                step(nc.vector.tensor_scalar(m[:], top[:], ALPHA, None, ALU.mult))
                step(nc.vector.tensor_tensor(m[:], m[:], top[:], ALU.max))
                step(nc.vector.tensor_scalar(fac[:, 1], fac[:, 0], ALPHA, None, ALU.mult))
                step(nc.vector.tensor_tensor(efac[:, 0], top[:], m[:], ALU.subtract))
                step(nc.vector.tensor_scalar(top[:], top[:], ALPHA, None, ALU.mult))
                nc.vector.tensor_tensor(efac[:, 1], top[:], m[:], ALU.subtract).then_inc(ready, 1)
                nc.vector.tensor_scalar(negb[:], b, -1.0, None, ALU.mult)
                for t in range(T):
                    nc.vector.tensor_scalar(edge[:, t, :], edge[:, t, :], -1.0, 1.0, ALU.mult, ALU.add)

            @block.gpsimd
            def _(pool):
                pool.wait_ge(chain, 1)
                nc.gpsimd.partition_all_reduce(bm[:], mx[:], P, RMAX).then_inc(most, 1)

            @block.scalar
            def _(act):
                act.wait_ge(ready, 1)
                nc.scalar.activation(fac[:], fac[:], ACT.Exp)
                nc.scalar.activation(efac[:], efac[:], ACT.Exp)


def gat_attention(nc, S, wh1, dst_rows, fac, efac, negb, edge, hp):
    W = DH + 1
    C = 3 * W
    HALF = N // 2
    BT = HALF // P
    R = 4
    UN = 2 * T
    with S:
        aall = S.sb("a_all", [P, 2, N], fp32)
        pos = S.sb("pos", [P, R, HALF], bf16)
        fx = S.sb("fx", [P, 2, T, 2, 3, W], bf16)
        fm = S.sb("fm", [P, 2, T, 3, W], bf16)
        rest = S.sb("rest", [P, 2, T, W], fp32)
        ev = S.sb("ev", [P, 4, 4 * C], fp32)
        part = S.sb("part", [P, BT, 2, W], fp32)
        whole = S.sb("whole", [P, BT, W], fp32)
        minus1 = S.sb("minus1", [P, BT], fp32)
        acc = S.pb("gat_ps", [P, 8, CW], fp32)
        parts_of = ev[:].rearrange("p b (i k r c) -> p (b i k) r c", k=2, r=3, c=W)
        pos_ready, unit_done, half_done, rest_step, cut, evac, post = (
            S.sem(n) for n in ("pos_ready", "unit_done", "half_done", "rest_step", "cut", "evacuated", "post_step"))
        a_landed = [S.sem(f"a_landed{e}") for e in range(2)]
        RS, PS = 6, 6
        DONE0, HALF0, EV0, POST0, POS0 = R, 3, 2, PS, 1
        with nc.Block() as block:

            def loop(engine, body):
                with engine.Fori(0, H // 2 - 1) as q:
                    for e in range(2):
                        body(q * 2 + e, e, False)
                for e in range(2):
                    body(H - 2 + e, e, e == 1)

            def one(h):
                return slice(h, h + 1) if isinstance(h, int) else bass.ds(h, 1)

            @block.sync
            def _(sp):
                def load(h, e):
                    sp.dma_start(aall[:, e, :], dst_rows[one(h), :].broadcast_to([P, N])).then_inc(a_landed[e], 16)

                def body(h, e, last):
                    if not last:
                        sp.wait_ge(pos_ready, h * UN + POS0)
                        load(h + 1, 1 - e)

                load(0, 0)
                loop(sp, body)

            @block.vector
            def _(dve):
                dve.sem_inc(pos_ready, POS0)

                def body(h, e, last):
                    dve.wait_ge(a_landed[e], h * 8 + (16 - 8 * e))
                    for half in range(2):
                        for jt in range(T):
                            u = half * T + jt
                            dve.wait_ge(unit_done, h * UN + (u - R + 1 + DONE0))
                            at = slice(half * HALF, (half + 1) * HALF)
                            nc.vector.scalar_tensor_tensor(
                                out=pos[:, u % R, :], in0=aall[:, e, at],
                                scalar=negb[:, jt, one(h)], in1=edge[:, jt, at],
                                op0=ALU.is_gt, op1=ALU.mult).then_inc(pos_ready, 1)

                loop(dve, body)

            @block.tensor
            def _(pe):
                pe.sem_inc(unit_done, DONE0)
                pe.sem_inc(half_done, HALF0)

                def body(h, e, last):
                    pe.wait_ge(cut, h * 3 + 3)
                    for half in range(2):
                        pe.wait_ge(evac, h * 2 + (half - 2 + 1 + EV0))
                        for jt in range(T):
                            u = half * T + jt
                            pe.wait_ge(pos_ready, h * UN + (u + 1 + POS0))
                            for i in range(BT):
                                col = (i % 2) * 2 * C
                                done = nc.tensor.matmul(acc[:, half * 4 + i // 2, col:col + 2 * C],
                                                        pos[:, u % R, i * P:(i + 1) * P],
                                                        fx[:, e, jt].rearrange("p k r c -> p (k r c)"),
                                                        start=(jt == 0 and i % 2 == 0), stop=False,
                                                        skip_group_check=True)
                            done.then_inc(unit_done, 1)
                            for i in range(BT):
                                col = (i % 2) * 2 * C + C
                                at = half * HALF + i * P
                                done = nc.tensor.matmul(acc[:, half * 4 + i // 2, col:col + C],
                                                        edge[:, jt, at:at + P],
                                                        fm[:, e, jt].rearrange("p r c -> p (r c)"),
                                                        start=False, stop=(jt == T - 1), skip_group_check=True)
                        done.then_inc(half_done, 1)

                loop(pe, body)

            @block.scalar
            def _(act):
                act.sem_inc(evac, EV0)

                def cut_parts(h, e):
                    act.wait_ge(half_done, h * 2 + (-2 + HALF0))
                    for r in range(3):
                        act.wait_ge(rest_step, h * RS + (2 * r + 2))
                        nc.scalar.copy(fm[:, e, :, r, :], rest[:, 1])
                        nc.scalar.mul(fx[:, e, :, 1, r, :], rest[:, 1], -1.0)
                        nc.scalar.copy(fx[:, e, :, 0, r, :], rest[:, 0]).then_inc(cut, 1)

                def evacuate(h, half):
                    act.wait_ge(half_done, h * 2 + (half + 1 + HALF0))
                    act.wait_ge(post, (h * 2 + half) * PS + (2 - PS + POST0))
                    nc.scalar.copy(ev[:], acc[:, half * 4:half * 4 + 4, 0:4 * C]).then_inc(evac, 1)

                def body(h, e, last):
                    if not last:
                        cut_parts(h + 1, 1 - e)
                    evacuate(h, 0)
                    evacuate(h, 1)

                cut_parts(0, 0)
                loop(act, body)

            @block.gpsimd
            def _(pool):
                pool.sem_inc(post, POST0)
                nc.gpsimd.memset(minus1[:], -1.0)

                def leave(h, e):
                    for k in range(2):
                        if not isinstance(h, int) or h > 0:
                            pool.wait_ge(cut, h * 3)
                        nc.gpsimd.tensor_tensor(rest[:, k], wh1[:, :, one(h), :].rearrange("p t o c -> p t (o c)"),
                                                fac[:, k, :, one(h)].broadcast_to([P, T, W]),
                                                ALU.mult).then_inc(rest_step, 1)
                    for r in range(2):
                        pool.wait_ge(cut, h * 3 + (r + 1))
                        for k in range(2):
                            piece = fx[:, e, :, 0, r, :] if k == 0 else fm[:, e, :, r, :]
                            nc.gpsimd.tensor_tensor(rest[:, k], rest[:, k], piece, ALU.subtract).then_inc(rest_step, 1)

                def finish(h, half):
                    pool.wait_ge(evac, h * 2 + (half + 1 + EV0))
                    step = Chain(pool, post, (h * 2 + half) * PS + POST0)
                    step(nc.gpsimd.tensor_tensor(part[:].rearrange("p i k c -> p (i k) c"), parts_of[:, :, 0, :],
                                                 parts_of[:, :, 1, :], ALU.add))
                    step(nc.gpsimd.tensor_tensor(part[:].rearrange("p i k c -> p (i k) c"), parts_of[:, :, 2, :],
                                                 part[:].rearrange("p i k c -> p (i k) c"), ALU.add))
                    tt = slice(half * BT, (half + 1) * BT)
                    for k in range(2):
                        ins = nc.gpsimd.tensor_tensor(part[:, :, k, :], part[:, :, k, :],
                                                      efac[:, k, tt, one(h)].broadcast_to([P, BT, W]), ALU.mult)
                        if k:
                            step(ins)
                    step(nc.gpsimd.tensor_tensor(whole[:], part[:, :, 0, :], part[:, :, 1, :], ALU.add))
                    step(nc.gpsimd.tensor_tensor(whole[:, :, DH], whole[:, :, DH], minus1[:], ALU.pow))
                    to = hp[:, tt, h * DH:(h + 1) * DH] if isinstance(h, int) else hp[:, tt, bass.ds(h * DH, DH)]
                    step(nc.gpsimd.tensor_tensor(to, whole[:, :, 0:DH],
                                                 whole[:, :, DH:DH + 1].broadcast_to([P, BT, DH]), ALU.mult))

                def body(h, e, last):
                    if not last:
                        leave(h + 1, 1 - e)
                    finish(h, 0)
                    finish(h, 1)

                leave(0, 0)
                loop(pool, body)


def close_layer1(nc, S, gamma, beta, ones, mhalf, hp, cur):
    x1 = cur[:, :].rearrange("p (t d) -> p t d", d=D)
    with S:
        gb = S.sb("gamma_beta", [P, 2, D], fp32)
        mean = S.sb("node_mean", [P, D], fp32)
        sq = S.sb("node_sq", [P, T, D], fp32)
        var = S.sb("node_var", [P, D], fp32)
        half = S.sb("minus_half", [P, D], fp32)
        sums = S.pb("sums_ps", [P, 2, CW], fp32)
        landed, summed, meant, centred, squared, spread, varied, rooted, scaled, shifted, y_ready, pc = (
            S.sem(n) for n in ("gb_landed", "bn_sums", "bn_mean", "bn_centred", "bn_squared", "bn_spread",
                               "bn_var", "bn_root", "bn_scaled", "bn_shifted", "y1_ready", "bn_chain"))
        with nc.Block() as block:

            @block.sync
            def _(sp):
                sp.dma_start(gb[:, 0, :], every(gamma)).then_inc(landed, 16)
                sp.dma_start(gb[:, 1, :], every(beta)).then_inc(landed, 16)

            @block.tensor
            def _(pe):
                for t in range(T):
                    last = nc.tensor.matmul(sums[:, 0, 0:D], ones[:], hp[:, t, :], start=(t == 0), stop=(t == T - 1))
                last.then_inc(summed, 1)
                for t in range(T):
                    pe.wait_ge(squared, t + 1)
                    last = nc.tensor.matmul(sums[:, 1, 0:D], ones[:], sq[:, t, :], start=(t == 0), stop=(t == T - 1))
                last.then_inc(spread, 1)

            @block.scalar
            def _(act):
                act.wait_ge(summed, 1)
                nc.scalar.mul(mean[:], sums[:, 0, 0:D], 1.0 / N).then_inc(meant, 1)
                for t in range(T):
                    act.wait_ge(centred, t + 1)
                    nc.scalar.activation(sq[:, t, :], hp[:, t, :], ACT.Square).then_inc(squared, 1)

            @block.vector
            def _(dve):
                dve.wait_ge(meant, 1)
                for t in range(T):
                    nc.vector.tensor_tensor(hp[:, t, :], hp[:, t, :], mean[:], ALU.subtract).then_inc(centred, 1)
                dve.wait_ge(spread, 1)
                nc.vector.tensor_scalar(var[:], sums[:, 1, 0:D], 1.0 / N, EPS, ALU.mult, ALU.add).then_inc(varied, 1)
                dve.wait_ge(rooted, 1)
                dve.wait_ge(squared, T)
                for t in range(T):
                    nc.vector.tensor_tensor(hp[:, t, :], hp[:, t, :], var[:], ALU.mult).then_inc(scaled, 1)
                for t in range(T):
                    dve.wait_ge(scaled, t + 1)
                    nc.vector.tensor_tensor(hp[:, t, :], hp[:, t, :], gb[:, 1, :], ALU.add).then_inc(shifted, 1)
                for t in range(T):
                    dve.wait_ge(shifted, t + 1)
                    nc.vector.scalar_tensor_tensor(out=hp[:, t, :], in0=hp[:, t, :], scalar=0.0, in1=x1[:, t, :],
                                                   op0=ALU.max, op1=ALU.add).then_inc(y_ready, 1)

            @block.gpsimd
            def _(pool):
                step = Chain(pool, pc)
                step(nc.gpsimd.memset(half[:], -0.5))
                pool.wait_ge(varied, 1)
                pool.wait_ge(landed, 32)
                step(nc.gpsimd.tensor_tensor(var[:], var[:], half[:], ALU.pow))
                nc.gpsimd.tensor_tensor(var[:], var[:], gb[:, 0, :], ALU.mult).then_inc(rooted, 1)

            layer_norm(nc, S, block, hp, mhalf, x1, y_ready)


def keep_first(nc, S, edge, keep):
    with S:
        tri = S.sb("tri", [P, P], bf16)
        col = S.sb("col", [P, T, T], bf16)
        below = S.sb("below", [T, T, P], bf16)
        held = S.sb("held", [T, CW], bf16)
        made, counted, kept_sums, cum, kept = (S.sem(n) for n in ("keep_const", "tile_counts", "tile_counts_kept",
                                                                  "cumulated", "kept"))
        mchain = S.sem("keep_chain")
        count_ps = S.pb("count_ps", [T, CW], fp32)
        cum_ps = S.pb("cum_ps", [P, 4, CW], fp32)
        with nc.Block() as block:

            @block.gpsimd
            def _(pool):
                step = Chain(pool, mchain)
                nc.gpsimd.memset(tri[:], 1.0)
                nc.gpsimd.memset(below[:], 1.0)
                step(nc.gpsimd.memset(col[:], 0.0))
                nc.gpsimd.affine_select(out=tri[:], in_=tri[:], pattern=[[1, P]], compare_op=ALU.is_ge,
                                        fill=0.0, base=0, channel_multiplier=-1)
                nc.gpsimd.affine_select(out=below[:], in_=below[:], pattern=[[1, T], [0, P]], compare_op=ALU.is_gt,
                                        fill=0.0, base=0, channel_multiplier=-1)
                nc.gpsimd.affine_select(out=col[:], in_=col[:], pattern=[[1, T], [-1, T]], compare_op=ALU.not_equal,
                                        fill=1.0, base=0, channel_multiplier=0).then_inc(made, 1)

            @block.tensor
            def _(pe):
                pe.wait_ge(made, 1)
                for c in range(NC):
                    at = slice(c * CW, (c + 1) * CW)
                    if c:
                        pe.wait_ge(kept_sums, c)
                    for t in range(T):
                        last = nc.tensor.matmul(count_ps[:], col[:, t, :], edge[:, t, at], start=(t == 0),
                                                stop=(t == T - 1))
                    last.then_inc(counted, 1)
                    pe.wait_ge(kept_sums, c + 1)
                    for t in range(T):
                        n = c * T + t
                        if n >= 4:
                            pe.wait_ge(kept, n - 3)
                        nc.tensor.matmul(cum_ps[:, n % 4, :], tri[:], edge[:, t, at], start=True, stop=False)
                        nc.tensor.matmul(cum_ps[:, n % 4, :], below[:, t, :], held[:], start=False,
                                         stop=True).then_inc(cum, 1)

            @block.scalar
            def _(act):
                for c in range(NC):
                    act.wait_ge(counted, c + 1)
                    if c:
                        act.wait_ge(cum, c * T)
                    nc.scalar.copy(held[:], count_ps[:]).then_inc(kept_sums, 1)

            @block.vector
            def _(dve):
                for n in range(NC * T):
                    c, t = n // T, n % T
                    dve.wait_ge(cum, n + 1)
                    at = slice(c * CW, (c + 1) * CW)
                    nc.vector.scalar_tensor_tensor(out=keep[:, t, at], in0=cum_ps[:, n % 4, :], scalar=KEEP + 0.5,
                                                   in1=edge[:, t, at], op0=ALU.is_lt, op1=ALU.mult).then_inc(kept, 1)


def mean_layer(nc, S, ident, mhalf, cur, mask, weights, bnb, leaky, out=None):
    xn = cur[:, :].rearrange("p (t d) -> p t d", d=D)
    Y0, Y1, Y2 = 256, 512, 0
    with S:
        xT_sb = S.sb("xT", [P, KT, N], fp32)
        w = S.sb("w_pair", [P, KT, 2 * D], fp32)
        bias = S.sb("bias", [P, 2, D], fp32)
        yb = S.sb("y_parts", [P, T, 3 * D + 2], bf16)
        OT = 2 if leaky else T
        own = S.sb("own", [P, OT, D], fp32)
        rest = S.sb("y_rest", [P, 2, D], fp32)
        weights(w, bias)
        transpose_nodes(nc, S, ident, xn, xT_sb)
        with S:
            ps = S.pb("proj_ps", [P, 4, CW], fp32)
            projected, cut0, left1, cut1, left2, biased, owned, joined = (
                S.sem(n) for n in ("projected", "cut0", "left1", "cut1", "left2", "biased", "owned", "joined"))
            with nc.Block() as block:

                @block.tensor
                def _(pe):
                    for t in range(T):
                        if t >= 4:
                            pe.wait_ge(left1, t - 3)
                            pe.wait_ge(biased, t - 3)
                        for k in range(KT):
                            last = nc.tensor.matmul(ps[:, t % 4, :], xT_sb[:, k, t * P:(t + 1) * P], w[:, k, :],
                                                    start=(k == 0), stop=(k == KT - 1))
                        last.then_inc(projected, 1)

                @block.scalar
                def _(act):
                    for t in range(T):
                        act.wait_ge(projected, t + 1)
                        nc.scalar.copy(yb[:, t, Y0:Y0 + D], ps[:, t % 4, 0:D]).then_inc(cut0, 1)
                        act.wait_ge(left1, t + 1)
                        nc.scalar.copy(yb[:, t, Y1:Y1 + D], rest[:, t % 2, :]).then_inc(cut1, 1)

                @block.vector
                def _(dve):
                    nc.vector.memset(yb[:, :, 3 * D:3 * D + 2], 1.0)
                    for t in range(T):
                        dve.wait_ge(cut0, t + 1)
                        if t >= 2:
                            dve.wait_ge(left2, t - 1)
                        nc.vector.tensor_tensor(rest[:, t % 2, :], ps[:, t % 4, 0:D], yb[:, t, Y0:Y0 + D],
                                                ALU.subtract).then_inc(left1, 1)
                        if leaky and t >= 2:
                            dve.wait_ge(joined, t - 1)
                        nc.vector.tensor_tensor(own[:, t % OT, :], ps[:, t % 4, D:2 * D], bias[:, 1, :],
                                                ALU.add).then_inc(biased, 1)
                        if leaky:
                            dve.wait_ge(biased, t + 1)
                            nc.vector.scalar_tensor_tensor(out=own[:, t % 2, :], in0=own[:, t % 2, :], scalar=SLOPE,
                                                           in1=own[:, t % 2, :], op0=ALU.mult, op1=ALU.max).then_inc(owned, 1)
                @block.gpsimd
                def _(pool):
                    for t in range(T):
                        pool.wait_ge(cut1, t + 1)
                        nc.gpsimd.tensor_tensor(yb[:, t, Y2:Y2 + D], rest[:, t % 2, :], yb[:, t, Y1:Y1 + D],
                                                ALU.subtract).then_inc(left2, 1)
                        if leaky:
                            pool.wait_ge(owned, t + 1)
                            nc.gpsimd.tensor_tensor(xn[:, t, :], own[:, t % 2, :], xn[:, t, :],
                                                    ALU.add).then_inc(joined, 1)
        with S:
            ps = S.pb("nb_ps", [P, 2, CW], fp32)
            cnt = S.sb("cnt", [P, 2, 3], fp32)
            tmp = S.sb("nb_tmp", [P, 2, D], fp32)
            y = xT_sb[:].rearrange("p k (t d) -> p (k t) d", d=D)
            added, chain, y_ready = S.sem("nb_added"), S.sem("nb_chain"), S.sem("y_ready")
            STEPS = 6
            with nc.Block() as block:

                @block.tensor
                def _(pe):
                    pe_free0 = 2
                    with pe.Fori(0, T // 2) as q:
                        for e in range(2):
                            pe.wait_ge(y_ready, q * 2 + (e - 2 + 1 + pe_free0))
                            for jt in range(T):
                                m = mask[:, jt, bass.ds(q * (2 * P) + e * P, P)]
                                nc.tensor.matmul(ps[:, e, 0:D], m, yb[:, jt, Y0:Y0 + D],
                                                 start=(jt == 0), stop=False, skip_group_check=True)
                                nc.tensor.matmul(ps[:, e, 0:D + 1], m, yb[:, jt, Y1:Y1 + D + 1],
                                                 start=False, stop=False, skip_group_check=True)
                                last = nc.tensor.matmul(ps[:, e, 0:D], m, yb[:, jt, Y2:Y2 + D],
                                                        start=False, stop=(jt == T - 1), skip_group_check=True)
                            last.then_inc(added, 1)

                @block.vector
                def _(dve):
                    dve.sem_inc(y_ready, 2)
                    step = Chain(dve, chain)
                    for t in range(T):
                        e = t % 2
                        dve.wait_ge(added, t + 1)
                        c = cnt[:, e, :]
                        step(nc.vector.tensor_scalar(c[:, 0:1], ps[:, e, D:D + 1], 1.0, None, ALU.max))
                        step(nc.vector.reciprocal(c[:, 1:2], c[:, 0:1]))
                        if leaky:
                            step(nc.vector.tensor_scalar(c[:, 2:3], ps[:, e, D:D + 1], 1.0, None, ALU.min))
                            step(nc.vector.scalar_tensor_tensor(out=tmp[:, e, :], in0=ps[:, e, 0:D], scalar=c[:, 1:2],
                                                                in1=bias[:, 0, :], op0=ALU.mult, op1=ALU.add))
                            step(nc.vector.scalar_tensor_tensor(out=tmp[:, e, :], in0=tmp[:, e, :], scalar=SLOPE,
                                                                in1=tmp[:, e, :], op0=ALU.mult, op1=ALU.max))
                            nc.vector.scalar_tensor_tensor(out=y[:, t, :], in0=tmp[:, e, :], scalar=c[:, 2:3],
                                                           in1=xn[:, t, :], op0=ALU.mult,
                                                           op1=ALU.add).then_inc(y_ready, 1)
                        else:
                            step(nc.vector.scalar_tensor_tensor(out=tmp[:, e, :], in0=ps[:, e, 0:D], scalar=c[:, 1:2],
                                                                in1=own[:, t, :], op0=ALU.mult, op1=ALU.add))
                            nc.vector.scalar_tensor_tensor(out=y[:, t, :], in0=tmp[:, e, :], scalar=0.0,
                                                           in1=xn[:, t, :], op0=ALU.max,
                                                           op1=ALU.add).then_inc(y_ready, 1)
        with S:
            start = S.sem("ln_start")
            stored = S.sem("out_stored")
            with nc.Block() as block:

                @block.scalar
                def _(act):
                    act.sem_inc(start, T)

                layer_norm(nc, S, block, y, mhalf, xn, start)
        if out is not None:
            with nc.Block() as block:

                @block.sync
                def _(sp):
                    sp.dma_start(tiles(out), xn).then_inc(stored, 16)
                    sp.wait_ge(stored, 16)


def weights2(nc, S, WnbT, WlineT, bnb, bline):
    def fill(w, bias):
        landed = S.sem("w2_landed")
        with nc.Block() as block:

            @block.sync
            def _(sp):
                for src, to in ((WnbT, w[:, :, 0:D]), (WlineT, w[:, :, D:2 * D])):
                    sp.dma_start(to, src.rearrange("(k p) o -> p k o", p=P)).then_inc(landed, 16)
                for src, i in ((bnb, 0), (bline, 1)):
                    sp.dma_start(bias[:, i, :], every(src)).then_inc(landed, 16)
                sp.wait_ge(landed, 64)
    return fill


def weights3(nc, S, WselfT, bself, WnbT, bnb, Wcomb, bcomb):
    def fill(w, bias):
        with S:
            wt = S.sb("w3_t", [P, 2, KT, D], fp32)
            wc = S.sb("w3_comb", [P, 2 * KT, D], fp32)
            bc = S.sb("b3_cols", [P, 2, KT], fp32)
            bb = S.sb("b3_all", [P, 2, KT, P], fp32)
            ps = S.pb("w3_ps", [P, 3, CW], fp32)
            landed, spread, made = S.sem("w3_landed"), S.sem("b3_spread"), S.sem("w3_made")
            with nc.Block() as block:

                @block.sync
                def _(sp):
                    sp.dma_start(wt[:, 0], WnbT.rearrange("(k p) o -> p k o", p=P)).then_inc(landed, 16)
                    sp.dma_start(wt[:, 1], WselfT.rearrange("(k p) o -> p k o", p=P)).then_inc(landed, 16)
                    sp.dma_start(wc[:], Wcomb.rearrange("(k p) o -> p k o", p=P)).then_inc(landed, 16)
                    sp.dma_start(bc[:, 0, :], bnb).then_inc(landed, 16)
                    sp.dma_start(bc[:, 1, :], bself).then_inc(landed, 16)
                    sp.dma_start(bias[:, 0, :], every(bcomb)).then_inc(landed, 16)

                @block.tensor
                def _(pe):
                    pe.wait_ge(landed, 96)
                    pe.wait_ge(spread, 1)
                    for k in range(KT):
                        for s in range(2):
                            for m in range(KT):
                                nc.tensor.matmul(ps[:, k, s * D:(s + 1) * D], wt[:, s, m, k * P:(k + 1) * P],
                                                 wc[:, (1 - s) * KT + m, :], start=(m == 0), stop=(m == KT - 1),
                                                 skip_group_check=True)
                    for s in range(2):
                        for m in range(KT):
                            last = nc.tensor.matmul(ps[:, 2, 0:D], bb[:, s, m, :], wc[:, (1 - s) * KT + m, :],
                                                    start=(s == 0 and m == 0), stop=(s == 1 and m == KT - 1))
                    last.then_inc(made, 1)

                @block.vector
                def _(dve):
                    dve.wait_ge(landed, 96)
                    nc.vector.tensor_copy(bb[:].rearrange("p s k n -> p (s k) n"),
                                          bc[:].rearrange("p s k -> p (s k)").unsqueeze(2).broadcast_to([P, 2 * KT, P])
                                          ).then_inc(spread, 1)
                    dve.wait_ge(made, 1)
                    nc.vector.tensor_copy(w[:], ps[:, 0:KT, :])
                    nc.vector.tensor_tensor(bias[:, 1, :], ps[:, 2, 0:D], bias[:, 0, :], ALU.add)
    return fill


def program(nc, x, x2, v, xT, x2T, adjT, W1T, a1, gamma, beta, Wnb2T, bnb2, Wline2T, bline2,
            Wself3T, bself3, Wnb3T, bnb3, Wcomb3, bcomb3, dst_rows, out):
    S = Space(nc)
    with S:
        ident = S.sb("ident", [P, P], fp32)
        ones = S.sb("ones", [P, P], fp32)
        mhalf = S.sb("mhalf", [P, T], fp32)
        negI = S.sb("negI", [P, P], bf16)
        shift = S.sb("shift", [P, H], fp32)
        cur = S.sb("cur", [P, T * D], fp32)
        edge = S.sb("edge", [P, T, N], bf16)
        nodes = cur[:, :].rearrange("p (t d) -> p t d", d=D)

        constants(nc, S, ident, ones, mhalf, negI)
        load_edges(nc, S, adjT, edge)

        shifts(nc, S, x, x2, shift)
        attnT = cur[:, :].rearrange("p (g n) -> p g n", g=G)
        for g in range(G):
            with S:
                kst = S.sb("kst", [P, HG, N], fp32r)
                qst = S.sb("qst", [P, HG, N], fp32r)
                vg = S.sb("vg", [P, T, GW], fp32)
                load_stacks(nc, S, g, xT, x2T, v, kst, qst, vg)
                attention(nc, S, g, kst, qst, vg, negI, shift, edge, ones, attnT)
        close_layer0(nc, S, x, ident, mhalf, cur)

        with S:
            hp = S.sb("hp", [P, T, D], fp32)
            gat_layer(nc, S, W1T, a1, ident, nodes, dst_rows, edge, hp)
            close_layer1(nc, S, gamma, beta, ones, mhalf, hp, cur)

        with S:
            keep = S.sb("keep", [P, T, N], bf16)
            keep_first(nc, S, edge, keep)
            mean_layer(nc, S, ident, mhalf, cur, keep, weights2(nc, S, Wnb2T, Wline2T, bnb2, bline2), None, True)

        mean_layer(nc, S, ident, mhalf, cur, edge,
                   weights3(nc, S, Wself3T, bself3, Wnb3T, bnb3, Wcomb3, bcomb3), None, False, out)


def gat_layer(nc, S, W1T, a1, ident, nodes, dst_rows, edge, hp):
    with S:
        wh1 = S.sb("wh1", [P, T, H, DH + 1], fp32)
        scores = S.sb("s_src_dst", [P, T, 2 * H], fp32)
        fac = S.sb("fac", [P, 2, T, H], fp32)
        efac = S.sb("efac", [P, 2, T, H], fp32)
        negb = S.sb("negb", [P, T, H], fp32)
        with S:
            xT_sb = S.sb("x1T", [P, KT, N], fp32)
            gat_features(nc, S, W1T, a1, ident, nodes, xT_sb, wh1, dst_rows, scores)
        gat_factors(nc, S, scores, fac, efac, negb, edge)
        gat_attention(nc, S, wh1, dst_rows, fac, efac, negb, edge, hp)


def kernel(x, adj, L0_gnn_x2, L0_gnn_v, L1_gnn_W, L1_gnn_a, L1_gnn_gamma, L1_gnn_beta, L2_gnn_W_nb, L2_gnn_b_nb,
           L2_gnn_W_line, L2_gnn_b_line, L3_gnn_W_self, L3_gnn_b_self, L3_gnn_W_nb, L3_gnn_b_nb, L3_gnn_W_comb,
           L3_gnn_b_comb):
    import numpy as np
    import concourse.bacc as bacc
    from concourse.bass_utils import run_bass_kernel_spmd

    def turned(a):
        return np.ascontiguousarray(np.asarray(a).T)

    def columns(a):
        return turned(np.asarray(a).reshape(KT, P))

    arrays = {
        "x": x, "x2": L0_gnn_x2, "v": L0_gnn_v, "xT": turned(x), "x2T": turned(L0_gnn_x2), "adjT": turned(adj),
        "W1T": turned(L1_gnn_W), "a1": L1_gnn_a, "gamma": L1_gnn_gamma, "beta": L1_gnn_beta,
        "Wnb2T": turned(L2_gnn_W_nb), "bnb2": L2_gnn_b_nb, "Wline2T": turned(L2_gnn_W_line), "bline2": L2_gnn_b_line,
        "Wself3T": turned(L3_gnn_W_self), "bself3": columns(L3_gnn_b_self), "Wnb3T": turned(L3_gnn_W_nb), "bnb3": columns(L3_gnn_b_nb),
        "Wcomb3": L3_gnn_W_comb, "bcomb3": L3_gnn_b_comb,
    }
    arrays = {f"in_{k}_dram": np.ascontiguousarray(a) for k, a in arrays.items()}
    nc = bacc.Bacc("TRN2", target_bir_lowering=False, num_devices=1)
    args = [nc.dram_tensor(k, a.shape, mybir.dt.from_np(a.dtype), kind="ExternalInput").ap() for k, a in arrays.items()]
    out = nc.dram_tensor("out_dram", (N, D), fp32, kind="ExternalOutput").ap()
    dst_rows = nc.dram_tensor("dst_rows_dram", (H, N), fp32, kind="Internal").ap()
    program(nc, *args, dst_rows, out)
    r = run_bass_kernel_spmd(nc, [arrays], core_ids=[0])
    return r.results[0]["out_dram"]
```

```python
from contextlib import ExitStack

import concourse.bass as bass
from concourse import mybir
from concourse.alu_op_type import AluOpType as ALU

fp32 = mybir.dt.float32
fp32r = mybir.dt.float32r
bf16 = mybir.dt.bfloat16
int32 = mybir.dt.int32
ACT = mybir.ActivationFunctionType
AX = mybir.AxisListType
RMAX = bass.bass_isa.ReduceOp.max

P = 128
N = 2048
D = 256
H = 8
DH = D // H
T = N // P
KT = D // P
CW = 512
NC = N // CW
HG = 4
G = H // HG
GW = HG * DH
SCALE = DH ** -0.5
NEG = -9.0e15
ALPHA = 0.2
SLOPE = 0.01
EPS = 1e-5
BIG = 1e30
KEEP = 64


class Chain:

    def __init__(self, eng, sem, base=0):
        self.eng, self.sem, self.n, self.base = eng, sem, 0, base

    def __call__(self, ins):
        self.n += 1
        ins.then_inc(self.sem, 1)
        self.eng.wait_ge(self.sem, self.base + self.n)


class Space:

    def __init__(self, nc):
        self.nc, self.base, self.scopes, self.n = nc, ExitStack(), [], 0

    def __enter__(self):
        self.scopes.append(ExitStack())
        return self

    def __exit__(self, *a):
        self.scopes.pop().close()
        if not self.scopes:
            self.base.close()

    def sb(self, name, shape, dt):
        self.n += 1
        return self.scopes[-1].enter_context(self.nc.sbuf_tensor(f"{name}_{self.n}", shape, dt))

    def pb(self, name, shape, dt):
        self.n += 1
        return self.scopes[-1].enter_context(self.nc.psum_tensor(f"{name}_{self.n}", shape, dt))

    def sem(self, name):
        self.n += 1
        return self.base.enter_context(self.nc.semaphore(f"{name}_{self.n}"))


def every(ap):
    return ap.rearrange("(o n) -> o n", o=1).broadcast_to([P, ap.shape[0]])


def tiles(ap):
    return ap.rearrange("(t p) n -> p t n", p=P)


def constants(nc, S, ident, ones, mhalf, negI):
    done, made = S.sem("const_chain"), S.sem("ident_made")
    with nc.Block() as block:

        @block.gpsimd
        def _(pool):
            step = Chain(pool, done)
            step(nc.gpsimd.memset(ident[:], 0.0))
            step(nc.gpsimd.memset(ones[:], 1.0))
            step(nc.gpsimd.memset(mhalf[:], -0.5))
            nc.gpsimd.affine_select(out=ident[:], in_=ident[:], pattern=[[-1, P]], compare_op=ALU.not_equal,
                                    fill=1.0, base=0, channel_multiplier=1).then_inc(made, 1)

        @block.vector
        def _(dve):
            dve.wait_ge(made, 1)
            nc.vector.tensor_scalar(negI[:], ident[:], NEG, None, ALU.mult)


def load_edges(nc, S, adjT, edge):
    R = 4
    with S:
        raw = S.sb("adj_raw", [P, R, N], int32)
        landed = [S.sem(f"adj_landed{i}") for i in range(R)]
        used = S.sem("adj_used")
        with nc.Block() as block:

            @block.sync
            def _(sp):
                for t in range(T):
                    if t >= R:
                        sp.wait_ge(used, t - R + 1)
                    sp.dma_start(raw[:, t % R, :], adjT[t * P:(t + 1) * P, :]).then_inc(landed[t % R], 16)

            @block.vector
            def _(dve):
                for t in range(T):
                    dve.wait_ge(landed[t % R], 16 * (t // R + 1))
                    nc.vector.tensor_scalar(edge[:, t, :], raw[:, t % R, :], 0, None, ALU.is_le).then_inc(used, 1)


def shifts(nc, S, x, x2, shift):
    with S:
        xs = S.sb("xs", [P, 2, T, D], fp32)
        sq = S.sb("sq", [P, 2, T * H], fp32)
        mx = S.sb("mx", [P, 2 * H], fp32)
        am = S.sb("am", [P, 2 * H], fp32)
        landed, squared, summed, reduced, largest, chain = (
            S.sem(n) for n in ("xs_landed", "squared", "sq_summed", "mx_reduced", "mx_all", "shift_chain"))
        with nc.Block() as block:

            @block.sync
            def _(sp):
                for i, src in enumerate((x, x2)):
                    sp.dma_start(xs[:, i], tiles(src)).then_inc(landed, 16)

            @block.scalar
            def _(act):
                act.wait_ge(landed, 32)
                for i in range(2):
                    nc.scalar.activation(xs[:, i], xs[:, i], ACT.Square).then_inc(squared, 1)

            @block.vector
            def _(dve):
                for i in range(2):
                    dve.wait_ge(squared, i + 1)
                    nc.vector.tensor_reduce(out=sq[:, i, :], in_=xs[:, i].rearrange("p t (h d) -> p (t h) d", d=DH),
                                            axis=AX.X, op=ALU.add).then_inc(summed, 1)
                    dve.wait_ge(summed, i + 1)
                    nc.vector.tensor_reduce(out=mx[:, i * H:(i + 1) * H],
                                            in_=sq[:, i, :].rearrange("p (t h) -> p h t", h=H),
                                            axis=AX.X, op=ALU.max).then_inc(reduced, 1)
                dve.wait_ge(largest, 1)
                step = Chain(dve, chain)
                step(nc.vector.tensor_tensor(mx[:, 0:H], am[:, 0:H], am[:, H:2 * H], ALU.add))
                nc.vector.tensor_scalar(shift[:], mx[:, 0:H], -SCALE / 2, None, ALU.mult)

            @block.gpsimd
            def _(pool):
                pool.wait_ge(reduced, 2)
                nc.gpsimd.partition_all_reduce(am[:], mx[:], P, RMAX).then_inc(largest, 1)


def load_stacks(nc, S, g, xT, x2T, v, kst, qst, vg):
    R = 4
    with S:
        raw = S.sb("raw", [P, R, N], fp32)
        landed = [S.sem(f"raw_landed{i}") for i in range(R)]
        high, klow, qlow, vland = S.sem("high"), S.sem("k_low"), S.sem("q_low"), S.sem("v_landed")
        order = [(src, dst, h) for h in range(HG) for src, dst in ((x2T, kst), (xT, qst))]
        with nc.Block() as block:

            @block.sync
            def _(sp):
                for n, (src, dst, h) in enumerate(order):
                    if n >= R:
                        sp.wait_ge(klow if n % 2 == 0 else qlow, (n - R) // 2 + 1)
                    rows = src[(g * HG + h) * DH:(g * HG + h + 1) * DH, :]
                    for r in range(P // DH):
                        sp.dma_start(raw[r * DH:(r + 1) * DH, n % R, :], rows).then_inc(landed[n % R], 16)
                sp.dma_start(vg[:], tiles(v)[:, :, g * GW:(g + 1) * GW]).then_inc(vland, 16)
                sp.wait_ge(vland, 16)

            @block.scalar
            def _(act):
                for n, (src, dst, h) in enumerate(order):
                    act.wait_ge(landed[n % R], 16 * (P // DH) * (n // R + 1))
                    nc.scalar.copy(dst[:, h, :], raw[:, n % R, :]).then_inc(high, 1)

            @block.vector
            def _(dve):
                for h in range(HG):
                    dve.wait_ge(high, 2 * h + 1)
                    for r in (1, 3):
                        at = slice(r * DH, (r + 1) * DH)
                        last = nc.vector.tensor_tensor(kst[at, h, :], raw[at, 2 * h % R, :],
                                                       kst[at, h, :].bitcast(fp32), ALU.subtract)
                    last.then_inc(klow, 1)

            @block.gpsimd
            def _(pool):
                for h in range(HG):
                    pool.wait_ge(high, 2 * h + 2)
                    nc.gpsimd.tensor_tensor(qst[64:128, h, :], raw[64:128, (2 * h + 1) % R, :],
                                            qst[64:128, h, :].bitcast(fp32), ALU.subtract).then_inc(qlow, 1)


def attention(nc, S, g, kst, qst, vg, negI, shift, edge, ones, attnT):
    PR = 8
    JP = T // 2
    U = JP * HG
    with S:
        ex = S.sb("ex", [P, PR, 2 * CW], fp32)
        esum = S.sb("esum", [P, HG, 2 * CW], fp32)
        recip = S.sb("recip", [P, CW], fp32)
        scores_ps = S.pb("scores_ps", [P, 2, 2 * CW], fp32)
        mixed_ps = S.pb("mixed_ps", [P, CW], fp32)
        total_ps = S.pb("total_ps", [P, CW], fp32)
        scores_ready, exp_ready, mixed, summed, totals, recip_ready, stored = (
            S.sem(n) for n in ("scores_ready", "exp_ready", "mixed", "summed", "totals", "recip_ready", "stored"))
        EXP0, MIX0, SUM0, TOT0, STO0 = 2, 2, PR, 1, 1
        with nc.Block() as block:

            @block.tensor
            def _(pe):
                pe.sem_inc(mixed, MIX0)
                pe.sem_inc(totals, TOT0)

                def score(ic, jp, h):
                    u = jp * HG + h
                    pe.wait_ge(exp_ready, ic * U + (u - 2 + 1 + EXP0))
                    for t in range(2):
                        jt = 2 * jp + t
                        to = scores_ps[:, u % 2, t * CW:(t + 1) * CW]
                        nc.tensor.matmul(to, kst[:, h, jt * P:(jt + 1) * P], qst[:, h, bass.ds(ic * CW, CW)],
                                         start=True, stop=False)
                        last = nc.tensor.matmul(to, negI[:], edge[:, jt, bass.ds(ic * CW, CW)],
                                                start=False, stop=True)
                    last.then_inc(scores_ready, 1)

                def mix(ic, jp, t):
                    if t == 0:
                        pe.wait_ge(exp_ready, ic * U + (jp * HG + HG + EXP0))
                    if t == 0 and jp == 0:
                        pe.wait_ge(stored, ic + STO0)
                    jt = 2 * jp + t
                    for h in range(HG):
                        u = jp * HG + h
                        last = nc.tensor.matmul(mixed_ps[h * DH:(h + 1) * DH, :], vg[:, jt, h * DH:(h + 1) * DH],
                                                ex[:, u % PR, t * CW:(t + 1) * CW],
                                                start=(jt == 0), stop=(jt == T - 1))
                    if t == 1:
                        last.then_inc(mixed, 1)

                with pe.Fori(0, NC) as ic:
                    for jp in range(JP):
                        score(ic, jp, 0)
                        score(ic, jp, 1)
                        if jp:
                            mix(ic, jp - 1, 0)
                        score(ic, jp, 2)
                        score(ic, jp, 3)
                        if jp:
                            mix(ic, jp - 1, 1)
                    mix(ic, JP - 1, 0)
                    mix(ic, JP - 1, 1)
                    pe.wait_ge(summed, ic * U + (U + SUM0))
                    for t in range(2):
                        for h in range(HG):
                            last = nc.tensor.matmul(total_ps[h * DH:(h + 1) * DH, :], ones[:, 0:DH],
                                                    esum[:, h, t * CW:(t + 1) * CW], start=(t == 0), stop=(t == 1))
                    last.then_inc(totals, 1)

            @block.scalar
            def _(act):
                act.sem_inc(exp_ready, EXP0)
                with act.Fori(0, NC) as ic:
                    for u in range(U):
                        act.wait_ge(scores_ready, ic * U + (u + 1))
                        act.wait_ge(mixed, ic * JP + (u // HG - PR // HG + 1 + MIX0))
                        act.wait_ge(summed, ic * U + (u - PR + 1 + SUM0))
                        nc.scalar.activation(ex[:, u % PR, :], scores_ps[:, u % 2, :], ACT.Exp,
                                             bias=shift[:, g * HG + u % HG:g * HG + u % HG + 1],
                                             scale=SCALE).then_inc(exp_ready, 1)

            @block.vector
            def _(dve):
                dve.sem_inc(summed, SUM0)
                dve.sem_inc(stored, STO0)
                with dve.Fori(0, NC) as ic:
                    for u in range(U):
                        h = u % HG
                        dve.wait_ge(exp_ready, ic * U + (u + 1 + EXP0))
                        if u < HG:
                            dve.wait_ge(totals, ic + TOT0)
                            nc.vector.tensor_copy(esum[:, h, :], ex[:, u % PR, :]).then_inc(summed, 1)
                        else:
                            dve.wait_ge(summed, ic * U + (u - HG + 1 + SUM0))
                            nc.vector.tensor_tensor(esum[:, h, :], esum[:, h, :], ex[:, u % PR, :],
                                                    ALU.add).then_inc(summed, 1)
                    dve.wait_ge(totals, ic + (1 + TOT0))
                    dve.wait_ge(mixed, ic * JP + (JP + MIX0))
                    nc.vector.reciprocal(recip[:], total_ps[:]).then_inc(recip_ready, 1)
                    dve.wait_ge(recip_ready, ic + 1)
                    nc.vector.tensor_tensor(attnT[:, g, bass.ds(ic * CW, CW)], mixed_ps[:], recip[:],
                                            ALU.mult).then_inc(stored, 1)


def enter_layer1(nc, S, x, W1T, a1, ident, mhalf, cur, edge, wh1, dst_rows, scores):
    attnT = cur[:, :].rearrange("p (g n) -> p g n", g=G)
    TG = 4
    GS = T // TG
    SW = 2 * H
    with S:
        xs = S.sb("x_nodes", [P, T, D], fp32)
        x1 = S.sb("x1", [P, T, D], fp32)
        xT_sb = S.sb("x1T", [P, KT, N], fp32)
        st = S.sb("bn_stats", [P, T, 6], fp32)
        mv = S.sb("mean_var", [P, T, 2], fp32)
        rs = S.sb("rstd", [P, T], fp32)
        w = S.sb("w1", [P, KT, D + SW], fp32)
        ab = S.sb("a_all", [P, 2, DH], fp32)
        wa = S.sb("wa_prod", [P, 2, KT, H, DH], fp32)
        arow = S.sb("arow", [H, N], fp32)
        attn_ps = S.pb("attn_ps", [P, 2, 2, D], fp32)
        x1t_ps = S.pb("x1T_ps", [P, 2, KT, 2 * P], fp32)
        wh_ps = S.pb("wh_ps", [P, 2, CW], fp32)
        row_ps = S.pb("row_ps", [P, 2, CW], fp32)
        names = ("x_landed", "w_landed", "wa_prod_ready", "wa_ready", "attn_turned", "added", "stats", "aggr",
                 "var_eps", "rstd", "normed", "x1_turned", "x1T_kept", "projected", "scores_kept", "wh_kept", "rows",
                 "rows_kept", "rows_written", "x1_kept")
        (x_landed, w_landed, wa_prod, wa_ready, attn_turned, added, stats, aggr, var_eps, rstd, normed, x1_turned,
         x1T_kept, projected, scores_kept, wh_kept, rows, rows_kept, written, x1_kept) = (S.sem(n) for n in names)
        with nc.Block() as block:

            @block.sync
            def _(sp):
                sp.dma_start(xs[:], tiles(x)).then_inc(x_landed, 16)
                sp.dma_start(w[:, :, 0:D], W1T.rearrange("(k p) o -> p k o", p=P)).then_inc(w_landed, 16)
                sp.dma_start(ab[:].rearrange("p s d -> p (s d)"), every(a1)).then_inc(w_landed, 16)
                sp.wait_ge(rows_kept, NC)
                sp.dma_start(dst_rows, arow[:]).then_inc(written, 16)
                sp.wait_ge(attn_turned, GS)
                sp.wait_ge(normed, T)
                sp.dma_start(cur[:, :], x1[:].rearrange("p t d -> p (t d)")).then_inc(x1_kept, 16)
                sp.wait_ge(written, 16)
                sp.wait_ge(x1_kept, 16)

            @block.tensor
            def _(pe):
                def attention_by_nodes(g):
                    if g:
                        pe.wait_ge(added, TG * g)
                    for t in range(TG * g, TG * (g + 1)):
                        for f in range(G):
                            last = nc.tensor.transpose(attn_ps[:, t % TG // 2, t % 2, f * GW:(f + 1) * GW],
                                                       attnT[:, f, t * P:(t + 1) * P], ident[:])
                    last.then_inc(attn_turned, 1)

                def features(g):
                    pe.wait_ge(normed, TG * (g + 1))
                    for t in range(TG * g, TG * (g + 1), 2):
                        if t >= 4:
                            pe.wait_ge(x1T_kept, t // 2 - 1)
                        for k in range(KT):
                            for s in range(2):
                                last = nc.tensor.transpose(x1t_ps[:, t // 2 % 2, k, s * P:(s + 1) * P],
                                                           x1[:, t + s, k * P:(k + 1) * P], ident[:])
                        last.then_inc(x1_turned, 1)
                    if g == 0:
                        pe.wait_ge(wa_ready, 2 * KT)
                    for t in range(TG * g, TG * (g + 1)):
                        pe.wait_ge(x1T_kept, t // 2 + 1)
                        if t >= 2:
                            pe.wait_ge(wh_kept, t - 1)
                        for k in range(KT):
                            last = nc.tensor.matmul(wh_ps[:, t % 2, 0:D + SW], xT_sb[:, k, t * P:(t + 1) * P],
                                                    w[:, k, :], start=(k == 0), stop=(k == KT - 1))
                        last.then_inc(projected, 1)
                    if g >= 2:
                        pe.wait_ge(rows_kept, g - 1)
                    for k in range(KT):
                        last = nc.tensor.matmul(row_ps[0:H, g % 2, :], w[:, k, D + H:D + SW],
                                                xT_sb[:, k, g * CW:(g + 1) * CW], start=(k == 0), stop=(k == KT - 1))
                    last.then_inc(rows, 1)

                attention_by_nodes(0)
                for g in range(GS):
                    if g + 1 < GS:
                        attention_by_nodes(g + 1)
                    features(g)

            @block.vector
            def _(dve):
                dve.wait_ge(w_landed, 32)
                for s in range(2):
                    for k in range(KT):
                        nc.vector.tensor_tensor(
                            wa[:, s, k], w[:, k, 0:D].rearrange("p (h d) -> p h d", d=DH),
                            ab[:, s, :].rearrange("p (o d) -> p o d", o=1).broadcast_to([P, H, DH]),
                            ALU.mult).then_inc(wa_prod, 1)
                for s in range(2):
                    for k in range(KT):
                        dve.wait_ge(wa_prod, s * KT + k + 1)
                        nc.vector.tensor_reduce(out=w[:, k, D + s * H:D + (s + 1) * H], in_=wa[:, s, k], axis=AX.X,
                                                op=ALU.add).then_inc(wa_ready, 1)
                nc.vector.memset(wh1[:, :, :, DH:DH + 1], 1.0)
                dve.wait_ge(x_landed, 16)

                def keep_scores(g):
                    for t in range(TG * g, TG * (g + 1)):
                        dve.wait_ge(projected, t + 1)
                        nc.vector.tensor_copy(scores[:, t, :], wh_ps[:, t % 2, D:D + SW]).then_inc(scores_kept, 1)

                for g in range(GS):
                    group = range(TG * g, TG * (g + 1))
                    dve.wait_ge(attn_turned, g + 1)
                    for t in group:
                        nc.vector.tensor_tensor(xs[:, t, :], attn_ps[:, t % TG // 2, t % 2, :], xs[:, t, :],
                                                ALU.add).then_inc(added, 1)
                    for t in group:
                        dve.wait_ge(added, t + 1)
                        nc.vector.bn_stats(st[:, t, :], xs[:, t, :]).then_inc(stats, 1)
                    for t in group:
                        dve.wait_ge(stats, t + 1)
                        nc.vector.bn_aggr(mv[:, t, :], st[:, t, :]).then_inc(aggr, 1)
                    if g:
                        keep_scores(g - 1)
                    for t in group:
                        nc.vector.tensor_scalar(edge[:, t, :], edge[:, t, :], 0.0, None, ALU.is_equal)
                    dve.wait_ge(rstd, g + 1)
                    for t in group:
                        nc.vector.tensor_scalar(x1[:, t, :], xs[:, t, :], mv[:, t, 0:1], rs[:, t:t + 1],
                                                ALU.subtract, ALU.mult).then_inc(normed, 1)
                keep_scores(GS - 1)

            @block.gpsimd
            def _(pool):
                for g in range(GS):
                    at = slice(TG * g, TG * (g + 1))
                    pool.wait_ge(aggr, TG * (g + 1))
                    nc.gpsimd.tensor_scalar(rs[:, at], mv[:, at, 1], EPS, None, ALU.add).then_inc(var_eps, 1)
                    pool.wait_ge(var_eps, g + 1)
                    nc.gpsimd.tensor_tensor(rs[:, at], rs[:, at], mhalf[:, at], ALU.pow).then_inc(rstd, 1)

            @block.scalar
            def _(act):
                for g in range(GS):
                    for t in range(TG * g, TG * (g + 1), 2):
                        act.wait_ge(x1_turned, t // 2 + 1)
                        nc.scalar.copy(xT_sb[:, :, t * P:(t + 2) * P], x1t_ps[:, t // 2 % 2]).then_inc(x1T_kept, 1)
                    for t in range(TG * g, TG * (g + 1)):
                        act.wait_ge(scores_kept, t + 1)
                        nc.scalar.copy(wh1[:, t, :, 0:DH], wh_ps[:, t % 2, 0:D].rearrange("p (h d) -> p h d", d=DH)
                                       ).then_inc(wh_kept, 1)
                    act.wait_ge(rows, g + 1)
                    nc.scalar.copy(arow[:, g * CW:(g + 1) * CW], row_ps[0:H, g % 2, :]).then_inc(rows_kept, 1)


def gat_factors(nc, S, scores, fac, efac, negb, bigb):
    b, a = scores[:, :, 0:H], scores[:, :, H:2 * H]
    with S:
        mx = S.sb("mx", [P, H], fp32)
        bm = S.sb("bm", [P, H], fp32)
        top = S.sb("top", [P, T, H], fp32)
        m = S.sb("m", [P, T, H], fp32)
        chain, most, ready = (S.sem(n) for n in ("fac_chain", "b_most", "fac_args"))
        ALL = bm[:].rearrange("p (o h) -> p o h", o=1).broadcast_to([P, T, H])
        with nc.Block() as block:

            @block.vector
            def _(dve):
                step = Chain(dve, chain)
                step(nc.vector.tensor_reduce(out=mx[:], in_=b.rearrange("p t h -> p h t"), axis=AX.X, op=ALU.max))
                dve.wait_ge(most, 1)
                step(nc.vector.tensor_tensor(fac[:, 0], b, ALL, ALU.subtract))
                step(nc.vector.tensor_tensor(top[:], a, ALL, ALU.add))
                step(nc.vector.tensor_scalar(m[:], top[:], ALPHA, None, ALU.mult))
                step(nc.vector.tensor_tensor(m[:], m[:], top[:], ALU.max))
                step(nc.vector.tensor_scalar(fac[:, 1], fac[:, 0], ALPHA, None, ALU.mult))
                step(nc.vector.tensor_tensor(efac[:, 0], top[:], m[:], ALU.subtract))
                step(nc.vector.tensor_scalar(top[:], top[:], ALPHA, None, ALU.mult))
                nc.vector.tensor_tensor(efac[:, 1], top[:], m[:], ALU.subtract).then_inc(ready, 1)
                nc.vector.tensor_scalar(negb[:], b, -1.0, None, ALU.mult)
                nc.vector.tensor_scalar(bigb[:], b, BIG, None, ALU.mult)
            @block.gpsimd
            def _(pool):
                pool.wait_ge(chain, 1)
                nc.gpsimd.partition_all_reduce(bm[:], mx[:], P, RMAX).then_inc(most, 1)

            @block.scalar
            def _(act):
                act.wait_ge(ready, 1)
                nc.scalar.activation(fac[:], fac[:], ACT.Exp)
                nc.scalar.activation(efac[:], efac[:], ACT.Exp)


def gat_attention(nc, S, wh1, dst_rows, fac, efac, negb, bigb, edge, hp):
    W = DH + 1
    C = 3 * W
    HALF = N // 2
    BT = HALF // P
    R = 4
    UN = 2 * T
    HR = T // 2
    RS_ = 4
    with S:
        aall = S.sb("a_all", [P, 2, N], fp32)
        pos = S.sb("pos", [P, R, HALF], bf16)
        steps = S.sb("steps", [P, RS_, HALF], bf16)
        bigh = S.sb("big_b_head", [P, 2, T], fp32)
        fx = S.sb("fx", [P, 2, T, 2, 3, W], bf16)
        fm = S.sb("fm", [P, 2, T, 3, W], bf16)
        rest = S.sb("rest", [P, 2, T, W], fp32)
        ev = S.sb("ev", [P, 4, 4 * C], fp32)
        part = S.sb("part", [P, BT, 2, W], fp32)
        whole = S.sb("whole", [P, BT, W], fp32)
        minus1 = S.sb("minus1", [P, BT], fp32)
        acc = S.pb("gat_ps", [P, 8, CW], fp32)
        parts_of = ev[:].rearrange("p b (i k r c) -> p (b i k) r c", k=2, r=3, c=W)
        pos_ready, unit_done, half_done, rest_step, cut, evac, post = (
            S.sem(n) for n in ("pos_ready", "unit_done", "half_done", "rest_step", "cut", "evacuated", "post_step"))
        a_landed = [S.sem(f"a_landed{e}") for e in range(2)]
        step_ready, bigh_ready = S.sem("step_ready"), S.sem("big_b_head_ready")
        RS, PS = 6, 6
        DONE0, HALF0, EV0, POST0, POS0 = R, 3, 2, PS, 2 * RS_
        with nc.Block() as block:

            def loop(engine, body):
                with engine.Fori(0, H // 2 - 1) as q:
                    for e in range(2):
                        body(q * 2 + e, e, False)
                for e in range(2):
                    body(H - 2 + e, e, e == 1)

            def one(h):
                return slice(h, h + 1) if isinstance(h, int) else bass.ds(h, 1)

            @block.sync
            def _(sp):
                def load(h, e):
                    sp.dma_start(aall[:, e, :], dst_rows[one(h), :].broadcast_to([P, N])).then_inc(a_landed[e], 16)

                def body(h, e, last):
                    if not last:
                        sp.wait_ge(pos_ready, h * UN + POS0)
                        sp.wait_ge(step_ready, h * (2 * HR) + 1)
                        load(h + 1, 1 - e)

                load(0, 0)
                loop(sp, body)

            @block.vector
            def _(dve):
                dve.sem_inc(pos_ready, POS0)

                def big_head(h, e):
                    nc.vector.tensor_scalar(bigh[:, e, :], bigb[:, :, one(h)].rearrange("p t o -> p (t o)"), 1.0,
                                            None, ALU.mult).then_inc(bigh_ready, 1)

                big_head(0, 0)

                def body(h, e, last):
                    dve.wait_ge(a_landed[e], h * 8 + (16 - 8 * e))
                    for half in range(2):
                        if half and not last:
                            big_head(h + 1, 1 - e)
                        for jt in range(T):
                            u = half * T + jt
                            dve.wait_ge(unit_done, h * UN + (u - R + 1 + DONE0))
                            at = slice(half * HALF, (half + 1) * HALF)
                            if jt % 2:
                                n = half * HR + jt // 2
                                dve.wait_ge(step_ready, h * (2 * HR) + (n + 1))
                                nc.vector.tensor_tensor(pos[:, u % R, :], steps[:, n % RS_, :], edge[:, jt, at],
                                                        ALU.min).then_inc(pos_ready, 1)
                                continue
                            nc.vector.scalar_tensor_tensor(
                                out=pos[:, u % R, :], in0=aall[:, e, at],
                                scalar=negb[:, jt, one(h)], in1=edge[:, jt, at],
                                op0=ALU.is_gt, op1=ALU.mult).then_inc(pos_ready, 1)

                loop(dve, body)

            @block.tensor
            def _(pe):
                pe.sem_inc(unit_done, DONE0)
                pe.sem_inc(half_done, HALF0)

                def body(h, e, last):
                    pe.wait_ge(cut, h * 3 + 3)
                    for half in range(2):
                        pe.wait_ge(evac, h * 2 + (half - 2 + 1 + EV0))
                        for jt in range(T):
                            u = half * T + jt
                            pe.wait_ge(pos_ready, h * UN + (u + 1 + POS0))
                            for i in range(BT):
                                col = (i % 2) * 2 * C
                                done = nc.tensor.matmul(acc[:, half * 4 + i // 2, col:col + 2 * C],
                                                        pos[:, u % R, i * P:(i + 1) * P],
                                                        fx[:, e, jt].rearrange("p k r c -> p (k r c)"),
                                                        start=(jt == 0 and i % 2 == 0), stop=False,
                                                        skip_group_check=True)
                            done.then_inc(unit_done, 1)
                            for i in range(BT):
                                col = (i % 2) * 2 * C + C
                                at = half * HALF + i * P
                                done = nc.tensor.matmul(acc[:, half * 4 + i // 2, col:col + C],
                                                        edge[:, jt, at:at + P],
                                                        fm[:, e, jt].rearrange("p r c -> p (r c)"),
                                                        start=False, stop=(jt == T - 1), skip_group_check=True)
                        done.then_inc(half_done, 1)

                loop(pe, body)

            @block.scalar
            def _(act):
                act.sem_inc(evac, EV0)

                def cut_parts(h, e):
                    act.wait_ge(half_done, h * 2 + (-2 + HALF0))
                    for r in range(3):
                        act.wait_ge(rest_step, h * RS + (2 * r + 2))
                        nc.scalar.copy(fm[:, e, :, r, :], rest[:, 1])
                        nc.scalar.mul(fx[:, e, :, 1, r, :], rest[:, 1], -1.0)
                        nc.scalar.copy(fx[:, e, :, 0, r, :], rest[:, 0]).then_inc(cut, 1)

                def evacuate(h, half):
                    act.wait_ge(half_done, h * 2 + (half + 1 + HALF0))
                    act.wait_ge(post, (h * 2 + half) * PS + (2 - PS + POST0))
                    nc.scalar.copy(ev[:], acc[:, half * 4:half * 4 + 4, 0:4 * C]).then_inc(evac, 1)

                def compare(h, e, half, first, count):
                    for n in range(half * HR + first, half * HR + first + count):
                        if n % (2 * HR) == 0:
                            act.wait_ge(a_landed[e], h * 8 + (16 - 8 * e))
                            act.wait_ge(bigh_ready, h + 1)
                        before = n - RS_
                        unit = before // HR * T + 2 * (before % HR) + 1
                        act.wait_ge(pos_ready, h * UN + (unit + 1 + POS0))
                        nc.scalar.activation(steps[:, n % RS_, :], aall[:, e, half * HALF:(half + 1) * HALF], ACT.Relu,
                                             bias=bigh[:, e, 2 * (n % HR) + 1:2 * (n % HR) + 2], scale=BIG).then_inc(step_ready, 1)

                def body(h, e, last):
                    compare(h, e, 0, RS_, HR - RS_)
                    compare(h, e, 1, 0, RS_)
                    if not last:
                        cut_parts(h + 1, 1 - e)
                    evacuate(h, 0)
                    compare(h, e, 1, RS_, HR - RS_)
                    if not last:
                        compare(h + 1, 1 - e, 0, 0, RS_)
                    evacuate(h, 1)

                cut_parts(0, 0)
                compare(0, 0, 0, 0, RS_)
                loop(act, body)

            @block.gpsimd
            def _(pool):
                pool.sem_inc(post, POST0)
                nc.gpsimd.memset(minus1[:], -1.0)

                def leave(h, e):
                    for k in range(2):
                        if not isinstance(h, int) or h > 0:
                            pool.wait_ge(cut, h * 3)
                        nc.gpsimd.tensor_tensor(rest[:, k], wh1[:, :, one(h), :].rearrange("p t o c -> p t (o c)"),
                                                fac[:, k, :, one(h)].broadcast_to([P, T, W]),
                                                ALU.mult).then_inc(rest_step, 1)
                    for r in range(2):
                        pool.wait_ge(cut, h * 3 + (r + 1))
                        for k in range(2):
                            piece = fx[:, e, :, 0, r, :] if k == 0 else fm[:, e, :, r, :]
                            nc.gpsimd.tensor_tensor(rest[:, k], rest[:, k], piece, ALU.subtract).then_inc(rest_step, 1)

                def finish(h, half):
                    pool.wait_ge(evac, h * 2 + (half + 1 + EV0))
                    step = Chain(pool, post, (h * 2 + half) * PS + POST0)
                    step(nc.gpsimd.tensor_tensor(part[:].rearrange("p i k c -> p (i k) c"), parts_of[:, :, 0, :],
                                                 parts_of[:, :, 1, :], ALU.add))
                    step(nc.gpsimd.tensor_tensor(part[:].rearrange("p i k c -> p (i k) c"), parts_of[:, :, 2, :],
                                                 part[:].rearrange("p i k c -> p (i k) c"), ALU.add))
                    tt = slice(half * BT, (half + 1) * BT)
                    for k in range(2):
                        ins = nc.gpsimd.tensor_tensor(part[:, :, k, :], part[:, :, k, :],
                                                      efac[:, k, tt, one(h)].broadcast_to([P, BT, W]), ALU.mult)
                        if k:
                            step(ins)
                    step(nc.gpsimd.tensor_tensor(whole[:], part[:, :, 0, :], part[:, :, 1, :], ALU.add))
                    step(nc.gpsimd.tensor_tensor(whole[:, :, DH], whole[:, :, DH], minus1[:], ALU.pow))
                    to = hp[:, tt, h * DH:(h + 1) * DH] if isinstance(h, int) else hp[:, tt, bass.ds(h * DH, DH)]
                    step(nc.gpsimd.tensor_tensor(to, whole[:, :, 0:DH],
                                                 whole[:, :, DH:DH + 1].broadcast_to([P, BT, DH]), ALU.mult))

                def body(h, e, last):
                    if not last:
                        leave(h + 1, 1 - e)
                    finish(h, 0)
                    finish(h, 1)

                leave(0, 0)
                loop(pool, body)


def close_layer1(nc, S, gamma, beta, ones, mhalf, hp, cur, edge, keep):
    x1 = cur[:, :].rearrange("p (t d) -> p t d", d=D)
    KR = 4
    NU = NC * T
    PT = NU // T
    with S:
        gb = S.sb("gamma_beta", [P, 2, D], fp32)
        mean = S.sb("node_mean", [P, D], fp32)
        sq = S.sb("node_sq", [P, 4, D], fp32)
        var = S.sb("node_var", [P, D], fp32)
        half = S.sb("minus_half", [P, D], fp32)
        st = S.sb("bn_stats", [P, T, 6], fp32)
        mv = S.sb("mean_var", [P, T, 2], fp32)
        rs = S.sb("rstd", [P, T], fp32)
        tri = S.sb("tri", [P, P], bf16)
        col = S.sb("col", [P, T, T], bf16)
        below = S.sb("below", [T, T, P], bf16)
        held = S.sb("held", [T, NC, CW], bf16)
        upto = S.sb("upto", [P, KR, CW], bf16)
        limit = S.sb("limit", [P, 1], fp32)
        sums = S.pb("sums_ps", [P, 2, CW], fp32)
        count_ps = S.pb("count_ps", [P, 2, CW], fp32)
        cum_ps = S.pb("cum_ps", [P, KR, CW], fp32)
        names = ("gb_landed", "consts", "const_chain", "bn_sums", "bn_mean", "bn_centred", "bn_squared", "bn_spread",
                 "bn_var", "bn_chain", "bn_root", "bn_scaled", "bn_shifted", "y1_ready", "ln_stats", "ln_aggr",
                 "ln_eps", "ln_rstd", "tile_counts", "counts_held", "cumulated", "upto_ready", "kept")
        (landed, consts, cc, summed, meant, centred, squared, spread, varied, pc, rooted, scaled, shifted, y_ready,
         stats, aggr, eps_done, rstd, counted, heldc, cum, upto_ready, kept) = (S.sem(n) for n in names)
        with nc.Block() as block:

            @block.sync
            def _(sp):
                sp.dma_start(gb[:, 0, :], every(gamma)).then_inc(landed, 16)
                sp.dma_start(gb[:, 1, :], every(beta)).then_inc(landed, 16)

            @block.tensor
            def _(pe):
                for t in range(T):
                    last = nc.tensor.matmul(sums[:, 0, 0:D], ones[:], hp[:, t, :], start=(t == 0), stop=(t == T - 1))
                last.then_inc(summed, 1)
                pe.wait_ge(consts, 1)
                for c in range(NC):
                    if c >= 2:
                        pe.wait_ge(heldc, c - 1)
                    for t in range(T):
                        last = nc.tensor.matmul(count_ps[0:T, c % 2, :], col[:, t, :],
                                                edge[:, t, c * CW:(c + 1) * CW], start=(t == 0), stop=(t == T - 1))
                    last.then_inc(counted, 1)
                for t in range(T):
                    pe.wait_ge(squared, t + 1)
                    nc.tensor.matmul(sums[:, 1, 0:D], ones[:], sq[:, t % 4, :], start=(t == 0),
                                     stop=(t == T - 1)).then_inc(spread, 1)
                for n in range(NU):
                    c, t = n // T, n % T
                    if t == 0:
                        pe.wait_ge(heldc, c + 1)
                    if n >= KR:
                        pe.wait_ge(upto_ready, n - KR + 1)
                    nc.tensor.matmul(cum_ps[:, n % KR, :], tri[:], edge[:, t, c * CW:(c + 1) * CW],
                                     start=True, stop=False)
                    nc.tensor.matmul(cum_ps[:, n % KR, :], below[:, t, :], held[:, c, :], start=False,
                                     stop=True).then_inc(cum, 1)

            @block.scalar
            def _(act):
                def square(t):
                    act.wait_ge(centred, t + 1)
                    if t >= 4:
                        act.wait_ge(spread, t - 3)
                    nc.scalar.activation(sq[:, t % 4, :], hp[:, t, :], ACT.Square).then_inc(squared, 1)

                def hold(c):
                    act.wait_ge(counted, c + 1)
                    nc.scalar.copy(held[:, c, :], count_ps[0:T, c % 2, :]).then_inc(heldc, 1)

                act.wait_ge(summed, 1)
                nc.scalar.mul(mean[:], sums[:, 0, 0:D], 1.0 / N).then_inc(meant, 1)
                for t in range(4):
                    square(t)
                for c in range(NC):
                    hold(c)
                for t in range(4, T):
                    square(t)
                act.wait_ge(consts, 1)
                for n in range(NU):
                    act.wait_ge(cum, n + 1)
                    if n >= KR:
                        act.wait_ge(kept, n - KR + 1)
                    nc.scalar.activation(upto[:, n % KR, :], cum_ps[:, n % KR, :], ACT.Relu, bias=limit[:],
                                         scale=-2.0).then_inc(upto_ready, 1)

            @block.vector
            def _(dve):
                def keep_units(first, count):
                    for n in range(first, first + count):
                        at = slice(n // T * CW, (n // T + 1) * CW)
                        dve.wait_ge(upto_ready, n + 1)
                        nc.vector.tensor_tensor(keep[:, n % T, at], upto[:, n % KR, :], edge[:, n % T, at],
                                                ALU.min).then_inc(kept, 1)

                dve.wait_ge(meant, 1)
                for t in range(T):
                    nc.vector.tensor_tensor(hp[:, t, :], hp[:, t, :], mean[:], ALU.subtract).then_inc(centred, 1)
                dve.wait_ge(spread, T)
                nc.vector.tensor_scalar(var[:], sums[:, 1, 0:D], 1.0 / N, EPS, ALU.mult, ALU.add).then_inc(varied, 1)
                dve.wait_ge(rooted, 1)
                dve.wait_ge(squared, T)
                for t in range(T + 1):
                    if t < T:
                        nc.vector.tensor_tensor(hp[:, t, :], hp[:, t, :], var[:], ALU.mult).then_inc(scaled, 1)
                        keep_units(PT * t, PT)
                    if t:
                        dve.wait_ge(shifted, t)
                        nc.vector.scalar_tensor_tensor(out=hp[:, t - 1, :], in0=hp[:, t - 1, :], scalar=0.0,
                                                       in1=x1[:, t - 1, :], op0=ALU.max,
                                                       op1=ALU.add).then_inc(y_ready, 1)
                        dve.wait_ge(y_ready, t)
                        nc.vector.bn_stats(st[:, t - 1, :], hp[:, t - 1, :]).then_inc(stats, 1)
                for t in range(T):
                    dve.wait_ge(stats, t + 1)
                    nc.vector.bn_aggr(mv[:, t, :], st[:, t, :]).then_inc(aggr, 1)
                dve.wait_ge(rstd, 1)
                for t in range(T):
                    nc.vector.tensor_scalar(x1[:, t, :], hp[:, t, :], mv[:, t, 0:1], rs[:, t:t + 1],
                                            ALU.subtract, ALU.mult)

            @block.gpsimd
            def _(pool):
                step = Chain(pool, cc)
                nc.gpsimd.memset(limit[:], 2.0 * KEEP + 1)
                nc.gpsimd.memset(half[:], -0.5)
                nc.gpsimd.memset(tri[:], 1.0)
                nc.gpsimd.memset(below[:], 1.0)
                step(nc.gpsimd.memset(col[:], 0.0))
                nc.gpsimd.affine_select(out=tri[:], in_=tri[:], pattern=[[1, P]], compare_op=ALU.is_ge,
                                        fill=0.0, base=0, channel_multiplier=-1)
                nc.gpsimd.affine_select(out=below[:], in_=below[:], pattern=[[1, T], [0, P]], compare_op=ALU.is_gt,
                                        fill=0.0, base=0, channel_multiplier=-1)
                nc.gpsimd.affine_select(out=col[:], in_=col[:], pattern=[[1, T], [-1, T]], compare_op=ALU.not_equal,
                                        fill=1.0, base=0, channel_multiplier=0).then_inc(consts, 1)
                pool.wait_ge(varied, 1)
                pool.wait_ge(landed, 32)
                step = Chain(pool, pc)
                step(nc.gpsimd.tensor_tensor(var[:], var[:], half[:], ALU.pow))
                nc.gpsimd.tensor_tensor(var[:], var[:], gb[:, 0, :], ALU.mult).then_inc(rooted, 1)
                for t in range(T):
                    pool.wait_ge(scaled, t + 1)
                    nc.gpsimd.tensor_tensor(hp[:, t, :], hp[:, t, :], gb[:, 1, :], ALU.add).then_inc(shifted, 1)
                pool.wait_ge(aggr, T)
                nc.gpsimd.tensor_scalar(rs[:], mv[:, :, 1], EPS, None, ALU.add).then_inc(eps_done, 1)
                pool.wait_ge(eps_done, 1)
                nc.gpsimd.tensor_tensor(rs[:], rs[:], mhalf[:], ALU.pow).then_inc(rstd, 1)


def mean_layer(nc, S, ident, mhalf, cur, mask, xT_sb, w, bias, leaky, out=None):
    xn = cur[:, :].rearrange("p (t d) -> p t d", d=D)
    Y2, Y0, Y1 = 0, D, 2 * D
    OT = 2 if leaky else T
    with S:
        yb = S.sb("y_parts", [P, T, 3 * D + 2], bf16)
        own = S.sb("own", [P, OT, D], fp32)
        with S:
            rest = S.sb("y_rest", [P, 2, D], fp32)
            turned = S.pb("turned", [P, 2, CW], fp32)
            ps = S.pb("proj_ps", [P, 4, CW], fp32)
            turned_ready, xT_kept, projected, cut0, left1, cut1, left2, biased, owned, joined = (
                S.sem(n) for n in ("turned_ready", "xT_kept", "projected", "cut0", "left1", "cut1", "left2", "biased",
                                   "owned", "joined"))
            with nc.Block() as block:

                @block.tensor
                def _(pe):
                    for t in range(T + 1):
                        if t < T:
                            if t >= 2:
                                pe.wait_ge(xT_kept, t - 1)
                            for k in range(KT):
                                last = nc.tensor.transpose(turned[:, t % 2, k * P:(k + 1) * P],
                                                           xn[:, t, k * P:(k + 1) * P], ident[:])
                            last.then_inc(turned_ready, 1)
                        if t:
                            s = t - 1
                            pe.wait_ge(xT_kept, s + 1)
                            if s >= 4:
                                pe.wait_ge(left1, s - 3)
                                pe.wait_ge(biased, s - 3)
                            for k in range(KT):
                                last = nc.tensor.matmul(ps[:, s % 4, :], xT_sb[:, k, s * P:(s + 1) * P], w[:, k, :],
                                                        start=(k == 0), stop=(k == KT - 1))
                            last.then_inc(projected, 1)

                @block.scalar
                def _(act):
                    for t in range(T + 1):
                        if t < T:
                            act.wait_ge(turned_ready, t + 1)
                            nc.scalar.copy(xT_sb[:, :, t * P:(t + 1) * P],
                                           turned[:, t % 2, 0:D].rearrange("p (k n) -> p k n", k=KT)).then_inc(xT_kept, 1)
                        if t:
                            s = t - 1
                            act.wait_ge(projected, s + 1)
                            nc.scalar.copy(yb[:, s, Y0:Y0 + D], ps[:, s % 4, 0:D]).then_inc(cut0, 1)
                            act.wait_ge(left1, s + 1)
                            nc.scalar.copy(yb[:, s, Y1:Y1 + D], rest[:, s % 2, :]).then_inc(cut1, 1)

                @block.vector
                def _(dve):
                    nc.vector.memset(yb[:, :, 3 * D:3 * D + 2], 1.0)
                    for t in range(T):
                        dve.wait_ge(cut0, t + 1)
                        if t >= 2:
                            dve.wait_ge(left2, t - 1)
                        nc.vector.tensor_tensor(rest[:, t % 2, :], ps[:, t % 4, 0:D], yb[:, t, Y0:Y0 + D],
                                                ALU.subtract).then_inc(left1, 1)
                        if leaky and t >= 2:
                            dve.wait_ge(joined, t - 1)
                        nc.vector.tensor_tensor(own[:, t % OT, :], ps[:, t % 4, D:2 * D], bias[:, 1, :],
                                                ALU.add).then_inc(biased, 1)
                        if leaky:
                            dve.wait_ge(biased, t + 1)
                            nc.vector.scalar_tensor_tensor(out=own[:, t % 2, :], in0=own[:, t % 2, :], scalar=SLOPE,
                                                           in1=own[:, t % 2, :], op0=ALU.mult,
                                                           op1=ALU.max).then_inc(owned, 1)

                @block.gpsimd
                def _(pool):
                    for t in range(T):
                        pool.wait_ge(cut1, t + 1)
                        nc.gpsimd.tensor_tensor(yb[:, t, Y2:Y2 + D], rest[:, t % 2, :], yb[:, t, Y1:Y1 + D],
                                                ALU.subtract).then_inc(left2, 1)
                        if leaky:
                            pool.wait_ge(owned, t + 1)
                            nc.gpsimd.tensor_tensor(xn[:, t, :], own[:, t % 2, :], xn[:, t, :],
                                                    ALU.add).then_inc(joined, 1)
        with S:
            ps = S.pb("nb_ps", [P, 2, CW], fp32)
            cnt = S.sb("cnt", [P, 2, 3], fp32)
            tmp = S.sb("nb_tmp", [P, 2, D], fp32)
            st = S.sb("bn_stats", [P, T, 6], fp32)
            mv = S.sb("mean_var", [P, T, 2], fp32)
            rs = S.sb("rstd", [P, T], fp32)
            y = xT_sb[:].rearrange("p k (t d) -> p (k t) d", d=D)
            added, chain, y_ready, stats, aggr, eps_done, rstd, normed, stored = (
                S.sem(n) for n in ("nb_added", "nb_chain", "y_ready", "ln_stats", "ln_aggr", "ln_eps", "ln_rstd",
                                   "normed", "out_stored"))
            FREE0 = 2
            TD = 4
            with nc.Block() as block:

                @block.tensor
                def _(pe):
                    with pe.Fori(0, T // 2) as q:
                        for e in range(2):
                            pe.wait_ge(y_ready, q * 2 + (e - 2 + 1 + FREE0))
                            for jt in range(T):
                                m = mask[:, jt, bass.ds(q * (2 * P) + e * P, P)]
                                nc.tensor.matmul(ps[:, e, 0:D], m, yb[:, jt, Y0:Y0 + D],
                                                 start=(jt == 0), stop=False, skip_group_check=True)
                                nc.tensor.matmul(ps[:, e, 0:D + 1], m, yb[:, jt, Y1:Y1 + D + 1],
                                                 start=False, stop=False, skip_group_check=True)
                                last = nc.tensor.matmul(ps[:, e, 0:D], m, yb[:, jt, Y2:Y2 + D],
                                                        start=False, stop=(jt == T - 1), skip_group_check=True)
                            last.then_inc(added, 1)

                @block.vector
                def _(dve):
                    dve.sem_inc(y_ready, FREE0)
                    step = Chain(dve, chain)

                    def normalise(t):
                        dve.wait_ge(rstd, t + 1)
                        nc.vector.tensor_scalar(xn[:, t, :], y[:, t, :], mv[:, t, 0:1], rs[:, t:t + 1],
                                                ALU.subtract, ALU.mult).then_inc(normed, 1)

                    for t in range(T):
                        e = t % 2
                        dve.wait_ge(added, t + 1)
                        c = cnt[:, e, :]
                        step(nc.vector.tensor_scalar(c[:, 0:1], ps[:, e, D:D + 1], 1.0, None, ALU.max))
                        step(nc.vector.reciprocal(c[:, 1:2], c[:, 0:1]))
                        if leaky:
                            step(nc.vector.tensor_scalar(c[:, 2:3], ps[:, e, D:D + 1], 1.0, None, ALU.min))
                            step(nc.vector.scalar_tensor_tensor(out=tmp[:, e, :], in0=ps[:, e, 0:D], scalar=c[:, 1:2],
                                                                in1=bias[:, 0, :], op0=ALU.mult, op1=ALU.add))
                            step(nc.vector.scalar_tensor_tensor(out=tmp[:, e, :], in0=tmp[:, e, :], scalar=SLOPE,
                                                                in1=tmp[:, e, :], op0=ALU.mult, op1=ALU.max))
                            nc.vector.scalar_tensor_tensor(out=y[:, t, :], in0=tmp[:, e, :], scalar=c[:, 2:3],
                                                           in1=xn[:, t, :], op0=ALU.mult,
                                                           op1=ALU.add).then_inc(y_ready, 1)
                        else:
                            step(nc.vector.scalar_tensor_tensor(out=tmp[:, e, :], in0=ps[:, e, 0:D], scalar=c[:, 1:2],
                                                                in1=own[:, t, :], op0=ALU.mult, op1=ALU.add))
                            nc.vector.scalar_tensor_tensor(out=y[:, t, :], in0=tmp[:, e, :], scalar=0.0,
                                                           in1=xn[:, t, :], op0=ALU.max,
                                                           op1=ALU.add).then_inc(y_ready, 1)
                        dve.wait_ge(y_ready, t + 1 + FREE0)
                        nc.vector.bn_stats(st[:, t, :], y[:, t, :]).then_inc(stats, 1)
                        dve.wait_ge(stats, t + 1)
                        nc.vector.bn_aggr(mv[:, t, :], st[:, t, :]).then_inc(aggr, 1)
                        if t:
                            normalise(t - 1)
                    normalise(T - 1)

                @block.gpsimd
                def _(pool):
                    for t in range(T):
                        pool.wait_ge(aggr, t + 1)
                        nc.gpsimd.tensor_scalar(rs[:, t:t + 1], mv[:, t, 1:2], EPS, None, ALU.add).then_inc(eps_done, 1)
                        pool.wait_ge(eps_done, t + 1)
                        nc.gpsimd.tensor_tensor(rs[:, t:t + 1], rs[:, t:t + 1], mhalf[:, 0:1],
                                                ALU.pow).then_inc(rstd, 1)

                if out is not None:
                    @block.sync
                    def _(sp):
                        for t in range(0, T, TD):
                            sp.wait_ge(normed, t + TD)
                            sp.dma_start(tiles(out)[:, t:t + TD, :], xn[:, t:t + TD, :]).then_inc(stored, 16)
                        sp.wait_ge(stored, 16 * (T // TD))


def pair_weights(nc, S, Wnb2T, bnb2, Wline2T, bline2, Wself3T, bself3, Wnb3T, bnb3, Wcomb3, bcomb3,
                 w2, bias2, w3, bias3):
    with S:
        wt = S.sb("w3_t", [P, 2, KT, D], fp32)
        wc = S.sb("w3_comb", [P, 2 * KT, D], fp32)
        bc = S.sb("b3_cols", [P, 2, KT], fp32)
        bb = S.sb("b3_all", [P, 2, KT, P], fp32)
        ps = S.pb("w3_ps", [P, 3, CW], fp32)
        landed2, landed3, spread, made = (S.sem(n) for n in ("w2_landed", "w3_landed", "b3_spread", "w3_made"))
        with nc.Block() as block:

            @block.sync
            def _(sp):
                sp.dma_start(wt[:, 0], Wnb3T.rearrange("(k p) o -> p k o", p=P)).then_inc(landed3, 16)
                sp.dma_start(wt[:, 1], Wself3T.rearrange("(k p) o -> p k o", p=P)).then_inc(landed3, 16)
                sp.dma_start(wc[:], Wcomb3.rearrange("(k p) o -> p k o", p=P)).then_inc(landed3, 16)
                sp.dma_start(bc[:, 0, :], bnb3).then_inc(landed3, 16)
                sp.dma_start(bc[:, 1, :], bself3).then_inc(landed3, 16)
                sp.dma_start(bias3[:, 0, :], every(bcomb3)).then_inc(landed3, 16)
                for src, to in ((Wnb2T, w2[:, :, 0:D]), (Wline2T, w2[:, :, D:2 * D])):
                    sp.dma_start(to, src.rearrange("(k p) o -> p k o", p=P)).then_inc(landed2, 16)
                for i, src in enumerate((bnb2, bline2)):
                    sp.dma_start(bias2[:, i, :], every(src)).then_inc(landed2, 16)
                sp.wait_ge(landed2, 64)

            @block.tensor
            def _(pe):
                pe.wait_ge(spread, 1)
                for k in range(KT):
                    for s in range(2):
                        for m in range(KT):
                            nc.tensor.matmul(ps[:, k, s * D:(s + 1) * D], wt[:, s, m, k * P:(k + 1) * P],
                                             wc[:, (1 - s) * KT + m, :], start=(m == 0), stop=(m == KT - 1),
                                             skip_group_check=True)
                for s in range(2):
                    for m in range(KT):
                        last = nc.tensor.matmul(ps[:, 2, 0:D], bb[:, s, m, :], wc[:, (1 - s) * KT + m, :],
                                                start=(s == 0 and m == 0), stop=(s == 1 and m == KT - 1))
                last.then_inc(made, 1)

            @block.vector
            def _(dve):
                dve.wait_ge(landed3, 96)
                nc.vector.tensor_copy(bb[:].rearrange("p s k n -> p (s k) n"),
                                      bc[:].rearrange("p s k -> p (s k)").unsqueeze(2).broadcast_to([P, 2 * KT, P])
                                      ).then_inc(spread, 1)
                dve.wait_ge(made, 1)
                nc.vector.tensor_copy(w3[:], ps[:, 0:KT, :])
                nc.vector.tensor_tensor(bias3[:, 1, :], ps[:, 2, 0:D], bias3[:, 0, :], ALU.add)


def program(nc, x, x2, v, xT, x2T, adjT, W1T, a1, gamma, beta, Wnb2T, bnb2, Wline2T, bline2,
            Wself3T, bself3, Wnb3T, bnb3, Wcomb3, bcomb3, dst_rows, out):
    S = Space(nc)
    with S:
        ident = S.sb("ident", [P, P], fp32)
        ones = S.sb("ones", [P, P], fp32)
        mhalf = S.sb("mhalf", [P, T], fp32)
        negI = S.sb("negI", [P, P], bf16)
        shift = S.sb("shift", [P, H], fp32)
        cur = S.sb("cur", [P, T * D], fp32)
        edge = S.sb("edge", [P, T, N], bf16)
        nodes = cur[:, :].rearrange("p (t d) -> p t d", d=D)

        constants(nc, S, ident, ones, mhalf, negI)
        load_edges(nc, S, adjT, edge)

        shifts(nc, S, x, x2, shift)
        attnT = cur[:, :].rearrange("p (g n) -> p g n", g=G)
        for g in range(G):
            with S:
                kst = S.sb("kst", [P, HG, N], fp32r)
                qst = S.sb("qst", [P, HG, N], fp32r)
                vg = S.sb("vg", [P, T, GW], fp32)
                load_stacks(nc, S, g, xT, x2T, v, kst, qst, vg)
                attention(nc, S, g, kst, qst, vg, negI, shift, edge, ones, attnT)

        with S:
            w2 = S.sb("w2", [P, KT, 2 * D], fp32)
            bias2 = S.sb("bias2", [P, 2, D], fp32)
            w3 = S.sb("w3", [P, KT, 2 * D], fp32)
            bias3 = S.sb("bias3", [P, 2, D], fp32)
            pair_weights(nc, S, Wnb2T, bnb2, Wline2T, bline2, Wself3T, bself3, Wnb3T, bnb3, Wcomb3, bcomb3,
                         w2, bias2, w3, bias3)
            with S:
                hp = S.sb("hp", [P, T, D], fp32)
                gat_layer(nc, S, x, W1T, a1, ident, mhalf, cur, dst_rows, edge, hp)
                keep = S.sb("keep", [P, T, N], bf16)
                close_layer1(nc, S, gamma, beta, ones, mhalf, hp, cur, edge, keep)
                xT_sb = hp[:].rearrange("p t d -> p (t d)").rearrange("p (k n) -> p k n", k=KT)
                mean_layer(nc, S, ident, mhalf, cur, keep, xT_sb, w2, bias2, True)
            xT_sb = S.sb("xT", [P, KT, N], fp32)
            mean_layer(nc, S, ident, mhalf, cur, edge, xT_sb, w3, bias3, False, out)


def gat_layer(nc, S, x, W1T, a1, ident, mhalf, cur, dst_rows, edge, hp):
    with S:
        wh1 = S.sb("wh1", [P, T, H, DH + 1], fp32)
        scores = S.sb("s_src_dst", [P, T, 2 * H], fp32)
        fac = S.sb("fac", [P, 2, T, H], fp32)
        efac = S.sb("efac", [P, 2, T, H], fp32)
        negb = S.sb("negb", [P, T, H], fp32)
        bigb = S.sb("bigb", [P, T, H], fp32)
        enter_layer1(nc, S, x, W1T, a1, ident, mhalf, cur, edge, wh1, dst_rows, scores)
        gat_factors(nc, S, scores, fac, efac, negb, bigb)
        gat_attention(nc, S, wh1, dst_rows, fac, efac, negb, bigb, edge, hp)


def kernel(x, adj, L0_gnn_x2, L0_gnn_v, L1_gnn_W, L1_gnn_a, L1_gnn_gamma, L1_gnn_beta, L2_gnn_W_nb, L2_gnn_b_nb,
           L2_gnn_W_line, L2_gnn_b_line, L3_gnn_W_self, L3_gnn_b_self, L3_gnn_W_nb, L3_gnn_b_nb, L3_gnn_W_comb,
           L3_gnn_b_comb):
    import numpy as np
    import concourse.bacc as bacc
    from concourse.bass_utils import run_bass_kernel_spmd

    def turned(a):
        return np.ascontiguousarray(np.asarray(a).T)

    def columns(a):
        return turned(np.asarray(a).reshape(KT, P))

    arrays = {
        "x": x, "x2": L0_gnn_x2, "v": L0_gnn_v, "xT": turned(x), "x2T": turned(L0_gnn_x2), "adjT": turned(adj),
        "W1T": turned(L1_gnn_W), "a1": L1_gnn_a, "gamma": L1_gnn_gamma, "beta": L1_gnn_beta,
        "Wnb2T": turned(L2_gnn_W_nb), "bnb2": L2_gnn_b_nb, "Wline2T": turned(L2_gnn_W_line), "bline2": L2_gnn_b_line,
        "Wself3T": turned(L3_gnn_W_self), "bself3": columns(L3_gnn_b_self), "Wnb3T": turned(L3_gnn_W_nb), "bnb3": columns(L3_gnn_b_nb),
        "Wcomb3": L3_gnn_W_comb, "bcomb3": L3_gnn_b_comb,
    }
    arrays = {f"in_{k}_dram": np.ascontiguousarray(a) for k, a in arrays.items()}
    nc = bacc.Bacc("TRN2", target_bir_lowering=False, num_devices=1)
    args = [nc.dram_tensor(k, a.shape, mybir.dt.from_np(a.dtype), kind="ExternalInput").ap() for k, a in arrays.items()]
    out = nc.dram_tensor("out_dram", (N, D), fp32, kind="ExternalOutput").ap()
    dst_rows = nc.dram_tensor("dst_rows_dram", (H, N), fp32, kind="Internal").ap()
    program(nc, *args, dst_rows, out)
    r = run_bass_kernel_spmd(nc, [arrays], core_ids=[0])
    return r.results[0]["out_dram"]
```

```python
from contextlib import ExitStack

import concourse.bass as bass
from concourse import mybir
from concourse.alu_op_type import AluOpType as ALU

fp32 = mybir.dt.float32
fp32r = mybir.dt.float32r
bf16 = mybir.dt.bfloat16
int32 = mybir.dt.int32
ACT = mybir.ActivationFunctionType
AX = mybir.AxisListType
RMAX = bass.bass_isa.ReduceOp.max

P = 128
N = 2048
D = 256
H = 8
DH = D // H
T = N // P
KT = D // P
CW = 512
NC = N // CW
HG = 4
G = H // HG
GW = HG * DH
SCALE = DH ** -0.5
NEG = -9.0e15
ALPHA = 0.2
SLOPE = 0.01
EPS = 1e-5
BIG = 1e20
TRUST = 1e-25
KEEP = 64
AR = 2
AHEAD = 2


class Chain:

    def __init__(self, eng, sem, base=0):
        self.eng, self.sem, self.n, self.base = eng, sem, 0, base

    def __call__(self, ins):
        self.n += 1
        ins.then_inc(self.sem, 1)
        self.eng.wait_ge(self.sem, self.base + self.n)


class Space:

    def __init__(self, nc):
        self.nc, self.base, self.scopes, self.n, self.sems = nc, ExitStack(), [], 0, []

    def __enter__(self):
        self.scopes.append(ExitStack())
        return self

    def __exit__(self, *a):
        self.scopes.pop().close()
        if not self.scopes:
            self.base.close()

    def sb(self, name, shape, dt):
        self.n += 1
        return self.scopes[-1].enter_context(self.nc.sbuf_tensor(f"{name}_{self.n}", shape, dt))

    def pb(self, name, shape, dt):
        self.n += 1
        return self.scopes[-1].enter_context(self.nc.psum_tensor(f"{name}_{self.n}", shape, dt))

    def sem(self, name):
        self.n += 1
        self.sems.append(self.base.enter_context(self.nc.semaphore(f"{name}_{self.n}")))
        return self.sems[-1]

    def clear_sems(self):
        sems, self.sems = self.sems, []
        with self.nc.Block() as block:

            @block.gpsimd
            def _(pool):
                for sem in sems:
                    pool.sem_clear(sem)

        self.base.close()


def every(ap):
    return ap.rearrange("(o n) -> o n", o=1).broadcast_to([P, ap.shape[0]])


def tiles(ap):
    return ap.rearrange("(t p) n -> p t n", p=P)


def constants(nc, S, ident, ones, mhalf, negI, low):
    done, made = S.sem("const_chain"), S.sem("ident_made")
    with nc.Block() as block:

        @block.gpsimd
        def _(pool):
            step = Chain(pool, done)
            step(nc.gpsimd.memset(ident[:], 0.0))
            step(nc.gpsimd.memset(ones[:], 1.0))
            step(nc.gpsimd.memset(mhalf[:], -0.5))
            step(nc.gpsimd.memset(low[:], 1.0))
            nc.gpsimd.affine_select(out=ident[:], in_=ident[:], pattern=[[-1, P]], compare_op=ALU.not_equal,
                                    fill=1.0, base=0, channel_multiplier=1).then_inc(made, 1)

        @block.vector
        def _(dve):
            dve.wait_ge(made, 1)
            nc.vector.tensor_scalar(negI[:], ident[:], NEG, None, ALU.mult)


def stack_rows(src, g, cols):
    return src[g * GW:(g + 1) * GW, cols].rearrange("(h d) n -> d h n", d=DH)


def convert(nc, edge, adj_raw, ones, jp, at):
    return nc.scalar.activation(edge[:, 2 * jp:2 * jp + 2, at], adj_raw[:, jp % AR], ACT.Relu, bias=ones[:, 0:1],
                                scale=-1.0)


def shifts(nc, S, xT, x2T, adjT, v, ident, ones, shift, kst, qst, v0, v1, adj_raw, edge):
    with S:
        xs = S.sb("xs", [P, 2, G, N], fp32)
        sq = S.sb("sq", [P, 2, N], bf16)
        member = S.sb("member", [P, G, H], bf16)
        mx = S.sb("mx", [H, 4], fp32)
        diag = S.sb("diag", [H, H], fp32)
        first = S.sb("first_raw", [P, 2, HG, CW], fp32)
        norms = S.pb("norms_ps", [P, 2, N], fp32)
        landed = [S.sem(f"xs_landed{i}") for i in range(4)]
        e_landed = [S.sem(f"first_edges_landed{i}") for i in range(AHEAD)]
        f_landed = [S.sem(f"first_landed{i}") for i in range(2)]
        chain_p, member_made, squared, normed, chain, spread, all_shift, high, v_landed = (
            S.sem(n) for n in ("member_chain", "member_made", "squared", "normed", "shift_chain", "shift_diag",
                               "shift_all", "first_high", "v_landed"))
        with nc.Block() as block:

            @block.sync
            def _(sp):
                for n in range(4):
                    src, g = (x2T, xT)[n % 2], n // 2
                    sp.dma_start(xs[:, n % 2, g, :], src[g * GW:(g + 1) * GW, :]).then_inc(landed[n], 16)
                for i, src in enumerate((x2T, xT)):
                    for r in range(P // DH):
                        sp.dma_start(first[r * DH:(r + 1) * DH, i], stack_rows(src, 0, slice(0, CW))
                                     ).then_inc(f_landed[i], 16)
                for jp in range(AHEAD):
                    sp.dma_start(adj_raw[:, jp % AR], tiles(adjT)[:, 2 * jp:2 * jp + 2, 0:CW]).then_inc(e_landed[jp], 16)
                sp.dma_start(v0, tiles(v)[:, :, 0:GW]).then_inc(v_landed, 16)
                sp.dma_start(v1[:], tiles(v)[:, :, GW:2 * GW]).then_inc(v_landed, 16)
                sp.wait_ge(v_landed, 32)

            @block.scalar
            def _(act):
                for n in range(4):
                    act.wait_ge(landed[n], 16)
                    if n >= 2:
                        act.wait_ge(normed, n - 1)
                    nc.scalar.activation(sq[:, n % 2, :], xs[:, n % 2, n // 2, :], ACT.Square).then_inc(squared, 1)
                for i, dst in enumerate((kst[:, :, 0:CW], qst[:, 0])):
                    act.wait_ge(f_landed[i], 16 * (P // DH))
                    nc.scalar.copy(dst, first[:, i]).then_inc(high, 1)
                for jp in range(AHEAD):
                    act.wait_ge(e_landed[jp], 16)
                    convert(nc, edge, adj_raw, ones, jp, slice(0, CW))

            @block.tensor
            def _(pe):
                pe.wait_ge(member_made, 1)
                for n in range(4):
                    pe.wait_ge(squared, n + 1)
                    for c in range(NC):
                        last = nc.tensor.matmul(norms[0:H, n % 2, c * CW:(c + 1) * CW], member[:, n // 2, :],
                                                sq[:, n % 2, c * CW:(c + 1) * CW],
                                                start=(n // 2 == 0), stop=(n // 2 == G - 1), skip_group_check=True)
                    last.then_inc(normed, 1)
                pe.wait_ge(spread, 1)
                nc.tensor.matmul(norms[:, 0, 0:H], ones[0:H, :], diag[:], start=True, stop=True).then_inc(all_shift, 1)

            @block.vector
            def _(dve):
                step = Chain(dve, chain)
                for i in range(2):
                    dve.wait_ge(normed, 2 + i + 1)
                    step(nc.vector.tensor_reduce(out=mx[:, i:i + 1], in_=norms[0:H, i, :], axis=AX.X, op=ALU.max))
                step(nc.vector.tensor_tensor(mx[:, 2:3], mx[:, 0:1], mx[:, 1:2], ALU.add))
                step(nc.vector.tensor_scalar(mx[:, 3:4], mx[:, 2:3], -SCALE / 2, None, ALU.mult))
                nc.vector.tensor_scalar(diag[:], ident[0:H, 0:H], mx[:, 3:4], None, ALU.mult).then_inc(spread, 1)
                dve.wait_ge(all_shift, 1)
                nc.vector.tensor_copy(shift[:], norms[:, 0, 0:H])
                dve.wait_ge(high, 1)
                for r in (1, 3):
                    dst = kst[r * DH:(r + 1) * DH, :, 0:CW]
                    nc.vector.tensor_tensor(dst, first[r * DH:(r + 1) * DH, 0], dst.bitcast(fp32), ALU.subtract)

            @block.gpsimd
            def _(pool):
                step = Chain(pool, chain_p)
                step(nc.gpsimd.memset(member[:], 1.0))
                step(nc.gpsimd.affine_select(out=member[:], in_=member[:], pattern=[[GW, G], [-DH, H]],
                                             compare_op=ALU.is_ge, fill=0.0, base=0, channel_multiplier=1))
                nc.gpsimd.affine_select(out=member[:], in_=member[:], pattern=[[-GW, G], [DH, H]],
                                        compare_op=ALU.is_gt, fill=0.0, base=DH, channel_multiplier=-1
                                        ).then_inc(member_made, 1)
                pool.wait_ge(high, 2)
                dst = qst[2 * DH:4 * DH, 0]
                nc.gpsimd.tensor_tensor(dst, first[2 * DH:4 * DH, 1], dst.bitcast(fp32), ALU.subtract)


def attention(nc, S, xT, x2T, adjT, kst, qst, v0, v1, negI, shift, adj_raw, edge, ones, low, attnT):
    PR = 8
    JP = T // 2
    U = JP * HG
    SR = 3
    KC = CW // (2 * P)
    with S:
        ex = S.sb("ex", [P, PR, 2 * CW], fp32)
        esum = S.sb("esum", [P, HG, 2 * CW], fp32)
        recip = S.sb("recip", [P, CW], fp32)
        least = S.sb("least_sum", [P, 1], fp32)
        raw = S.sb("raw", [P, HG, CW], fp32)
        scores_ps = S.pb("scores_ps", [P, SR, 2 * CW], fp32)
        mixed_ps = S.pb("mixed_ps", [P, CW], fp32)
        total_ps = S.pb("total_ps", [P, CW], fp32)
        (scores_ready, exp_ready, mixed, summed, totals, recip_ready, stored, lowest, converted, raw_landed, high,
         k_high, k_quarter, k_made, q_made) = (
            S.sem(n) for n in ("scores_ready", "exp_ready", "mixed", "summed", "totals", "recip_ready", "stored",
                               "lowest", "edges_converted", "raw_landed", "stack_high", "k_high", "k_quarter",
                               "k_made", "q_made"))
        k0_landed = S.sem("k0_landed")
        adj_landed = [S.sem(f"adj_landed{i}") for i in range(AR)]
        EXP0, MIX0, SUM0, TOT0, STO0, QM0 = 2 * SR, 2, PR, 1, 1, 1

        def columns(c):
            return slice(c * CW, (c + 1) * CW)

        def load_raw(eng, src, g, c, landed):
            for r in range(P // DH):
                eng.dma_start(raw[r * DH:(r + 1) * DH], stack_rows(src, g, columns(c))).then_inc(landed, 16)

        def wait_raw(eng, n):
            if n < NC - 1:
                eng.wait_ge(k0_landed, 16 * (P // DH) * (n + 1))
            else:
                eng.wait_ge(raw_landed, 16 * (P // DH) * (n - NC + 2))

        def slot(u):
            return u % SR

        def before(u):
            return u - SR if u >= SR else max(b for b in range(U) if slot(b) == slot(u)) - U

        SHARED = 2 * NC - 2

        def shared(g, c):
            return NC * g + c <= SHARED

        def chunk_at(it, jp):
            if not isinstance(it, int):
                return None
            if it == 0 and jp in (0, 3, 5):
                c = (0, 3, 5).index(jp) + 1
                return 0, c, c - 1
            if it == NC - 1 and jp in (3, 5, 7):
                c = (jp - 3) // 2
                return 1, c, 2 * NC - 1 + c
            return None
        with nc.Block() as block:

            @block.sync
            def _(sp):
                def load(it, last, first=False):
                    for jp in range(AHEAD, JP + AHEAD):
                        if last and jp >= JP:
                            break
                        if first and jp in (AHEAD, AHEAD + 4, AHEAD + 6):
                            c = (AHEAD, AHEAD + 4, AHEAD + 6).index(jp) + 1
                            if c > 1:
                                sp.wait_ge(k_made, c - 1)
                                sp.wait_ge(k_quarter, c - 1)
                            load_raw(sp, x2T, 0, c, k0_landed)
                        sp.wait_ge(converted, it * JP + (jp - AR + 1))
                        tt = jp % JP
                        at = (columns(it + jp // JP) if isinstance(it, int) else bass.ds(it * CW + jp // JP * CW, CW))
                        sp.dma_start(adj_raw[:, jp % AR], tiles(adjT)[:, 2 * tt:2 * tt + 2, at]
                                     ).then_inc(adj_landed[jp % AR], 16)

                load(0, False, True)
                with sp.Fori(1, NC - 1) as it:
                    load(it, False)
                load(NC - 1, True)

            @block.gpsimd
            def _(pool):
                def lower(at, dst):
                    return nc.gpsimd.tensor_tensor(dst[at], raw[at], dst[at].bitcast(fp32), ALU.subtract)

                def stack_k(g, c, n):
                    dst = kst[:, :, c * CW:(c + 1) * CW]
                    if g:
                        load_raw(pool, x2T, g, c, raw_landed)
                    if shared(g, c):
                        pool.wait_ge(k_high, NC * g + c)
                        lower(slice(3 * DH, 4 * DH), dst).then_inc(k_made, 1)
                        pool.wait_ge(k_quarter, NC * g + c)
                    else:
                        wait_raw(pool, n)
                        nc.gpsimd.tensor_copy(dst, raw[:]).then_inc(high, 1)
                        pool.wait_ge(high, NC + 1)
                        lower(slice(DH, 2 * DH), dst)
                        lower(slice(3 * DH, 4 * DH), dst).then_inc(k_made, 1)
                    pool.wait_ge(k_made, NC * g + c)

                def stack_q(it, n):
                    load_raw(pool, xT, it // NC, it % NC, raw_landed)
                    dst = qst[:, it % 2]
                    wait_raw(pool, n)
                    nc.gpsimd.tensor_copy(dst, raw[:]).then_inc(high, 1)
                    pool.wait_ge(high, it + (it > NC))
                    lower(slice(2 * DH, 4 * DH), dst).then_inc(q_made, 1)
                    pool.wait_ge(q_made, it + QM0)

                for c in range(1, NC):
                    stack_k(0, c, c - 1)
                n0 = NC - 2
                stack_q(1, n0 + 1)
                for it in range(2, NC + 1):
                    pool.wait_ge(scores_ready, U * (it - 1))
                    stack_q(it, n0 + it)
                for c in range(NC):
                    pool.wait_ge(scores_ready, U * (NC - 1) + HG * KC * (c + 1))
                    stack_k(1, c, n0 + NC + 1 + c)
                for it in range(NC + 1, 2 * NC):
                    pool.wait_ge(scores_ready, U * (it - 1))
                    stack_q(it, n0 + NC + it)

            @block.tensor
            def _(pe):
                pe.sem_inc(mixed, MIX0)
                pe.sem_inc(totals, TOT0)
                pe.sem_inc(q_made, QM0)

                def rounds(g):
                    vg = (v0, v1)[g]
                    with pe.Fori(NC * g, NC * (g + 1)) as it:

                        def score(jp, h):
                            u = jp * HG + h
                            if h == 0:
                                if g == 0:
                                    pe.wait_ge(converted, it * JP + (jp + 1))
                                made = jp // KC + NC * g
                                if made:
                                    pe.wait_ge(k_made, made)
                                    pe.wait_ge(k_quarter, min(made, SHARED))
                                if jp == 0:
                                    pe.wait_ge(q_made, it + QM0)
                            pe.wait_ge(exp_ready, it * U + (before(u) + 1 + EXP0))
                            for t in range(2):
                                jt = 2 * jp + t
                                to = scores_ps[:, slot(u), t * CW:(t + 1) * CW]
                                nc.tensor.matmul(to, kst[:, h, jt * P:(jt + 1) * P],
                                                 qst[:, bass.ds(it % 2, 1), h, :].rearrange("p o n -> p (o n)"),
                                                 start=True, stop=False)
                                last = nc.tensor.matmul(to, negI[:], edge[:, jt, bass.ds(it * CW - g * N, CW)],
                                                        start=False, stop=True)
                            last.then_inc(scores_ready, 1)

                        def mix(jp, t):
                            if t == 0:
                                pe.wait_ge(exp_ready, it * U + (jp * HG + HG + EXP0))
                            if t == 0 and jp == 0:
                                pe.wait_ge(stored, it + STO0)
                            jt = 2 * jp + t
                            for h in range(HG):
                                u = jp * HG + h
                                last = nc.tensor.matmul(mixed_ps[h * DH:(h + 1) * DH, :],
                                                        vg[:, jt, h * DH:(h + 1) * DH],
                                                        ex[:, u % PR, t * CW:(t + 1) * CW],
                                                        start=(jt == 0), stop=(jt == T - 1))
                            if t == 1:
                                last.then_inc(mixed, 1)

                        for jp in range(JP):
                            score(jp, 0)
                            score(jp, 1)
                            if jp:
                                mix(jp - 1, 0)
                            score(jp, 2)
                            score(jp, 3)
                            if jp:
                                mix(jp - 1, 1)
                        mix(JP - 1, 0)
                        mix(JP - 1, 1)
                        pe.wait_ge(summed, it * U + (U + SUM0))
                        for t in range(2):
                            for h in range(HG):
                                last = nc.tensor.matmul(total_ps[h * DH:(h + 1) * DH, :], ones[:, 0:DH],
                                                        esum[:, h, t * CW:(t + 1) * CW], start=(t == 0), stop=(t == 1))
                        last.then_inc(totals, 1)

                for g in range(G):
                    rounds(g)

            @block.scalar
            def _(act):
                act.sem_inc(exp_ready, EXP0)
                act.sem_inc(converted, AHEAD)

                def round_(it, g, last):
                    for u in range(U):
                        jp, h = u // HG, u % HG
                        ahead = g == 0 and h == 2 and not (last and jp + AHEAD >= JP)
                        if ahead:
                            n = jp // AR + 1
                            act.wait_ge(adj_landed[(jp + AHEAD) % AR], it * (16 * JP // AR) + 16 * n)
                        act.wait_ge(scores_ready, it * U + (u + 1))
                        act.wait_ge(mixed, it * JP + (u // HG - PR // HG + 1 + MIX0))
                        act.wait_ge(summed, it * U + (u - PR + 1 + SUM0))
                        nc.scalar.activation(ex[:, u % PR, :], scores_ps[:, slot(u), :], ACT.Exp,
                                             bias=shift[:, g * HG + h:g * HG + h + 1],
                                             scale=SCALE).then_inc(exp_ready, 1)
                        if ahead:
                            tt = jp + AHEAD
                            c = it + tt // JP
                            at = slice(c * CW, (c + 1) * CW) if isinstance(c, int) else bass.ds(c * CW, CW)
                            convert(nc, edge, adj_raw, ones, tt % JP, at).then_inc(converted, 1)
                        due = chunk_at(it, jp) if h == 1 else None
                        if due:
                            wait_raw(act, due[2])
                            nc.scalar.copy(kst[:, :, due[1] * CW:(due[1] + 1) * CW], raw[:]).then_inc(k_high, 1)

                round_(0, 0, False)
                with act.Fori(1, NC - 1) as it:
                    round_(it, 0, False)
                round_(NC - 1, 0, True)
                with act.Fori(NC, 2 * NC) as it:
                    round_(it, 1, False)

            @block.vector
            def _(dve):
                dve.sem_inc(summed, SUM0)
                dve.sem_inc(stored, STO0)

                def round_(it, g):
                    for u in range(U):
                        jp, h = u // HG, u % HG
                        dve.wait_ge(exp_ready, it * U + (u + 1 + EXP0))
                        if u < HG:
                            dve.wait_ge(totals, it + TOT0)
                            nc.vector.tensor_copy(esum[:, h, :], ex[:, u % PR, :]).then_inc(summed, 1)
                        else:
                            dve.wait_ge(summed, it * U + (u - HG + 1 + SUM0))
                            nc.vector.tensor_tensor(esum[:, h, :], esum[:, h, :], ex[:, u % PR, :],
                                                    ALU.add).then_inc(summed, 1)
                        due = chunk_at(it, jp) if h == 1 else None
                        if due:
                            dve.wait_ge(k_high, NC * due[0] + due[1])
                            dst = kst[DH:2 * DH, :, due[1] * CW:(due[1] + 1) * CW]
                            nc.vector.tensor_tensor(dst, raw[DH:2 * DH], dst.bitcast(fp32),
                                                    ALU.subtract).then_inc(k_quarter, 1)
                    dve.wait_ge(totals, it + (1 + TOT0))
                    dve.wait_ge(mixed, it * JP + (JP + MIX0))
                    at = slice(it % NC * CW, (it % NC + 1) * CW) if isinstance(it, int) else bass.ds(it * CW - g * N, CW)
                    nc.vector.tensor_scalar(recip[:], total_ps[:], TRUST / 2, None, ALU.max).then_inc(recip_ready, 1)
                    nc.vector.tensor_copy(attnT[:, g, at], mixed_ps[:]).then_inc(stored, 1)
                    dve.wait_ge(recip_ready, it * 2 + 1)
                    nc.vector.tensor_reduce(out=least[:], in_=recip[:], axis=AX.X, op=ALU.min).then_inc(lowest, 1)
                    dve.wait_ge(lowest, it * 2 + 1)
                    nc.vector.tensor_tensor(low, least[:], low, ALU.min).then_inc(lowest, 1)
                    nc.vector.reciprocal(recip[:], recip[:]).then_inc(recip_ready, 1)
                    dve.wait_ge(stored, it + (1 + STO0))
                    dve.wait_ge(recip_ready, it * 2 + 2)
                    nc.vector.tensor_tensor(attnT[:, g, at], attnT[:, g, at], recip[:], ALU.mult)

                round_(0, 0)
                with dve.Fori(1, NC - 1) as it:
                    round_(it, 0)
                round_(NC - 1, 0)
                with dve.Fori(NC, 2 * NC) as it:
                    round_(it, 1)


def general_attention(nc, S, layer, low, trust, ones, ident, srcs, adj, scratch, to):
    U = T * H
    LOADS = 4
    STEPS = 7 if layer == 0 else 9
    with S:
        fine = S.sb("fine", [P, 1], fp32)
        doubt = S.sb("doubt", [P, 1], int32)
        adj_raw = S.sb("gen_adj", [P, N], int32)
        mask = S.sb("gen_mask", [P, N], fp32)
        fill = S.sb("gen_fill", [P, N], fp32)
        sc = S.sb("gen_scores", [P, N], fp32)
        pT = S.sb("gen_probsT", [P, N], fp32)
        src = S.sb("gen_src", [P, N], fp32)
        dst = S.sb("gen_dst", [P, P], fp32)
        vh = S.sb("gen_v", [P, T, DH], fp32)
        col = S.sb("gen_col", [P, 4], fp32)
        res = S.sb("gen_result", [P, P], fp32)
        sc_ps = S.pb("gen_scores_ps", [P, NC, CW], fp32)
        pT_ps = S.pb("gen_probsT_ps", [P, 2, CW], fp32)
        res_ps = S.pb("gen_result_ps", [P, CW], fp32)
        names = ("ok_ready", "ok_counted", "doubt_ready", "landed", "scored", "chain", "shifted", "exp_ready",
                 "probs_ready", "turned", "kept", "summed", "result_ready", "stored", "returned")
        (ok_ready, ok_counted, doubt_ready, landed, scored, chain, shifted, exp_ready, probs_ready, turned, kept,
         summed, result_ready, stored, returned) = (S.sem("gen_" + n) for n in names)

        def in_doubt(eng):
            eng.wait_ge(doubt_ready, 1)
            return eng.value_load(doubt[0:1, 0:1], min_val=0, max_val=1) > 0

        with nc.Block() as block:

            @block.sync
            def _(sp):
                with sp.If(in_doubt(sp)):
                    sp.sem_inc(stored, 16)
                    with sp.Fori(0, U) as u:
                        tile = bass.ds(u // H * P, P)
                        rows = bass.ds(u % H * DH, DH)
                        sp.wait_ge(stored, u * 16 + 16)
                        sp.dma_start(adj_raw[:], adj[tile, :]).then_inc(landed, 16)
                        if layer == 0:
                            xT, x2T, v = srcs
                            sp.dma_start(src[0:DH, :], x2T[rows, :]).then_inc(landed, 16)
                            sp.dma_start(dst[0:DH, :], xT[rows, tile]).then_inc(landed, 16)
                            sp.dma_start(vh[:], tiles(v)[:, :, rows]).then_inc(landed, 16)
                        else:
                            score_rows, wh = srcs
                            sp.dma_start(src[:], score_rows[bass.ds(u % H, 1), :].broadcast_to([P, N])
                                         ).then_inc(landed, 16)
                            sp.dma_start(dst[:, 0:1], score_rows[bass.ds(u % H + H, 1), tile].rearrange("o n -> n o")
                                         ).then_inc(landed, 16)
                            sp.dma_start(vh[:], wh[:, :, bass.ds(u % H, 1), 0:DH].rearrange("p t o d -> p t (o d)")
                                         ).then_inc(landed, 16)
                        sp.wait_ge(result_ready, u + 1)
                        if layer == 0:
                            sp.dma_start(scratch[rows, tile], res[0:DH, :]).then_inc(stored, 16)
                        else:
                            sp.dma_start(scratch[tile, rows], res[:, 0:DH]).then_inc(stored, 16)
                    sp.wait_ge(stored, 16 * (U + 1))
                    if layer == 0:
                        sp.dma_start(to, scratch.rearrange("(g p) n -> p g n", p=P)).then_inc(returned, 16)
                    else:
                        sp.dma_start(to, tiles(scratch)).then_inc(returned, 16)
                    sp.wait_ge(returned, 16)

            @block.tensor
            def _(pe):
                pe.wait_ge(ok_ready, 1)
                nc.tensor.matmul(res_ps[:, 0:1], ones[:], fine[:], start=True, stop=True).then_inc(ok_counted, 1)
                with pe.If(in_doubt(pe)):
                    with pe.Fori(0, U) as u:
                        if layer == 0:
                            pe.wait_ge(landed, u * (16 * LOADS) + 16 * LOADS)
                            for c in range(NC):
                                last = nc.tensor.matmul(sc_ps[:, c, :], dst[0:DH, :], src[0:DH, c * CW:(c + 1) * CW],
                                                        start=True, stop=True)
                            last.then_inc(scored, 1)
                        pe.wait_ge(probs_ready, u + 1)
                        for c in range(NC):
                            if c >= 2:
                                pe.wait_ge(kept, u * NC + (c - 1))
                            for t in range(c * NC, (c + 1) * NC):
                                last = nc.tensor.transpose(pT_ps[:, c % 2, t % NC * P:(t % NC + 1) * P],
                                                           sc[:, t * P:(t + 1) * P], ident[:])
                            last.then_inc(turned, 1)
                        pe.wait_ge(kept, u * NC + NC)
                        for t in range(T):
                            probs, vals = pT[:, t * P:(t + 1) * P], vh[:, t, :]
                            if layer == 0:
                                last = nc.tensor.matmul(res_ps[0:DH, 0:P], vals, probs, start=(t == 0), stop=(t == T - 1))
                            else:
                                last = nc.tensor.matmul(res_ps[:, 0:DH], probs, vals, start=(t == 0), stop=(t == T - 1))
                        last.then_inc(summed, 1)

            @block.scalar
            def _(act):
                with act.If(in_doubt(act)):
                    with act.Fori(0, U) as u:
                        act.wait_ge(shifted, u + 1)
                        nc.scalar.activation(sc[:], sc[:], ACT.Exp, bias=col[:, 1:2]).then_inc(exp_ready, 1)
                        for c in range(NC):
                            act.wait_ge(turned, u * NC + (c + 1))
                            nc.scalar.copy(pT[:, c * CW:(c + 1) * CW], pT_ps[:, c % 2, :]).then_inc(kept, 1)

            @block.vector
            def _(dve):
                nc.vector.tensor_scalar(fine[:], low, trust, None, ALU.is_ge).then_inc(ok_ready, 1)
                dve.wait_ge(ok_counted, 1)
                nc.vector.tensor_scalar(doubt[:], res_ps[:, 0:1], float(P), None, ALU.is_lt).then_inc(doubt_ready, 1)
                with dve.If(in_doubt(dve)):
                    with dve.Fori(0, U) as u:
                        step = Chain(dve, chain, u * STEPS)
                        dve.wait_ge(landed, u * (16 * LOADS) + 16 * LOADS)
                        step(nc.vector.tensor_scalar(mask[:], adj_raw[:], 0, None, ALU.is_gt))
                        step(nc.vector.tensor_scalar(fill[:], mask[:], 0.0, NEG, ALU.is_equal, ALU.mult))
                        if layer == 0:
                            dve.wait_ge(scored, u + 1)
                            step(nc.vector.scalar_tensor_tensor(out=sc[:], in0=sc_ps[:].rearrange("p c n -> p (c n)"),
                                                                scalar=SCALE, in1=mask[:], op0=ALU.mult, op1=ALU.mult))
                        else:
                            step(nc.vector.tensor_scalar(sc[:], src[:], dst[:, 0:1], None, ALU.add))
                            step(nc.vector.scalar_tensor_tensor(out=sc[:], in0=sc[:], scalar=ALPHA, in1=sc[:],
                                                                op0=ALU.mult, op1=ALU.max))
                            step(nc.vector.tensor_tensor(sc[:], sc[:], mask[:], ALU.mult))
                        step(nc.vector.tensor_tensor(sc[:], sc[:], fill[:], ALU.add))
                        step(nc.vector.tensor_reduce(out=col[:, 0:1], in_=sc[:], axis=AX.X, op=ALU.max))
                        nc.vector.tensor_scalar(col[:, 1:2], col[:, 0:1], -1.0, None, ALU.mult).then_inc(shifted, 1)
                        dve.wait_ge(exp_ready, u + 1)
                        step(nc.vector.tensor_reduce(out=col[:, 2:3], in_=sc[:], axis=AX.X, op=ALU.add))
                        step(nc.vector.reciprocal(col[:, 3:4], col[:, 2:3]))
                        nc.vector.tensor_scalar(sc[:], sc[:], col[:, 3:4], None, ALU.mult).then_inc(probs_ready, 1)
                        dve.wait_ge(summed, u + 1)
                        if layer == 0:
                            nc.vector.tensor_copy(res[0:DH, :], res_ps[0:DH, 0:P]).then_inc(result_ready, 1)
                        else:
                            nc.vector.tensor_copy(res[:, 0:DH], res_ps[:, 0:DH]).then_inc(result_ready, 1)


def enter_layer1(nc, S, x, W1T, a1, ident, mhalf, cur, edge, wh1, score_rows, scores, pair, sources):
    attnT = cur[:, :].rearrange("p (g n) -> p g n", g=G)
    TG = 4
    GS = T // TG
    SW = 2 * H
    with S:
        xs = S.sb("x_nodes", [P, T, D], fp32)
        x1 = S.sb("x1", [P, T, D], fp32)
        xT_sb = S.sb("x1T", [P, KT, N], fp32)
        st = S.sb("bn_stats", [P, T, 6], fp32)
        mv = S.sb("mean_var", [P, T, 2], fp32)
        rs = S.sb("rstd", [P, T], fp32)
        w = S.sb("w1", [P, KT, D + SW], fp32)
        ab = S.sb("a_all", [P, 2, DH], fp32)
        wa = S.sb("wa_prod", [P, 2, KT, H, DH], fp32)
        arow = S.sb("arow", [SW, N], fp32)
        attn_ps = S.pb("attn_ps", [P, 2, 2, D], fp32)
        x1t_ps = S.pb("x1T_ps", [P, 2, KT, 2 * P], fp32)
        wh_ps = S.pb("wh_ps", [P, 2, CW], fp32)
        row_ps = S.pb("row_ps", [P, 2, CW], fp32)
        x_landed = [S.sem(f"x_landed{g}") for g in range(GS)]
        names = ("w_landed", "wa_prod_ready", "wa_ready", "attn_turned", "added", "stats", "aggr",
                 "var_eps", "rstd", "normed", "x1_turned", "x1T_kept", "projected", "scores_kept", "wh_kept", "rows",
                 "rows_kept", "rows_written", "x1_kept")
        (w_landed, wa_prod, wa_ready, attn_turned, added, stats, aggr, var_eps, rstd, normed, x1_turned,
         x1T_kept, projected, scores_kept, wh_kept, rows, rows_kept, written, x1_kept) = (S.sem(n) for n in names)
        pair_landed = S.sem("pair_weights_landed")
        with nc.Block() as block:

            @block.sync
            def _(sp):
                sp.dma_start(w[:, :, 0:D], W1T.rearrange("(k p) o -> p k o", p=P)).then_inc(w_landed, 16)
                sp.dma_start(ab[:].rearrange("p s d -> p (s d)"), every(a1)).then_inc(w_landed, 16)
                for g in range(GS):
                    at = slice(TG * g, TG * (g + 1))
                    sp.dma_start(xs[:, at, :], tiles(x)[:, at, :]).then_inc(x_landed[g], 16)
                pair_there = pair.load(sp, pair_landed, *sources)
                sp.wait_ge(attn_turned, GS)
                for g in range(GS):
                    at = slice(TG * g, TG * (g + 1))
                    sp.wait_ge(normed, TG * (g + 1))
                    sp.dma_start(cur[:, :].rearrange("p (t d) -> p t d", d=D)[:, at, :], x1[:, at, :]
                                 ).then_inc(x1_kept, 16)
                sp.wait_ge(rows_kept, NC)
                sp.dma_start(score_rows, arow[:]).then_inc(written, 16)
                sp.wait_ge(written, 16)
                sp.wait_ge(x1_kept, 16 * GS)
                sp.wait_ge(pair_landed, pair_there)

            @block.tensor
            def _(pe):
                def attention_by_nodes(g):
                    if g:
                        pe.wait_ge(added, TG * g)
                    for t in range(TG * g, TG * (g + 1)):
                        for f in range(G):
                            last = nc.tensor.transpose(attn_ps[:, t % TG // 2, t % 2, f * GW:(f + 1) * GW],
                                                       attnT[:, f, t * P:(t + 1) * P], ident[:])
                    last.then_inc(attn_turned, 1)

                def features(g):
                    pe.wait_ge(normed, TG * (g + 1))
                    for t in range(TG * g, TG * (g + 1), 2):
                        if t >= 4:
                            pe.wait_ge(x1T_kept, t // 2 - 1)
                        for k in range(KT):
                            for s in range(2):
                                last = nc.tensor.transpose(x1t_ps[:, t // 2 % 2, k, s * P:(s + 1) * P],
                                                           x1[:, t + s, k * P:(k + 1) * P], ident[:])
                        last.then_inc(x1_turned, 1)
                    if g == 0:
                        pe.wait_ge(wa_ready, 2 * KT)
                    for t in range(TG * g, TG * (g + 1)):
                        pe.wait_ge(x1T_kept, t // 2 + 1)
                        if t >= 2:
                            pe.wait_ge(wh_kept, t - 1)
                        for k in range(KT):
                            last = nc.tensor.matmul(wh_ps[:, t % 2, 0:D + SW], xT_sb[:, k, t * P:(t + 1) * P],
                                                    w[:, k, :], start=(k == 0), stop=(k == KT - 1))
                        last.then_inc(projected, 1)
                    if g >= 2:
                        pe.wait_ge(rows_kept, g - 1)
                    for k in range(KT):
                        last = nc.tensor.matmul(row_ps[0:SW, g % 2, :], w[:, k, D:D + SW],
                                                xT_sb[:, k, g * CW:(g + 1) * CW], start=(k == 0), stop=(k == KT - 1))
                    last.then_inc(rows, 1)

                attention_by_nodes(0)
                for g in range(GS):
                    if g + 1 < GS:
                        attention_by_nodes(g + 1)
                    features(g)

            @block.vector
            def _(dve):
                dve.wait_ge(w_landed, 32)
                for s in range(2):
                    for k in range(KT):
                        nc.vector.tensor_tensor(
                            wa[:, s, k], w[:, k, 0:D].rearrange("p (h d) -> p h d", d=DH),
                            ab[:, s, :].rearrange("p (o d) -> p o d", o=1).broadcast_to([P, H, DH]),
                            ALU.mult).then_inc(wa_prod, 1)
                for s in range(2):
                    for k in range(KT):
                        dve.wait_ge(wa_prod, s * KT + k + 1)
                        nc.vector.tensor_reduce(out=w[:, k, D + s * H:D + (s + 1) * H], in_=wa[:, s, k], axis=AX.X,
                                                op=ALU.add).then_inc(wa_ready, 1)
                nc.vector.memset(wh1[:, :, :, DH:DH + 1], 1.0)
                def keep_scores(g):
                    for t in range(TG * g, TG * (g + 1)):
                        dve.wait_ge(projected, t + 1)
                        nc.vector.tensor_copy(scores[:, t, :], wh_ps[:, t % 2, D:D + SW]).then_inc(scores_kept, 1)

                for g in range(GS):
                    group = range(TG * g, TG * (g + 1))
                    dve.wait_ge(x_landed[g], 16)
                    dve.wait_ge(attn_turned, g + 1)
                    for t in group:
                        nc.vector.tensor_tensor(xs[:, t, :], attn_ps[:, t % TG // 2, t % 2, :], xs[:, t, :],
                                                ALU.add).then_inc(added, 1)
                    for t in group:
                        dve.wait_ge(added, t + 1)
                        nc.vector.bn_stats(st[:, t, :], xs[:, t, :]).then_inc(stats, 1)
                    for t in group:
                        dve.wait_ge(stats, t + 1)
                        nc.vector.bn_aggr(mv[:, t, :], st[:, t, :]).then_inc(aggr, 1)
                    if g:
                        keep_scores(g - 1)
                    for t in group:
                        nc.vector.tensor_scalar(edge[:, t, :], edge[:, t, :], 0.0, None, ALU.is_equal)
                    dve.wait_ge(rstd, g + 1)
                    for t in group:
                        nc.vector.tensor_scalar(x1[:, t, :], xs[:, t, :], mv[:, t, 0:1], rs[:, t:t + 1],
                                                ALU.subtract, ALU.mult).then_inc(normed, 1)
                keep_scores(GS - 1)

            @block.gpsimd
            def _(pool):
                for g in range(GS):
                    at = slice(TG * g, TG * (g + 1))
                    pool.wait_ge(aggr, TG * (g + 1))
                    nc.gpsimd.tensor_scalar(rs[:, at], mv[:, at, 1], EPS, None, ALU.add).then_inc(var_eps, 1)
                    pool.wait_ge(var_eps, g + 1)
                    nc.gpsimd.tensor_tensor(rs[:, at], rs[:, at], mhalf[:, at], ALU.pow).then_inc(rstd, 1)

            @block.scalar
            def _(act):
                for g in range(GS):
                    for t in range(TG * g, TG * (g + 1), 2):
                        act.wait_ge(x1_turned, t // 2 + 1)
                        nc.scalar.copy(xT_sb[:, :, t * P:(t + 2) * P], x1t_ps[:, t // 2 % 2]).then_inc(x1T_kept, 1)
                    for t in range(TG * g, TG * (g + 1)):
                        act.wait_ge(scores_kept, t + 1)
                        nc.scalar.copy(wh1[:, t, :, 0:DH], wh_ps[:, t % 2, 0:D].rearrange("p (h d) -> p h d", d=DH)
                                       ).then_inc(wh_kept, 1)
                    act.wait_ge(rows, g + 1)
                    nc.scalar.copy(arow[:, g * CW:(g + 1) * CW], row_ps[0:SW, g % 2, :]).then_inc(rows_kept, 1)


def gat_factors(nc, S, scores, fac, efac, negb, bigb):
    b, a = scores[:, :, 0:H], scores[:, :, H:2 * H]
    with S:
        mx = S.sb("mx", [P, H], fp32)
        bm = S.sb("bm", [P, H], fp32)
        top = S.sb("top", [P, T, H], fp32)
        m = S.sb("m", [P, T, H], fp32)
        chain, most, ready = (S.sem(n) for n in ("fac_chain", "b_most", "fac_args"))
        ALL = bm[:].rearrange("p (o h) -> p o h", o=1).broadcast_to([P, T, H])
        with nc.Block() as block:

            @block.vector
            def _(dve):
                step = Chain(dve, chain)
                step(nc.vector.tensor_reduce(out=mx[:], in_=b.rearrange("p t h -> p h t"), axis=AX.X, op=ALU.max))
                dve.wait_ge(most, 1)
                step(nc.vector.tensor_tensor(fac[:, 0], b, ALL, ALU.subtract))
                step(nc.vector.tensor_tensor(top[:], a, ALL, ALU.add))
                step(nc.vector.tensor_scalar(m[:], top[:], ALPHA, None, ALU.mult))
                step(nc.vector.tensor_tensor(m[:], m[:], top[:], ALU.max))
                step(nc.vector.tensor_scalar(fac[:, 1], fac[:, 0], ALPHA, None, ALU.mult))
                step(nc.vector.tensor_tensor(efac[:, 0], top[:], m[:], ALU.subtract))
                step(nc.vector.tensor_scalar(top[:], top[:], ALPHA, None, ALU.mult))
                nc.vector.tensor_tensor(efac[:, 1], top[:], m[:], ALU.subtract).then_inc(ready, 1)
                nc.vector.tensor_scalar(negb[:], b, -1.0, None, ALU.mult)
                nc.vector.tensor_scalar(bigb[:], b, BIG, None, ALU.mult)
            @block.gpsimd
            def _(pool):
                pool.wait_ge(chain, 1)
                nc.gpsimd.partition_all_reduce(bm[:], mx[:], P, RMAX).then_inc(most, 1)

            @block.scalar
            def _(act):
                act.wait_ge(ready, 1)
                nc.scalar.activation(fac[:], fac[:], ACT.Exp)
                nc.scalar.activation(efac[:], efac[:], ACT.Exp)


def gat_attention(nc, S, wh1, score_rows, fac, efac, negb, bigb, edge, sums, low, hp, pair):
    W = DH + 1
    C = 3 * W
    HALF = N // 2
    BT = HALF // P
    R = 4
    UN = 2 * T
    HR = T // 2
    RS_ = 4
    with S:
        aall = S.sb("a_all", [P, 2, N], fp32)
        pos = S.sb("pos", [P, R, HALF], bf16)
        steps = S.sb("steps", [P, RS_, HALF], bf16)
        bigh = S.sb("big_b_head", [P, 2, T], fp32)
        fx = S.sb("fx", [P, 2, T, 2, 3, W], bf16)
        fm = S.sb("fm", [P, 2, T, 3, W], bf16)
        rest = S.sb("rest", [P, 2, T, W], fp32)
        ev = S.sb("ev", [P, 4, 4 * C], fp32)
        part = S.sb("part", [P, BT, 2, W], fp32)
        whole = S.sb("whole", [P, BT, W], fp32)
        minus1 = S.sb("minus1", [P, BT], fp32)
        tiny = S.sb("tiny", [P, BT], fp32)
        den = S.sb("den", [P, BT], fp32)
        acc = S.pb("gat_ps", [P, 8, CW], fp32)
        parts_of = ev[:].rearrange("p b (i k r c) -> p (b i k) r c", k=2, r=3, c=W)
        pos_ready, unit_done, half_done, rest_step, cut, evac, post = (
            S.sem(n) for n in ("pos_ready", "unit_done", "half_done", "rest_step", "cut", "evacuated", "post_step"))
        a_landed = [S.sem(f"a_landed{e}") for e in range(2)]
        step_ready, bigh_ready = S.sem("step_ready"), S.sem("big_b_head_ready")
        RS, PS = 6, 7
        DONE0, HALF0, EV0, POST0, POS0 = R, 3, 2, PS, 2 * RS_
        with nc.Block() as block:

            def loop(engine, body):
                with engine.Fori(0, H // 2 - 1) as q:
                    for e in range(2):
                        body(q * 2 + e, e, False)
                for e in range(2):
                    body(H - 2 + e, e, e == 1)

            def one(h):
                return slice(h, h + 1) if isinstance(h, int) else bass.ds(h, 1)

            @block.sync
            def _(sp):
                def load(h, e):
                    sp.dma_start(aall[:, e, :], score_rows[one(h + H), :].broadcast_to([P, N])).then_inc(a_landed[e], 16)

                def body(h, e, last):
                    if not last:
                        sp.wait_ge(pos_ready, h * UN + POS0)
                        sp.wait_ge(step_ready, h * (2 * HR) + 1)
                        load(h + 1, 1 - e)

                load(0, 0)
                loop(sp, body)

            @block.vector
            def _(dve):
                dve.sem_inc(pos_ready, POS0)

                def big_head(h, e):
                    nc.vector.tensor_scalar(bigh[:, e, :], bigb[:, :, one(h)].rearrange("p t o -> p (t o)"), 1.0,
                                            None, ALU.mult).then_inc(bigh_ready, 1)

                pair.spread_bias()
                big_head(0, 0)
                pair.keep(dve, acc[:, 4:7])

                def body(h, e, last):
                    dve.wait_ge(a_landed[e], h * 8 + (16 - 8 * e))
                    for half in range(2):
                        if half and not last:
                            big_head(h + 1, 1 - e)
                        for jt in range(T):
                            u = half * T + jt
                            dve.wait_ge(unit_done, h * UN + (u - R + 1 + DONE0))
                            at = slice(half * HALF, (half + 1) * HALF)
                            if jt % 2:
                                n = half * HR + jt // 2
                                dve.wait_ge(step_ready, h * (2 * HR) + (n + 1))
                                nc.vector.tensor_tensor(pos[:, u % R, :], steps[:, n % RS_, :], edge[:, jt, at],
                                                        ALU.min).then_inc(pos_ready, 1)
                                continue
                            nc.vector.scalar_tensor_tensor(
                                out=pos[:, u % R, :], in0=aall[:, e, at],
                                scalar=negb[:, jt, one(h)], in1=edge[:, jt, at],
                                op0=ALU.is_gt, op1=ALU.mult).then_inc(pos_ready, 1)

                loop(dve, body)
                dve.wait_ge(post, 2 * H * PS + POST0)
                nc.vector.tensor_reduce(out=low, in_=sums[:].rearrange("p t h -> p (t h)"), axis=AX.X, op=ALU.min)

            @block.tensor
            def _(pe):
                pe.sem_inc(unit_done, DONE0)
                pe.sem_inc(half_done, HALF0)
                pair.products(pe, acc[:, 4:7])
                pe.wait_ge(pair.kept, 1)

                def body(h, e, last):
                    pe.wait_ge(cut, h * 3 + 3)
                    for half in range(2):
                        pe.wait_ge(evac, h * 2 + (half - 2 + 1 + EV0))
                        for jt in range(T):
                            u = half * T + jt
                            pe.wait_ge(pos_ready, h * UN + (u + 1 + POS0))
                            for i in range(BT):
                                col = (i % 2) * 2 * C
                                done = nc.tensor.matmul(acc[:, half * 4 + i // 2, col:col + 2 * C],
                                                        pos[:, u % R, i * P:(i + 1) * P],
                                                        fx[:, e, jt].rearrange("p k r c -> p (k r c)"),
                                                        start=(jt == 0 and i % 2 == 0), stop=False,
                                                        skip_group_check=True)
                            done.then_inc(unit_done, 1)
                            for i in range(BT):
                                col = (i % 2) * 2 * C + C
                                at = half * HALF + i * P
                                done = nc.tensor.matmul(acc[:, half * 4 + i // 2, col:col + C],
                                                        edge[:, jt, at:at + P],
                                                        fm[:, e, jt].rearrange("p r c -> p (r c)"),
                                                        start=False, stop=(jt == T - 1), skip_group_check=True)
                        done.then_inc(half_done, 1)

                loop(pe, body)

            @block.scalar
            def _(act):
                act.sem_inc(evac, EV0)

                def cut_parts(h, e):
                    act.wait_ge(half_done, h * 2 + (-2 + HALF0))
                    for r in range(3):
                        act.wait_ge(rest_step, h * RS + (2 * r + 2))
                        nc.scalar.copy(fm[:, e, :, r, :], rest[:, 1])
                        nc.scalar.mul(fx[:, e, :, 1, r, :], rest[:, 1], -1.0)
                        nc.scalar.copy(fx[:, e, :, 0, r, :], rest[:, 0]).then_inc(cut, 1)

                def evacuate(h, half):
                    act.wait_ge(half_done, h * 2 + (half + 1 + HALF0))
                    act.wait_ge(post, (h * 2 + half) * PS + (2 - PS + POST0))
                    nc.scalar.copy(ev[:], acc[:, half * 4:half * 4 + 4, 0:4 * C]).then_inc(evac, 1)

                def compare(h, e, half, first, count):
                    for n in range(half * HR + first, half * HR + first + count):
                        if n % (2 * HR) == 0:
                            act.wait_ge(a_landed[e], h * 8 + (16 - 8 * e))
                            act.wait_ge(bigh_ready, h + 1)
                        before = n - RS_
                        unit = before // HR * T + 2 * (before % HR) + 1
                        act.wait_ge(pos_ready, h * UN + (unit + 1 + POS0))
                        nc.scalar.activation(steps[:, n % RS_, :], aall[:, e, half * HALF:(half + 1) * HALF], ACT.Relu,
                                             bias=bigh[:, e, 2 * (n % HR) + 1:2 * (n % HR) + 2],
                                             scale=BIG).then_inc(step_ready, 1)

                def body(h, e, last):
                    compare(h, e, 0, RS_, HR - RS_)
                    compare(h, e, 1, 0, RS_)
                    if not last:
                        cut_parts(h + 1, 1 - e)
                    evacuate(h, 0)
                    compare(h, e, 1, RS_, HR - RS_)
                    if not last:
                        compare(h + 1, 1 - e, 0, 0, RS_)
                    evacuate(h, 1)

                cut_parts(0, 0)
                compare(0, 0, 0, 0, RS_)
                loop(act, body)

            @block.gpsimd
            def _(pool):
                pool.sem_inc(post, POST0)
                nc.gpsimd.memset(minus1[:], -1.0)
                nc.gpsimd.memset(tiny[:], TRUST * 1e-10)

                def leave(h, e):
                    for k in range(2):
                        if not isinstance(h, int) or h > 0:
                            pool.wait_ge(cut, h * 3)
                        nc.gpsimd.tensor_tensor(rest[:, k], wh1[:, :, one(h), :].rearrange("p t o c -> p t (o c)"),
                                                fac[:, k, :, one(h)].broadcast_to([P, T, W]),
                                                ALU.mult).then_inc(rest_step, 1)
                    for r in range(2):
                        pool.wait_ge(cut, h * 3 + (r + 1))
                        for k in range(2):
                            piece = fx[:, e, :, 0, r, :] if k == 0 else fm[:, e, :, r, :]
                            nc.gpsimd.tensor_tensor(rest[:, k], rest[:, k], piece, ALU.subtract).then_inc(rest_step, 1)

                def finish(h, half):
                    pool.wait_ge(evac, h * 2 + (half + 1 + EV0))
                    step = Chain(pool, post, (h * 2 + half) * PS + POST0)
                    step(nc.gpsimd.tensor_tensor(part[:].rearrange("p i k c -> p (i k) c"), parts_of[:, :, 0, :],
                                                 parts_of[:, :, 1, :], ALU.add))
                    step(nc.gpsimd.tensor_tensor(part[:].rearrange("p i k c -> p (i k) c"), parts_of[:, :, 2, :],
                                                 part[:].rearrange("p i k c -> p (i k) c"), ALU.add))
                    tt = slice(half * BT, (half + 1) * BT)
                    for k in range(2):
                        ins = nc.gpsimd.tensor_tensor(part[:, :, k, :], part[:, :, k, :],
                                                      efac[:, k, tt, one(h)].broadcast_to([P, BT, W]), ALU.mult)
                        if k:
                            step(ins)
                    step(nc.gpsimd.tensor_tensor(whole[:], part[:, :, 0, :], part[:, :, 1, :], ALU.add))
                    step(nc.gpsimd.tensor_tensor(den[:], whole[:, :, DH], tiny[:], ALU.add))
                    nc.gpsimd.tensor_tensor(whole[:, :, DH], den[:], minus1[:], ALU.pow)
                    step(nc.gpsimd.tensor_copy(sums[:, tt, one(h)], den[:].rearrange("p (t o) -> p t o", o=1)))
                    to = hp[:, tt, h * DH:(h + 1) * DH] if isinstance(h, int) else hp[:, tt, bass.ds(h * DH, DH)]
                    step(nc.gpsimd.tensor_tensor(to, whole[:, :, 0:DH],
                                                 whole[:, :, DH:DH + 1].broadcast_to([P, BT, DH]), ALU.mult))

                def body(h, e, last):
                    if not last:
                        leave(h + 1, 1 - e)
                    finish(h, 0)
                    finish(h, 1)

                leave(0, 0)
                loop(pool, body)


def close_layer1(nc, S, gamma, beta, ident, ones, mhalf, hp, cur, edge, deg):
    x1 = cur[:, :].rearrange("p (t d) -> p t d", d=D)
    KR = 4
    NU = NC * T
    FIRST = 4 * NC
    PT = (NU - FIRST) // T
    with S:
        beta_all = S.sb("beta_all", [P, D], fp32)
        gcol = S.sb("gamma_col", [P, KT], fp32)
        vcol = S.sb("var_col", [P, KT], fp32)
        diag = S.sb("var_diag", [P, KT, P], fp32)
        mean = S.sb("node_mean", [P, D], fp32)
        sq = S.sb("node_sq", [P, 4, D], fp32)
        var = S.sb("node_var", [P, D], fp32)
        st = S.sb("bn_stats", [P, T, 6], fp32)
        mv = S.sb("mean_var", [P, T, 2], fp32)
        rs = S.sb("rstd", [P, T], fp32)
        tri = S.sb("tri", [P, P], bf16)
        above = S.sb("above", [P, P], bf16)
        degrow = S.sb("degree_row", [1, N], fp32)
        upto = S.sb("upto", [P, KR, CW], bf16)
        limit = S.sb("limit", [P, 1], fp32)
        degrees = S.sem("degrees")
        sums = S.pb("sums_ps", [P, 2, CW], fp32)
        deg_ps = S.pb("degrees_ps", [P, T], fp32)
        cum_ps = S.pb("cum_ps", [P, NC, CW], fp32)
        names = ("gb_landed", "consts", "const_chain", "bn_sums", "bn_mean", "bn_centred", "bn_squared", "bn_spread",
                 "bn_var", "bn_chain", "bn_root", "bn_factor", "bn_scale", "bn_scale_kept",
                 "bn_scaled", "bn_shifted", "y1_ready", "ln_stats", "ln_aggr",
                 "ln_eps", "ln_rstd", "passed", "row_kept", "cumulated", "upto_ready", "kept")
        (landed, consts, cc, summed, meant, centred, squared, spread, varied, pc, rooted, factored, scale_ready,
         var_kept, scaled, shifted, y_ready,
         stats, aggr, eps_done, rstd, passed, row_kept, cum, upto_ready, kept) = (S.sem(n) for n in names)
        with nc.Block() as block:

            @block.sync
            def _(sp):
                sp.dma_start(gcol[:], gamma).then_inc(landed, 16)
                sp.dma_start(beta_all[:], every(beta)).then_inc(landed, 16)

            @block.tensor
            def _(pe):
                for t in range(T):
                    last = nc.tensor.matmul(sums[:, 0, 0:D], ones[:], hp[:, t, :], start=(t == 0), stop=(t == T - 1))
                last.then_inc(summed, 1)
                def up_to_source(t, c):
                    nc.tensor.matmul(cum_ps[:, c, :], tri[:], edge[:, t, c * CW:(c + 1) * CW], start=(t == 0),
                                     stop=False, skip_group_check=True).then_inc(cum, 1)

                def cumulate(t):
                    for c in range(NC):
                        pe.wait_ge(upto_ready, t * NC + c + 1)
                        nc.tensor.matmul(cum_ps[:, c, :], above[:], edge[:, t, c * CW:(c + 1) * CW], start=False,
                                         stop=(t == T - 1), skip_group_check=True).then_inc(passed, 1)
                        if t + 1 < T:
                            up_to_source(t + 1, c)

                pe.wait_ge(consts, 1)
                for c in range(NC):
                    up_to_source(0, c)
                for b in range(4):
                    cumulate(b)
                    for t in range(4 * b, 4 * b + 4):
                        pe.wait_ge(squared, t + 1)
                        for k in range(KT):
                            last = nc.tensor.matmul(sums[:, 1, k:k + 1], sq[:, t % 4, k * P:(k + 1) * P], ones[:, 0:1],
                                                    start=(t == 0 and k == 0), stop=(t == T - 1), skip_group_check=True)
                        last.then_inc(spread, 1)
                cumulate(4)
                pe.wait_ge(rooted, KT)
                nc.tensor.matmul(sums[:, 0, 0:D], ones[:], diag[:].rearrange("p k n -> p (k n)"),
                                 start=True, stop=True).then_inc(scale_ready, 1)
                for t in range(5, T):
                    cumulate(t)
                pe.wait_ge(row_kept, NC)
                for t in range(T):
                    last = nc.tensor.matmul(deg_ps[:, t:t + 1], degrow[:, t * P:(t + 1) * P], ones[0:1, 0:1],
                                            start=(t == 0), stop=(t == T - 1), skip_group_check=True)
                last.then_inc(degrees, 1)

            @block.scalar
            def _(act):
                def square(t):
                    act.wait_ge(centred, t + 1)
                    if t >= 4:
                        act.wait_ge(spread, t - 3)
                    nc.scalar.activation(sq[:, t % 4, :], hp[:, t, :], ACT.Square).then_inc(squared, 1)

                def compare(t):
                    for n in range(t * NC, (t + 1) * NC):
                        act.wait_ge(cum, n + 1)
                        if n >= KR:
                            act.wait_ge(kept, n - KR + 1)
                        nc.scalar.activation(upto[:, n % KR, :], cum_ps[:, n % NC, :], ACT.Sign, bias=limit[:],
                                             scale=-2.0).then_inc(upto_ready, 1)

                act.wait_ge(summed, 1)
                nc.scalar.mul(mean[:], sums[:, 0, 0:D], 1.0 / N).then_inc(meant, 1)
                act.wait_ge(consts, 1)
                for b in range(4):
                    for t in range(4 * b, 4 * b + 4):
                        square(t)
                    compare(b)
                for t in range(4, T):
                    compare(t)
                for c in range(NC):
                    act.wait_ge(passed, (T - 1) * NC + c + 1)
                    nc.scalar.copy(degrow[:, c * CW:(c + 1) * CW], cum_ps[0:1, c, :]).then_inc(row_kept, 1)

            @block.vector
            def _(dve):
                def keep_units(first, count):
                    for n in range(first, first + count):
                        t, at = n // NC, slice(n % NC * CW, (n % NC + 1) * CW)
                        dve.wait_ge(passed, n + 1)
                        nc.vector.tensor_tensor(edge[:, t, at], upto[:, n % KR, :], edge[:, t, at],
                                                ALU.mult).then_inc(kept, 1)

                dve.wait_ge(meant, 1)
                for t in range(T):
                    nc.vector.tensor_tensor(hp[:, t, :], hp[:, t, :], mean[:], ALU.subtract).then_inc(centred, 1)
                keep_units(0, FIRST)
                dve.wait_ge(spread, T)
                nc.vector.tensor_scalar(vcol[:], sums[:, 1, 0:KT], 1.0 / N, EPS, ALU.mult,
                                        ALU.add).then_inc(varied, 1)
                dve.wait_ge(factored, 1)
                for k in range(KT):
                    nc.vector.tensor_scalar(diag[:, k, :], ident[:], vcol[:, k:k + 1], None,
                                            ALU.mult).then_inc(rooted, 1)
                dve.wait_ge(scale_ready, 1)
                nc.vector.tensor_copy(var[:], sums[:, 0, 0:D]).then_inc(var_kept, 1)
                dve.wait_ge(var_kept, 1)
                dve.wait_ge(squared, T)
                for t in range(T + 1):
                    if t < T:
                        nc.vector.tensor_tensor(hp[:, t, :], hp[:, t, :], var[:], ALU.mult).then_inc(scaled, 1)
                        keep_units(FIRST + PT * t, PT)
                    if t:
                        dve.wait_ge(shifted, t)
                        nc.vector.scalar_tensor_tensor(out=hp[:, t - 1, :], in0=hp[:, t - 1, :], scalar=0.0,
                                                       in1=x1[:, t - 1, :], op0=ALU.max,
                                                       op1=ALU.add).then_inc(y_ready, 1)
                        dve.wait_ge(y_ready, t)
                        nc.vector.bn_stats(st[:, t - 1, :], hp[:, t - 1, :]).then_inc(stats, 1)
                for t in range(T):
                    dve.wait_ge(stats, t + 1)
                    nc.vector.bn_aggr(mv[:, t, :], st[:, t, :]).then_inc(aggr, 1)
                dve.wait_ge(degrees, 1)
                nc.vector.tensor_copy(deg[:], deg_ps[:])
                dve.wait_ge(rstd, 1)
                for t in range(T):
                    nc.vector.tensor_scalar(x1[:, t, :], hp[:, t, :], mv[:, t, 0:1], rs[:, t:t + 1],
                                            ALU.subtract, ALU.mult)

            @block.gpsimd
            def _(pool):
                step = Chain(pool, cc)
                nc.gpsimd.memset(limit[:], 2.0 * KEEP + 1)
                nc.gpsimd.memset(tri[:], 1.0)
                step(nc.gpsimd.memset(above[:], 1.0))
                nc.gpsimd.affine_select(out=tri[:], in_=tri[:], pattern=[[1, P]], compare_op=ALU.is_ge,
                                        fill=0.0, base=0, channel_multiplier=-1)
                nc.gpsimd.affine_select(out=above[:], in_=above[:], pattern=[[-1, P]], compare_op=ALU.is_gt,
                                        fill=0.0, base=0, channel_multiplier=1).then_inc(consts, 1)
                pool.wait_ge(varied, 1)
                pool.wait_ge(landed, 32)
                step = Chain(pool, pc)
                step(nc.gpsimd.tensor_tensor(vcol[:], vcol[:], mhalf[:, 0:KT], ALU.pow))
                nc.gpsimd.tensor_tensor(vcol[:], vcol[:], gcol[:], ALU.mult).then_inc(factored, 1)
                for t in range(T):
                    pool.wait_ge(scaled, t + 1)
                    nc.gpsimd.tensor_tensor(hp[:, t, :], hp[:, t, :], beta_all[:], ALU.add).then_inc(shifted, 1)
                pool.wait_ge(aggr, T)
                nc.gpsimd.tensor_scalar(rs[:], mv[:, :, 1], EPS, None, ALU.add).then_inc(eps_done, 1)
                pool.wait_ge(eps_done, 1)
                nc.gpsimd.tensor_tensor(rs[:], rs[:], mhalf[:], ALU.pow).then_inc(rstd, 1)


def mean_layer(nc, S, ident, mhalf, cur, edge, deg, xT_sb, w, bias, leaky, out=None):
    xn = cur[:, :].rearrange("p (t d) -> p t d", d=D)
    OT = 2 if leaky else T
    MR = 2
    with S:
        yb = S.sb("y_halves", [P, T, 2, D], fp32r)
        own = S.sb("own", [P, OT, D], fp32)
        mask = S.sb("mask", [P, MR, T, P], fp32r)

        def make_mask(t):
            return nc.scalar.activation(mask[:, t % MR], edge[:, :, t * P:(t + 1) * P],
                                        ACT.Relu if leaky else ACT.Square)

        with S:
            turned = S.pb("turned", [P, 2, CW], fp32)
            ps = S.pb("proj_ps", [P, 4, CW], fp32)
            turned_ready, xT_kept, projected, high, low, biased, owned, joined = (
                S.sem(n) for n in ("turned_ready", "xT_kept", "projected", "y_high", "y_low", "biased", "owned",
                                   "joined"))
            with nc.Block() as block:

                @block.tensor
                def _(pe):
                    for t in range(T + 1):
                        if t < T:
                            if t >= 2:
                                pe.wait_ge(xT_kept, t - 1)
                            for k in range(KT):
                                last = nc.tensor.transpose(turned[:, t % 2, k * P:(k + 1) * P],
                                                           xn[:, t, k * P:(k + 1) * P], ident[:])
                            last.then_inc(turned_ready, 1)
                        if t:
                            s = t - 1
                            pe.wait_ge(xT_kept, s + 1)
                            if s >= 4:
                                pe.wait_ge(low, s - 3)
                                pe.wait_ge(biased, s - 3)
                            for k in range(KT):
                                last = nc.tensor.matmul(ps[:, s % 4, :], xT_sb[:, k, s * P:(s + 1) * P], w[:, k, :],
                                                        start=(k == 0), stop=(k == KT - 1))
                            last.then_inc(projected, 1)

                @block.scalar
                def _(act):
                    for t in range(T + 1):
                        if t < T:
                            act.wait_ge(turned_ready, t + 1)
                            nc.scalar.copy(xT_sb[:, :, t * P:(t + 1) * P],
                                           turned[:, t % 2, 0:D].rearrange("p (k n) -> p k n", k=KT)).then_inc(xT_kept, 1)
                        if t:
                            s = t - 1
                            act.wait_ge(projected, s + 1)
                            nc.scalar.copy(yb[:, s, 0, :], ps[:, s % 4, 0:D]).then_inc(high, 1)
                    for t in range(MR):
                        make_mask(t)

                @block.vector
                def _(dve):
                    for t in range(T):
                        dve.wait_ge(high, t + 1)
                        nc.vector.tensor_tensor(yb[:, t, 1, :], ps[:, t % 4, 0:D], yb[:, t, 0, :].bitcast(fp32),
                                                ALU.subtract).then_inc(low, 1)
                        if leaky and t >= 2:
                            dve.wait_ge(joined, t - 1)
                        nc.vector.tensor_tensor(own[:, t % OT, :], ps[:, t % 4, D:2 * D], bias[:, 1, :],
                                                ALU.add).then_inc(biased, 1)
                        if leaky:
                            dve.wait_ge(biased, t + 1)
                            nc.vector.scalar_tensor_tensor(out=own[:, t % 2, :], in0=own[:, t % 2, :], scalar=SLOPE,
                                                           in1=own[:, t % 2, :], op0=ALU.mult,
                                                           op1=ALU.max).then_inc(owned, 1)

                if leaky:
                    @block.gpsimd
                    def _(pool):
                        for t in range(T):
                            pool.wait_ge(owned, t + 1)
                            nc.gpsimd.tensor_tensor(xn[:, t, :], own[:, t % 2, :], xn[:, t, :],
                                                    ALU.add).then_inc(joined, 1)
        with S:
            ps = S.pb("nb_ps", [P, 2, CW], fp32)
            tmp = S.sb("nb_tmp", [P, 2, D], fp32)
            cnt = S.sb("cnt", [P, 3, T], fp32)
            st = S.sb("bn_stats", [P, T, 6], fp32)
            mv = S.sb("mean_var", [P, T, 2], fp32)
            rs = S.sb("rstd", [P, T], fp32)
            y = xT_sb[:].rearrange("p k (t d) -> p (k t) d", d=D)
            masked, added, chain, y_ready, stats, aggr, eps_done, rstd, normed, stored = (
                S.sem(n) for n in ("masked", "nb_added", "nb_chain", "y_ready", "ln_stats", "ln_aggr", "ln_eps",
                                   "ln_rstd", "normed", "out_stored"))
            FREE0 = 2
            TD = 4
            with nc.Block() as block:

                @block.tensor
                def _(pe):
                    with pe.Fori(0, T // MR) as q:
                        for e in range(MR):
                            pe.wait_ge(masked, q * MR + (e + 1))
                            pe.wait_ge(y_ready, q * MR + (e - 2 + 1 + FREE0))
                            for jt in range(T):
                                for half in range(2):
                                    last = nc.tensor.matmul(ps[:, e, 0:D], mask[:, e, jt, :], yb[:, jt, half, :],
                                                            start=(jt == 0 and half == 0),
                                                            stop=(jt == T - 1 and half == 1))
                            last.then_inc(added, 1)

                @block.scalar
                def _(act):
                    act.sem_inc(masked, MR)
                    for t in range(MR, T):
                        act.wait_ge(added, t - MR + 1)
                        make_mask(t).then_inc(masked, 1)

                @block.vector
                def _(dve):
                    dve.sem_inc(y_ready, FREE0)
                    step = Chain(dve, chain)
                    if leaky:
                        step(nc.vector.tensor_scalar(cnt[:, 0], deg[:], float(KEEP), None, ALU.min))
                        nc.vector.tensor_scalar(cnt[:, 2], cnt[:, 0], 1.0, None, ALU.min)
                        step(nc.vector.tensor_scalar(cnt[:, 1], cnt[:, 0], 1.0, None, ALU.max))
                    else:
                        step(nc.vector.tensor_scalar(cnt[:, 1], deg[:], 1.0, None, ALU.max))
                    step(nc.vector.reciprocal(cnt[:, 1], cnt[:, 1]))

                    def normalise(t):
                        dve.wait_ge(rstd, t + 1)
                        nc.vector.tensor_scalar(xn[:, t, :], y[:, t, :], mv[:, t, 0:1], rs[:, t:t + 1],
                                                ALU.subtract, ALU.mult).then_inc(normed, 1)

                    for t in range(T):
                        e = t % 2
                        dve.wait_ge(added, t + 1)
                        over, some = cnt[:, 1, t:t + 1], cnt[:, 2, t:t + 1]
                        if leaky:
                            step(nc.vector.scalar_tensor_tensor(out=tmp[:, e, :], in0=ps[:, e, 0:D], scalar=over,
                                                                in1=bias[:, 0, :], op0=ALU.mult, op1=ALU.add))
                            step(nc.vector.scalar_tensor_tensor(out=tmp[:, e, :], in0=tmp[:, e, :], scalar=SLOPE,
                                                                in1=tmp[:, e, :], op0=ALU.mult, op1=ALU.max))
                            nc.vector.scalar_tensor_tensor(out=y[:, t, :], in0=tmp[:, e, :], scalar=some,
                                                           in1=xn[:, t, :], op0=ALU.mult,
                                                           op1=ALU.add).then_inc(y_ready, 1)
                        else:
                            step(nc.vector.scalar_tensor_tensor(out=tmp[:, e, :], in0=ps[:, e, 0:D], scalar=over,
                                                                in1=own[:, t, :], op0=ALU.mult, op1=ALU.add))
                            nc.vector.scalar_tensor_tensor(out=y[:, t, :], in0=tmp[:, e, :], scalar=0.0,
                                                           in1=xn[:, t, :], op0=ALU.max,
                                                           op1=ALU.add).then_inc(y_ready, 1)
                        dve.wait_ge(y_ready, t + 1 + FREE0)
                        nc.vector.bn_stats(st[:, t, :], y[:, t, :]).then_inc(stats, 1)
                        dve.wait_ge(stats, t + 1)
                        nc.vector.bn_aggr(mv[:, t, :], st[:, t, :]).then_inc(aggr, 1)
                        if t:
                            normalise(t - 1)
                    normalise(T - 1)

                @block.gpsimd
                def _(pool):
                    for t in range(T):
                        pool.wait_ge(aggr, t + 1)
                        nc.gpsimd.tensor_scalar(rs[:, t:t + 1], mv[:, t, 1:2], EPS, None, ALU.add).then_inc(eps_done, 1)
                        pool.wait_ge(eps_done, t + 1)
                        nc.gpsimd.tensor_tensor(rs[:, t:t + 1], rs[:, t:t + 1], mhalf[:, 0:1],
                                                ALU.pow).then_inc(rstd, 1)

                if out is not None:
                    @block.sync
                    def _(sp):
                        for t in range(0, T, TD):
                            sp.wait_ge(normed, t + TD)
                            sp.dma_start(tiles(out)[:, t:t + TD, :], xn[:, t:t + TD, :]).then_inc(stored, 16)
                        sp.wait_ge(stored, 16 * (T // TD))


class PairWeights:

    def __init__(self, nc, S, w2, bias2, w3, bias3):
        self.nc, self.w2, self.bias2, self.w3, self.bias3 = nc, w2, bias2, w3, bias3
        self.wt = S.sb("w3_t", [P, 2, KT, D], fp32)
        self.wc = S.sb("w3_comb", [P, 2 * KT, D], fp32)
        self.bc = S.sb("b3_cols", [P, 2, KT], fp32)
        self.bb = S.sb("b3_all", [P, 2, KT, P], fp32)
        self.spread, self.made, self.kept = (S.sem(n) for n in ("b3_spread", "w3_made", "w3_kept"))

    def load(self, sp, landed, Wnb2T, bnb2, Wline2T, bline2, Wself3T, bself3, Wnb3T, bnb3, Wcomb3, bcomb3):
        sp.dma_start(self.wt[:, 0], Wnb3T.rearrange("(k p) o -> p k o", p=P)).then_inc(landed, 16)
        sp.dma_start(self.wt[:, 1], Wself3T.rearrange("(k p) o -> p k o", p=P)).then_inc(landed, 16)
        sp.dma_start(self.wc[:], Wcomb3.rearrange("(k p) o -> p k o", p=P)).then_inc(landed, 16)
        sp.dma_start(self.bc[:, 0, :], bnb3).then_inc(landed, 16)
        sp.dma_start(self.bc[:, 1, :], bself3).then_inc(landed, 16)
        sp.dma_start(self.bias3[:, 0, :], every(bcomb3)).then_inc(landed, 16)
        for src, to in ((Wnb2T, self.w2[:, :, 0:D]), (Wline2T, self.w2[:, :, D:2 * D])):
            sp.dma_start(to, src.rearrange("(k p) o -> p k o", p=P)).then_inc(landed, 16)
        for i, src in enumerate((bnb2, bline2)):
            sp.dma_start(self.bias2[:, i, :], every(src)).then_inc(landed, 16)
        return 16 * 10

    def spread_bias(self):
        self.nc.vector.tensor_copy(self.bb[:].rearrange("p s k n -> p (s k) n"),
                                   self.bc[:].rearrange("p s k -> p (s k)").unsqueeze(2).broadcast_to([P, 2 * KT, P])
                                   ).then_inc(self.spread, 1)

    def products(self, pe, ps):
        nc = self.nc
        for k in range(KT):
            for s in range(2):
                for m in range(KT):
                    nc.tensor.matmul(ps[:, k, s * D:(s + 1) * D], self.wt[:, s, m, k * P:(k + 1) * P],
                                     self.wc[:, (1 - s) * KT + m, :], start=(m == 0), stop=(m == KT - 1),
                                     skip_group_check=True)
        pe.wait_ge(self.spread, 1)
        for s in range(2):
            for m in range(KT):
                last = nc.tensor.matmul(ps[:, 2, 0:D], self.bb[:, s, m, :], self.wc[:, (1 - s) * KT + m, :],
                                        start=(s == 0 and m == 0), stop=(s == 1 and m == KT - 1))
        last.then_inc(self.made, 1)

    def keep(self, dve, ps):
        dve.wait_ge(self.made, 1)
        self.nc.vector.tensor_copy(self.w3[:], ps[:, 0:KT, :])
        self.nc.vector.tensor_tensor(self.bias3[:, 1, :], ps[:, 2, 0:D], self.bias3[:, 0, :],
                                     ALU.add).then_inc(self.kept, 1)


def program(nc, x, v, xT, x2T, adj, adjT, W1T, a1, gamma, beta, Wnb2T, bnb2, Wline2T, bline2,
            Wself3T, bself3, Wnb3T, bnb3, Wcomb3, bcomb3, score_rows, scratch0, scratch1, out):
    S = Space(nc)
    with S:
        ident = S.sb("ident", [P, P], fp32)
        ones = S.sb("ones", [P, P], fp32)
        mhalf = S.sb("mhalf", [P, T], fp32)
        negI = S.sb("negI", [P, P], bf16)
        shift = S.sb("shift", [P, H], fp32)
        cur = S.sb("cur", [P, T * D], fp32)
        edge = S.sb("edge", [P, T, N], bf16)
        deg = S.sb("degrees", [P, T], fp32)
        low = S.sb("lowest_sums", [P, 2], fp32)

        constants(nc, S, ident, ones, mhalf, negI, low)

        attnT = cur[:, :].rearrange("p (g n) -> p g n", g=G)
        with S:
            kst = S.sb("kst", [P, HG, N], fp32r)
            qst = S.sb("qst", [P, 2, HG, CW], fp32r)
            v0 = attnT[:, 1, :].rearrange("p (t d) -> p t d", d=GW)
            v1 = S.sb("v1", [P, T, GW], fp32)
            adj_raw = S.sb("adj_raw", [P, AR, 2, CW], int32)
            shifts(nc, S, xT, x2T, adjT, v, ident, ones, shift, kst, qst, v0, v1, adj_raw, edge)
            attention(nc, S, xT, x2T, adjT, kst, qst, v0, v1, negI, shift, adj_raw, edge, ones, low[:, 0:1], attnT)
        general_attention(nc, S, 0, low[:, 0:1], TRUST, ones, ident, (xT, x2T, v), adj, scratch0, attnT)

        S.clear_sems()

        with S:
            w2 = S.sb("w2", [P, KT, 2 * D], fp32)
            bias2 = S.sb("bias2", [P, 2, D], fp32)
            w3 = S.sb("w3", [P, KT, 2 * D], fp32)
            bias3 = S.sb("bias3", [P, 2, D], fp32)
            sources = (Wnb2T, bnb2, Wline2T, bline2, Wself3T, bself3, Wnb3T, bnb3, Wcomb3, bcomb3)
            with S:
                hp = S.sb("hp", [P, T, D], fp32)
                gat_layer(nc, S, x, W1T, a1, adj, ones, ident, mhalf, low, cur, score_rows, scratch1, edge, hp,
                          (w2, bias2, w3, bias3), sources)
                close_layer1(nc, S, gamma, beta, ident, ones, mhalf, hp, cur, edge, deg)
                xT_sb = hp[:].rearrange("p t d -> p (t d)").rearrange("p (k n) -> p k n", k=KT)
                mean_layer(nc, S, ident, mhalf, cur, edge, deg, xT_sb, w2, bias2, True)
            xT_sb = S.sb("xT", [P, KT, N], fp32)
            mean_layer(nc, S, ident, mhalf, cur, edge, deg, xT_sb, w3, bias3, False, out)


def gat_layer(nc, S, x, W1T, a1, adj, ones, ident, mhalf, low, cur, score_rows, scratch1, edge, hp,
              weights, sources):
    with S:
        wh1 = S.sb("wh1", [P, T, H, DH + 1], fp32)
        scores = S.sb("s_src_dst", [P, T, 2 * H], fp32)
        fac = S.sb("fac", [P, 2, T, H], fp32)
        efac = S.sb("efac", [P, 2, T, H], fp32)
        negb = S.sb("negb", [P, T, H], fp32)
        bigb = S.sb("bigb", [P, T, H], fp32)
        pair = PairWeights(nc, S, *weights)
        enter_layer1(nc, S, x, W1T, a1, ident, mhalf, cur, edge, wh1, score_rows, scores, pair, sources)
        gat_factors(nc, S, scores, fac, efac, negb, bigb)
        sums = S.sb("gat_sums", [P, T, H], fp32)
        gat_attention(nc, S, wh1, score_rows, fac, efac, negb, bigb, edge, sums, low[:, 1:2], hp, pair)
        general_attention(nc, S, 1, low[:, 1:2], TRUST, ones, ident, (score_rows, wh1), adj, scratch1, hp[:])


def kernel(x, adj, L0_gnn_x2, L0_gnn_v, L1_gnn_W, L1_gnn_a, L1_gnn_gamma, L1_gnn_beta, L2_gnn_W_nb, L2_gnn_b_nb,
           L2_gnn_W_line, L2_gnn_b_line, L3_gnn_W_self, L3_gnn_b_self, L3_gnn_W_nb, L3_gnn_b_nb, L3_gnn_W_comb,
           L3_gnn_b_comb):
    import numpy as np
    import concourse.bacc as bacc
    from concourse.bass_utils import run_bass_kernel_spmd

    def turned(a):
        return np.ascontiguousarray(np.asarray(a).T)

    def columns(a):
        return turned(np.asarray(a).reshape(KT, P))

    arrays = {
        "x": x, "v": L0_gnn_v, "xT": turned(x), "x2T": turned(L0_gnn_x2), "adj": adj, "adjT": turned(adj),
        "W1T": turned(L1_gnn_W), "a1": L1_gnn_a, "gamma": columns(L1_gnn_gamma), "beta": L1_gnn_beta,
        "Wnb2T": turned(L2_gnn_W_nb), "bnb2": L2_gnn_b_nb, "Wline2T": turned(L2_gnn_W_line), "bline2": L2_gnn_b_line,
        "Wself3T": turned(L3_gnn_W_self), "bself3": columns(L3_gnn_b_self),
        "Wnb3T": turned(L3_gnn_W_nb), "bnb3": columns(L3_gnn_b_nb),
        "Wcomb3": L3_gnn_W_comb, "bcomb3": L3_gnn_b_comb,
    }
    arrays = {f"in_{k}_dram": np.ascontiguousarray(a) for k, a in arrays.items()}
    nc = bacc.Bacc("TRN2", target_bir_lowering=False, num_devices=1)
    args = [nc.dram_tensor(k, a.shape, mybir.dt.from_np(a.dtype), kind="ExternalInput").ap() for k, a in arrays.items()]
    out = nc.dram_tensor("out_dram", (N, D), fp32, kind="ExternalOutput").ap()
    score_rows = nc.dram_tensor("score_rows_dram", (2 * H, N), fp32, kind="Internal").ap()
    scratch0 = nc.dram_tensor("general0_dram", (D, N), fp32, kind="Internal").ap()
    scratch1 = nc.dram_tensor("general1_dram", (N, D), fp32, kind="Internal").ap()
    program(nc, *args, score_rows, scratch0, scratch1, out)
    r = run_bass_kernel_spmd(nc, [arrays], core_ids=[0])
    return r.results[0]["out_dram"]
```
